# Optimizing a Trainium2 kernel written in Bass

```python
import numpy as np
import jax
import jax.numpy as jnp

def _softmax(x, axis=-1):
    return jax.nn.softmax(x, axis=axis)

def _gelu(x):
    return jax.nn.gelu(x, approximate=True)

def _silu(x):
    return jax.nn.silu(x)

def _sigmoid(x):
    return jax.nn.sigmoid(x)

def _layernorm(x, axis=-1, eps=1e-05):
    m = jnp.mean(x, axis=axis, keepdims=True)
    v = jnp.var(x, axis=axis, keepdims=True)
    return (x - m) / jnp.sqrt(v + eps)

def _scatter_add(tgt, idx, src, axis=0):
    return tgt.at[idx].add(src)

def _segment_sum(src, seg, n):
    return jax.ops.segment_sum(src, seg, n)
kernel_name = 'mk_perceiver_d2_seqx_r8_6b68b2'

def setup_inputs(seed: int=0):
    np.random.seed(seed)
    _w = jnp.asarray

    def _rec_inputs():
        import jax
        import jax.numpy as jnp
        _rk = jax.random.key(seed)
        x = -0.000125 + 0.9999 * jax.random.normal(jax.random.fold_in(_rk, 1), (32, 64, 128), jnp.float32)
        _lenS = 64 - jax.random.randint(jax.random.fold_in(_rk, 7), (32,), 0, max(1, 64 // 4) + 1, jnp.int32)
        _lenS2 = 128 - jax.random.randint(jax.random.fold_in(_rk, 8), (32,), 0, max(1, 128 // 4) + 1, jnp.int32)
        _ctx_768P = jax.random.normal(jax.random.fold_in(_rk, 11), (32, 16, 96), jnp.float32)
        _ctx_768c = jax.random.dirichlet(jax.random.fold_in(_rk, 511), 0.3 * jnp.ones((16,), jnp.float32), (32, 128))
        _ctx_768t = jnp.einsum('bsk,bkd->bsd', _ctx_768c, _ctx_768P)
        _ctx_768t = _ctx_768t * jax.lax.rsqrt(jnp.mean(jnp.square(_ctx_768t)) + 1e-12) * 0.953939
        ctx_768 = 0.00272024 + 0.999456 * (_ctx_768t + 0.3 * jax.random.normal(jax.random.fold_in(_rk, 611), (32, 128, 96), jnp.float32))
        _validS = jnp.arange(64)[None, :] < _lenS[:, None]
        _validS2 = jnp.arange(128)[None, :] < _lenS2[:, None]
        _causal = jnp.tril(jnp.ones((64, 64), dtype=bool))
        mask_BxS2_bf1 = jnp.ones((32, 128), dtype=bool)
        return (x, ctx_768, mask_BxS2_bf1)
    x, ctx_768, mask_BxS2_bf1 = _rec_inputs()

    def _L0_xattn_setup():
        import jax, jax.numpy as jnp
        import numpy as np
        HEADS = 16
        DIM_HEAD = 64
        SCALE = DIM_HEAD ** (-0.5)
        QUERY_DIM = 128
        CONTEXT_DIM = 96
        INNER_DIM = HEADS * DIM_HEAD
        key = jax.random.key(seed)
        ks = jax.random.split(key, 7)
        B, Nq, Nk = (8, 512, 77)
        x = jax.random.normal(ks[0], (B, Nq, QUERY_DIM), dtype=jnp.float32)
        context = jax.random.normal(ks[1], (B, Nk, CONTEXT_DIM), dtype=jnp.float32)
        Wq = jax.random.normal(ks[2], (QUERY_DIM, INNER_DIM), dtype=jnp.float32) * QUERY_DIM ** (-0.5)
        Wk = jax.random.normal(ks[3], (CONTEXT_DIM, INNER_DIM), dtype=jnp.float32) * CONTEXT_DIM ** (-0.5)
        Wv = jax.random.normal(ks[4], (CONTEXT_DIM, INNER_DIM), dtype=jnp.float32) * CONTEXT_DIM ** (-0.5)
        Wo = jax.random.normal(ks[5], (INNER_DIM, QUERY_DIM), dtype=jnp.float32) * INNER_DIM ** (-0.5)
        bo = jnp.zeros((QUERY_DIM,), dtype=jnp.float32)
        return {'x': x, 'context': context, 'Wq': Wq, 'Wk': Wk, 'Wv': Wv, 'Wo': Wo, 'bo': bo}
    _L0_xattn_all = _L0_xattn_setup()
    _L0_xattn_in = {k: v for k, v in _L0_xattn_all.items() if k in ('Wq', 'Wk', 'Wv', 'Wo', 'bo')}
    del _L0_xattn_all

    def _L0_attn_setup():
        import jax, jax.numpy as jnp
        import numpy as np
        D_MODEL = 128
        D_STATE = 16
        key = jax.random.key(seed)
        ks = jax.random.split(key, 8)
        d, n = (D_MODEL, D_STATE)
        x = jax.random.normal(ks[0], (4, 256, d), dtype=jnp.float32)
        A_log = jax.random.normal(ks[1], (d, n), dtype=jnp.float32)
        Dp = jax.random.normal(ks[2], (d,), dtype=jnp.float32)
        s1 = 1.0 / np.sqrt(d)
        W_xproj = jax.random.uniform(ks[3], (d, d + 2 * n), jnp.float32, -s1, s1)
        b_xproj = jax.random.uniform(ks[4], (d + 2 * n,), jnp.float32, -s1, s1)
        W_out = jax.random.uniform(ks[5], (d, d), jnp.float32, -s1, s1)
        b_out = jax.random.uniform(ks[6], (d,), jnp.float32, -s1, s1)
        return {'x': x, 'A_log': A_log, 'Dp': Dp, 'W_xproj': W_xproj, 'b_xproj': b_xproj, 'W_out': W_out, 'b_out': b_out}
    _L0_attn_all = _L0_attn_setup()
    _L0_attn_in = {k: v for k, v in _L0_attn_all.items() if k in ('A_log', 'Dp', 'W_xproj', 'b_xproj', 'W_out', 'b_out')}
    del _L0_attn_all

    def _L0_ffn_setup():
        import jax, jax.numpy as jnp
        import numpy as np
        B, L, H = (8, 256, 128)
        E, K, R = (8, 2, 64)

        def _gates(cls_tok, Wr):
            logits = cls_tok @ Wr.T
            top_vals, top_idx = jax.lax.top_k(logits, K)
            neg_inf = jnp.full_like(logits, -jnp.inf)
            rows = jnp.arange(logits.shape[0])[:, None]
            masked = neg_inf.at[rows, top_idx].set(top_vals)
            return jax.nn.softmax(masked, axis=-1)
        key = jax.random.key(seed)
        k1, k2, k3, k4 = jax.random.split(key, 4)
        x = jax.random.normal(k1, (B, L, H), dtype=jnp.float32)
        Wr = jax.random.normal(k2, (E, H), dtype=jnp.float32) * (1.0 / np.sqrt(H))
        A = jax.random.normal(k3, (E, R, H), dtype=jnp.float32) * (1.0 / np.sqrt(H))
        Bw = jax.random.normal(k4, (E, H, R), dtype=jnp.float32) * (1.0 / np.sqrt(R))
        return {'x': x, 'Wr': Wr, 'A': A, 'Bw': Bw}
    _L0_ffn_all = _L0_ffn_setup()
    _L0_ffn_in = {k: v for k, v in _L0_ffn_all.items() if k in ('Wr', 'A', 'Bw')}
    del _L0_ffn_all

    def _L1_xattn_setup():
        import jax, jax.numpy as jnp
        import numpy as np
        DIM = 128
        CTX_DIM = 96
        HEADS = 16
        key = jax.random.key(seed)
        ks = jax.random.split(key, 7)
        B, N, M = (4, 512, 32)
        x = jax.random.normal(ks[0], (B, N, DIM), dtype=jnp.float32)
        context = jax.random.normal(ks[1], (B, M, CTX_DIM), dtype=jnp.float32)
        context_mask = jnp.ones((B, M), dtype=bool)
        s_d = 1.0 / np.sqrt(DIM)
        s_c = 1.0 / np.sqrt(CTX_DIM)
        Wq = jax.random.normal(ks[2], (DIM, DIM), dtype=jnp.float32) * s_d
        Wk = jax.random.normal(ks[3], (CTX_DIM, DIM), dtype=jnp.float32) * s_c
        Wv = jax.random.normal(ks[4], (CTX_DIM, DIM), dtype=jnp.float32) * s_c
        Wo = jax.random.normal(ks[5], (DIM, DIM), dtype=jnp.float32) * s_d
        return {'x': x, 'context': context, 'context_mask': context_mask, 'Wq': Wq, 'Wk': Wk, 'Wv': Wv, 'Wo': Wo}
    _L1_xattn_all = _L1_xattn_setup()
    _L1_xattn_in = {k: v for k, v in _L1_xattn_all.items() if k in ('Wq', 'Wk', 'Wv', 'Wo')}
    del _L1_xattn_all

    def _L1_attn_setup():
        import jax, jax.numpy as jnp
        import numpy as np
        B, S, D_MODEL, D_K = (4, 256, 128, 1)
        D_QKV = D_MODEL * D_K
        MASK_NEG = -9000000000000000.0

        def _scaled_dot_product_attention(q, k, v):
            d_k = k.shape[-1]
            scores = jnp.einsum('bqd,bkd->bqk', q, k) / jnp.sqrt(jnp.float32(d_k))
            scores = jnp.triu(scores, k=0)
            scores = jnp.where(scores == 0, MASK_NEG, scores)
            attn = jax.nn.softmax(scores, axis=-1)
            return jnp.einsum('bqk,bkd->bqd', attn, v)
        key = jax.random.key(seed)
        kx, kw = jax.random.split(key)
        x = jax.random.normal(kx, (B, S, D_MODEL), dtype=jnp.float32)
        W = jax.random.normal(kw, (D_MODEL, 3 * D_QKV), dtype=jnp.float32) * (1.0 / np.sqrt(D_MODEL))
        return {'x': x, 'W': W}
    _L1_attn_all = _L1_attn_setup()
    _L1_attn_in = {k: v for k, v in _L1_attn_all.items() if k in ('W',)}
    del _L1_attn_all

    def _L1_ffn_setup():
        import jax, jax.numpy as jnp
        import numpy as np
        LATENT = 128
        LEAF_W = 64
        DEPTH = 4
        N_LEAVES = 2 ** DEPTH
        N_NODES = 2 ** DEPTH - 1
        B, S = (4, 256)

        def _fff_params(key, prefix):
            ks = jax.random.split(key, 4)
            d, h, l, n = (LATENT, LEAF_W, N_LEAVES, N_NODES)
            s_in = 1.0 / np.sqrt(d).astype(np.float32)
            s_h = 1.0 / np.sqrt(h).astype(np.float32)
            return {f'{prefix}_node_w': jax.random.normal(ks[0], (n, d), jnp.float32) * s_in, f'{prefix}_node_b': jax.random.normal(ks[1], (n,), jnp.float32) * s_in, f'{prefix}_w1': jax.random.normal(ks[2], (l, d, h), jnp.float32) * s_in, f'{prefix}_b1': jnp.zeros((l, h), jnp.float32), f'{prefix}_w2': jax.random.normal(ks[3], (l, h, d), jnp.float32) * s_h, f'{prefix}_b2': jnp.zeros((l, d), jnp.float32)}

        def _fff(x, node_w, node_b, w1, b1, w2, b2):
            Bx, Sx, D = x.shape
            xf = x.reshape(-1, D)
            N = xf.shape[0]
            cur = jnp.zeros((N,), jnp.int32)
            for _ in range(DEPTH):
                pw = node_w[cur]
                score = jnp.einsum('nd,nd->n', xf, pw) + node_b[cur]
                cur = 2 * cur + 1 + (score >= 0).astype(jnp.int32)
            leaf = cur - N_NODES
            sel = jax.nn.one_hot(leaf, N_LEAVES, dtype=xf.dtype)
            hidden_all = jax.nn.relu(jnp.einsum('nd,ldh->lnh', xf, w1) + b1[:, None, :])
            hidden = hidden_all * sel.T[:, :, None]
            out = jnp.einsum('lnh,lho->no', hidden, w2) + sel @ b2
            return out.reshape(Bx, Sx, D)
        key = jax.random.key(seed)
        kx, kq, kk, kv = jax.random.split(key, 4)
        inp = {'x': jax.random.normal(kx, (B, S, LATENT), jnp.float32)}
        inp.update(_fff_params(kq, 'q'))
        inp.update(_fff_params(kk, 'k'))
        inp.update(_fff_params(kv, 'v'))
        return inp
    _L1_ffn_all = _L1_ffn_setup()
    _L1_ffn_in = {k: v for k, v in _L1_ffn_all.items() if k in ('q_node_w', 'q_node_b', 'q_w1', 'q_b1', 'q_w2', 'q_b2', 'k_node_w', 'k_node_b', 'k_w1', 'k_b1', 'k_w2', 'k_b2', 'v_node_w', 'v_node_b', 'v_w1', 'v_b1', 'v_w2', 'v_b2')}
    del _L1_ffn_all
    return {'x': x, 'ctx_768': ctx_768, 'mask_BxS2_bf1': mask_BxS2_bf1, 'L0_xattn_Wq': _L0_xattn_in['Wq'], 'L0_xattn_Wk': _L0_xattn_in['Wk'], 'L0_xattn_Wv': _L0_xattn_in['Wv'], 'L0_xattn_Wo': _L0_xattn_in['Wo'], 'L0_xattn_bo': _L0_xattn_in['bo'], 'L0_attn_A_log': _L0_attn_in['A_log'], 'L0_attn_Dp': _L0_attn_in['Dp'], 'L0_attn_W_xproj': _L0_attn_in['W_xproj'], 'L0_attn_b_xproj': _L0_attn_in['b_xproj'], 'L0_attn_W_out': _L0_attn_in['W_out'], 'L0_attn_b_out': _L0_attn_in['b_out'], 'L0_ffn_Wr': _L0_ffn_in['Wr'], 'L0_ffn_A': _L0_ffn_in['A'], 'L0_ffn_Bw': _L0_ffn_in['Bw'], 'L1_xattn_Wq': _L1_xattn_in['Wq'], 'L1_xattn_Wk': _L1_xattn_in['Wk'], 'L1_xattn_Wv': _L1_xattn_in['Wv'], 'L1_xattn_Wo': _L1_xattn_in['Wo'], 'L1_attn_W': _L1_attn_in['W'], 'L1_ffn_q_node_w': _L1_ffn_in['q_node_w'], 'L1_ffn_q_node_b': _L1_ffn_in['q_node_b'], 'L1_ffn_q_w1': _L1_ffn_in['q_w1'], 'L1_ffn_q_b1': _L1_ffn_in['q_b1'], 'L1_ffn_q_w2': _L1_ffn_in['q_w2'], 'L1_ffn_q_b2': _L1_ffn_in['q_b2'], 'L1_ffn_k_node_w': _L1_ffn_in['k_node_w'], 'L1_ffn_k_node_b': _L1_ffn_in['k_node_b'], 'L1_ffn_k_w1': _L1_ffn_in['k_w1'], 'L1_ffn_k_b1': _L1_ffn_in['k_b1'], 'L1_ffn_k_w2': _L1_ffn_in['k_w2'], 'L1_ffn_k_b2': _L1_ffn_in['k_b2'], 'L1_ffn_v_node_w': _L1_ffn_in['v_node_w'], 'L1_ffn_v_node_b': _L1_ffn_in['v_node_b'], 'L1_ffn_v_w1': _L1_ffn_in['v_w1'], 'L1_ffn_v_b1': _L1_ffn_in['v_b1'], 'L1_ffn_v_w2': _L1_ffn_in['v_w2'], 'L1_ffn_v_b2': _L1_ffn_in['v_b2']}

def reference(x, ctx_768, mask_BxS2_bf1, L0_xattn_Wq, L0_xattn_Wk, L0_xattn_Wv, L0_xattn_Wo, L0_xattn_bo, L0_attn_A_log, L0_attn_Dp, L0_attn_W_xproj, L0_attn_b_xproj, L0_attn_W_out, L0_attn_b_out, L0_ffn_Wr, L0_ffn_A, L0_ffn_Bw, L1_xattn_Wq, L1_xattn_Wk, L1_xattn_Wv, L1_xattn_Wo, L1_attn_W, L1_ffn_q_node_w, L1_ffn_q_node_b, L1_ffn_q_w1, L1_ffn_q_b1, L1_ffn_q_w2, L1_ffn_q_b2, L1_ffn_k_node_w, L1_ffn_k_node_b, L1_ffn_k_w1, L1_ffn_k_b1, L1_ffn_k_w2, L1_ffn_k_b2, L1_ffn_v_node_w, L1_ffn_v_node_b, L1_ffn_v_w1, L1_ffn_v_b1, L1_ffn_v_w2, L1_ffn_v_b2):
    import jax
    import jax.numpy as jnp

    def _L0_xattn_ref(x, context, Wq, Wk, Wv, Wo, bo):
        import jax, jax.numpy as jnp
        import numpy as np
        HEADS = 16
        DIM_HEAD = 64
        SCALE = DIM_HEAD ** (-0.5)
        QUERY_DIM = 128
        CONTEXT_DIM = 96
        INNER_DIM = HEADS * DIM_HEAD
        B, Nq, _ = x.shape
        Nk = context.shape[1]
        q = x @ Wq
        k = context @ Wk
        v = context @ Wv
        q = q.reshape(B, Nq, HEADS, DIM_HEAD).transpose(0, 2, 1, 3)
        k = k.reshape(B, Nk, HEADS, DIM_HEAD).transpose(0, 2, 1, 3)
        v = v.reshape(B, Nk, HEADS, DIM_HEAD).transpose(0, 2, 1, 3)
        sim = jnp.einsum('bhid,bhjd->bhij', q, k) * SCALE
        attn = jax.nn.softmax(sim, axis=-1)
        out = jnp.einsum('bhij,bhjd->bhid', attn, v)
        out = out.transpose(0, 2, 1, 3).reshape(B, Nq, INNER_DIM)
        return out @ Wo + bo

    def _L0_attn_ref(x, A_log, Dp, W_xproj, b_xproj, W_out, b_out):
        import jax, jax.numpy as jnp
        import numpy as np
        D_MODEL = 128
        D_STATE = 16
        Bsz, L, d = x.shape
        n = A_log.shape[1]
        proj = x @ W_xproj + b_xproj
        delta = jax.nn.softplus(proj[..., :d])
        Bm = proj[..., d:d + n]
        Cm = proj[..., d + n:]
        A = -jnp.exp(A_log)
        A_bar = jnp.exp(delta[..., None] * A)
        Bx = delta[..., None] * Bm[:, :, None, :] * x[..., None]

        def step(h, inp):
            ab, bx, c = inp
            h = ab * h + bx
            y = jnp.sum(h * c[:, None, :], axis=-1)
            return (h, y)
        h0 = jnp.zeros((Bsz, d, n), dtype=x.dtype)
        _, ys = jax.lax.scan(step, h0, (jnp.swapaxes(A_bar, 0, 1), jnp.swapaxes(Bx, 0, 1), jnp.swapaxes(Cm, 0, 1)))
        y = jnp.swapaxes(ys, 0, 1) + Dp * x
        return y @ W_out + b_out

    def _L0_ffn_ref(x, Wr, A, Bw):
        import jax, jax.numpy as jnp
        import numpy as np
        B, L, H = (8, 256, 128)
        E, K, R = (8, 2, 64)

        def _gates(cls_tok, Wr):
            logits = cls_tok @ Wr.T
            top_vals, top_idx = jax.lax.top_k(logits, K)
            neg_inf = jnp.full_like(logits, -jnp.inf)
            rows = jnp.arange(logits.shape[0])[:, None]
            masked = neg_inf.at[rows, top_idx].set(top_vals)
            return jax.nn.softmax(masked, axis=-1)
        gates = _gates(x[:, 0, :], Wr)
        mid = jnp.einsum('blh,erh->belr', x, A)
        expert_out = jnp.einsum('belr,ehr->belh', mid, Bw)
        weighted = jnp.einsum('be,belh->blh', gates, expert_out)
        return x + weighted

    def _L1_xattn_ref(x, context, context_mask, Wq, Wk, Wv, Wo):
        import jax, jax.numpy as jnp
        import numpy as np
        DIM = 128
        CTX_DIM = 96
        HEADS = 16
        B, N, _ = x.shape
        M = context.shape[1]
        hd = DIM // HEADS
        scale = hd ** (-0.5)
        q = (x @ Wq).reshape(B, N, HEADS, hd).transpose(0, 2, 1, 3)
        k = (context @ Wk).reshape(B, M, HEADS, hd).transpose(0, 2, 1, 3)
        v = (context @ Wv).reshape(B, M, HEADS, hd).transpose(0, 2, 1, 3)
        scores = jnp.einsum('bhid,bhjd->bhij', q, k) * scale
        max_neg = -jnp.finfo(scores.dtype).max
        scores = jnp.where(context_mask[:, None, None, :], scores, max_neg)
        attn = jax.nn.softmax(scores, axis=-1)
        out = jnp.einsum('bhij,bhjd->bhid', attn, v)
        out = out.transpose(0, 2, 1, 3).reshape(B, N, DIM)
        return out @ Wo

    def _L1_attn_ref(x, W):
        import jax, jax.numpy as jnp
        import numpy as np
        B, S, D_MODEL, D_K = (4, 256, 128, 1)
        D_QKV = D_MODEL * D_K
        MASK_NEG = -9000000000000000.0

        def _scaled_dot_product_attention(q, k, v):
            d_k = k.shape[-1]
            scores = jnp.einsum('bqd,bkd->bqk', q, k) / jnp.sqrt(jnp.float32(d_k))
            scores = jnp.triu(scores, k=0)
            scores = jnp.where(scores == 0, MASK_NEG, scores)
            attn = jax.nn.softmax(scores, axis=-1)
            return jnp.einsum('bqk,bkd->bqd', attn, v)
        qkv = jnp.einsum('bsd,df->bsf', x, W)
        q, k, v = jnp.split(qkv, 3, axis=-1)
        return _scaled_dot_product_attention(q, k, v)

    def _L1_ffn_ref(x, q_node_w, q_node_b, q_w1, q_b1, q_w2, q_b2, k_node_w, k_node_b, k_w1, k_b1, k_w2, k_b2, v_node_w, v_node_b, v_w1, v_b1, v_w2, v_b2):
        import jax, jax.numpy as jnp
        import numpy as np
        LATENT = 128
        LEAF_W = 64
        DEPTH = 4
        N_LEAVES = 2 ** DEPTH
        N_NODES = 2 ** DEPTH - 1
        B, S = (4, 256)

        def _fff_params(key, prefix):
            ks = jax.random.split(key, 4)
            d, h, l, n = (LATENT, LEAF_W, N_LEAVES, N_NODES)
            s_in = 1.0 / np.sqrt(d).astype(np.float32)
            s_h = 1.0 / np.sqrt(h).astype(np.float32)
            return {f'{prefix}_node_w': jax.random.normal(ks[0], (n, d), jnp.float32) * s_in, f'{prefix}_node_b': jax.random.normal(ks[1], (n,), jnp.float32) * s_in, f'{prefix}_w1': jax.random.normal(ks[2], (l, d, h), jnp.float32) * s_in, f'{prefix}_b1': jnp.zeros((l, h), jnp.float32), f'{prefix}_w2': jax.random.normal(ks[3], (l, h, d), jnp.float32) * s_h, f'{prefix}_b2': jnp.zeros((l, d), jnp.float32)}

        def _fff(x, node_w, node_b, w1, b1, w2, b2):
            Bx, Sx, D = x.shape
            xf = x.reshape(-1, D)
            N = xf.shape[0]
            cur = jnp.zeros((N,), jnp.int32)
            for _ in range(DEPTH):
                pw = node_w[cur]
                score = jnp.einsum('nd,nd->n', xf, pw) + node_b[cur]
                cur = 2 * cur + 1 + (score >= 0).astype(jnp.int32)
            leaf = cur - N_NODES
            sel = jax.nn.one_hot(leaf, N_LEAVES, dtype=xf.dtype)
            hidden_all = jax.nn.relu(jnp.einsum('nd,ldh->lnh', xf, w1) + b1[:, None, :])
            hidden = hidden_all * sel.T[:, :, None]
            out = jnp.einsum('lnh,lho->no', hidden, w2) + sel @ b2
            return out.reshape(Bx, Sx, D)
        q = _fff(x, q_node_w, q_node_b, q_w1, q_b1, q_w2, q_b2)
        k = _fff(x, k_node_w, k_node_b, k_w1, k_b1, k_w2, k_b2)
        v = _fff(x, v_node_w, v_node_b, v_w1, v_b1, v_w2, v_b2)
        scale = 1.0 / np.sqrt(LATENT).astype(np.float32)
        attn = jax.nn.softmax(jnp.einsum('bqd,bkd->bqk', q, k) * scale, axis=-1)
        return jnp.einsum('bqk,bkd->bqd', attn, v)
    x = x + _L0_xattn_ref(_layernorm(x, axis=-1), ctx_768, L0_xattn_Wq, L0_xattn_Wk, L0_xattn_Wv, L0_xattn_Wo, L0_xattn_bo)
    x = x + _L0_attn_ref(_layernorm(x, axis=-1), L0_attn_A_log, L0_attn_Dp, L0_attn_W_xproj, L0_attn_b_xproj, L0_attn_W_out, L0_attn_b_out)
    x = x + _L0_ffn_ref(_layernorm(x, axis=-1), L0_ffn_Wr, L0_ffn_A, L0_ffn_Bw)
    x = x + _L1_xattn_ref(_layernorm(x, axis=-1), ctx_768, mask_BxS2_bf1, L1_xattn_Wq, L1_xattn_Wk, L1_xattn_Wv, L1_xattn_Wo)
    x = x + _L1_attn_ref(_layernorm(x, axis=-1), L1_attn_W)
    x = x + _L1_ffn_ref(_layernorm(x, axis=-1), L1_ffn_q_node_w, L1_ffn_q_node_b, L1_ffn_q_w1, L1_ffn_q_b1, L1_ffn_q_w2, L1_ffn_q_b2, L1_ffn_k_node_w, L1_ffn_k_node_b, L1_ffn_k_w1, L1_ffn_k_b1, L1_ffn_k_w2, L1_ffn_k_b2, L1_ffn_v_node_w, L1_ffn_v_node_b, L1_ffn_v_w1, L1_ffn_v_b1, L1_ffn_v_w2, L1_ffn_v_b2)
    return x

_drawn_inputs = setup_inputs


def setup_inputs(seed=0):
    import zlib

    import numpy as np

    out = dict(_drawn_inputs(seed))
    spreads = {'L0_xattn_bo': (0.0, 0.1),
     'L1_ffn_q_b1': (0.0, 0.8),
     'L1_ffn_q_b2': (0.0, 0.8),
     'L1_ffn_k_b1': (0.0, 0.8),
     'L1_ffn_k_b2': (0.0, 0.8),
     'L1_ffn_v_b1': (0.0, 0.8),
     'L1_ffn_v_b2': (0.0, 0.635)}
    factors = {'L1_ffn_q_node_w': 3.404,
     'L1_ffn_q_node_b': 8.0,
     'L1_ffn_q_w1': 4.09,
     'L1_ffn_q_w2': 3.372,
     'L1_ffn_k_node_w': 3.381,
     'L1_ffn_k_node_b': 8.0,
     'L1_ffn_k_w1': 3.942,
     'L1_ffn_k_w2': 3.38,
     'L1_ffn_v_node_b': 3.3}
    for name, (base, spread) in spreads.items():
        noise = np.random.default_rng([zlib.crc32(name.encode()), seed]).standard_normal(out[name].shape)
        drawn = base * np.exp(spread * noise) if base else spread * noise
        out[name] = jnp.asarray(drawn.astype(out[name].dtype))
    for name, factor in factors.items():
        out[name] = (out[name] * factor).astype(out[name].dtype)
    return out
```

```python
from contextlib import ExitStack

import numpy as np

import concourse.bass as bass
from concourse import mybir

F32 = mybir.dt.float32
BF16 = mybir.dt.bfloat16
U8 = mybir.dt.uint8
ALU = mybir.AluOpType
ACT = mybir.ActivationFunctionType
AX = mybir.AxisListType

P = 128
EPS = 1e-5
BIG = 1e30
MASK_NEG = -9000000000000000.0


def wait(eng, sem, value):
    if isinstance(value, int) and value <= 0:
        return
    eng.wait_ge(sem, value)


def build(nc, A, out):
    B, S, D = 32, 64, 128
    KEYS, CD = 128, 96
    H = 16
    T = B * S // P
    CH = 4
    CT = T // CH
    CW = CT * P
    NS = 16
    E, R = 8, 64
    LV, LW = 16, 64
    NB = LV * LW // P
    NN = 15
    XA_SCALE = (64 ** -0.5, 8 ** -0.5)
    D_SCALE = float(D) ** -0.5

    with ExitStack() as ctx:
        def sb(name, shape, dt=F32):
            return ctx.enter_context(nc.sbuf_tensor(name, shape, dt))

        def sem(name):
            return ctx.enter_context(nc.semaphore(name))

        bank = [ctx.enter_context(nc.psum_tensor(f"bank{n}", [P, 1024], F32)) for n in range(4)]

        def ps(n):
            return bank[n // 2][:, 512 * (n % 2):512 * (n % 2) + 512]

        x = sb("x_sb", [P, T, D])
        xnT = sb("xnT", [P, T * P])
        ident = sb("ident", [P, P])
        ones = sb("ones", [1, P])
        st6 = sb("st6", [P, T, 6])
        mean = sb("mean", [P, T])
        lnv = sb("lnv", [P, 3, T])
        rstd = sb("rstd", [P, T])
        std = sb("std", [P, T])
        xn = sb("xn", [P, 2, D])
        epsc = sb("epsc", [P, 1])
        onec = sb("onec", [P, 1])
        rows = sb("rows", [1, 3 * P])
        ctxT = sb("ctxT", [CD + 1, B * KEYS])
        cx = sb("cx", [P, 4, CD])
        wqT = sb("wqT", [64, H, P])
        wkT = sb("wkT", [64, H, CD])
        wvT = sb("wvT", [64, H, CD])
        wo = sb("wo", [64, H, P])
        wqT1 = sb("wqT1", [P, P])
        wkT1 = sb("wkT1", [P, CD])
        wvT1 = sb("wvT1", [P, CD])
        wo1 = sb("wo1", [P, P])
        M = sb("M", [P, H, CD])
        N = sb("N", [CD, H, P])
        hmask = sb("hmask", [P, H])
        pool = sb("pool", [P, 17920])

        def at(o, shape, parts=P, dt=F32):
            n = int(np.prod(shape))
            words = n * (2 if dt is BF16 else 4) // 4
            v = pool[0:parts, o:o + words]
            if dt is not F32:
                v = v.bitcast(dt)
            if len(shape) == 2:
                v = v.rearrange("p (a b) -> p a b", b=shape[1])
            elif len(shape) == 3:
                v = v.rearrange("p (a b c) -> p a b c", b=shape[1], c=shape[2])
            return v

        qmT = [at(2048 * n, (2, H, S), CD + 1) for n in range(2)]
        OT = [at(4096 + 2048 * n, (H, P), CD) for n in range(2)]
        prob = [at(8192 + 1024 * n, (8, KEYS)) for n in range(2)]
        PT = [at(10240 + 1024 * n, (8, P)) for n in range(2)]
        msk8 = pool[0:CD + 1, 12288:12288 + B * KEYS // 4].bitcast(U8)
        mx = sb("mx", [P, 2, 8])
        sm = sb("sm", [P, 2, 8])
        rs = sb("rs", [P, 2, 8])
        wkm = at(8192, (H, CD))
        wom = at(10240, (H, P))

        wx = sb("wx", [P, 160])
        wout = sb("wout", [P, P])
        bx = sb("bx", [P, 1])
        bbc = sb("bbc", [32, 1])
        alog = sb("alog", [P, NS])
        amin = sb("amin", [P, NS])
        dp = sb("dp", [P, 1])
        ddp = sb("ddp", [P, P])
        delta = at(0, (2048,))
        du = at(2048, (2048,))
        abar = [at(4096 + 2048 * n, (2048,)) for n in range(2)]
        bxs = [at(8192 + 512 * n, (512,)) for n in range(2)]
        hs = [at(9216 + 512 * n, (512,)) for n in range(2)]
        hc = [at(10240 + 512 * n, (512,)) for n in range(2)]
        tmp = [at(11264 + 512 * n, (512,)) for n in range(4)]
        yT = at(13312, (2048,))
        bcs = at(15360, (2048,), 96, BF16)
        bcf = at(16384, (512,), 32)
        bcr = at(16896, (512,), 32)
        bselb = sb("bselb", [96, 32, P], BF16)

        wrT = sb("wrT", [P, E])
        aT = at(0, (E * R // P, P))
        bw = at(512, (E * R // P, D))
        midT = [at(1024 + 2048 * n, (4, CW)) for n in range(2)]
        lg = sb("lg", [B, E])
        gt = sb("gt", [B, E, E])
        eq = sb("eq", [B, E, E])
        tri = sb("tri", [B, E, E])
        rank = sb("rank", [B, E])
        lmx = sb("lmx", [B, 2])
        gate = sb("gate", [B, E])
        gT = sb("gT", [E, B])
        esel = sb("esel", [E, 4, P])
        gx = sb("gx", [P, 4, B])

        wqkv = at(0, (384,))
        qT = at(1024, (2048,))
        kT = at(3072, (2048,))
        v = at(5120, (T, D))
        sc = at(7168, (T, S))
        pd = at(8192, (T, P))
        pdT = at(10240, (T, P))
        keep = at(12288, (S,))
        eqz = at(12352, (T, S))
        amx = sb("amx", [P, T])
        asm = sb("asm", [P, T])
        ars = sb("ars", [P, T])

        w1 = sb("w1", [P, 3, LV * LW])
        w2 = sb("w2", [P, 3, NB, D])
        b1 = sb("b1", [P, 3, NB])
        b2 = sb("b2", [96, D])
        nw = sb("nw", [P, 3 * NN])
        nb = sb("nb", [1, 3 * NN])
        hT = [at(7168 + 4096 * n, (NB, CW)) for n in range(2)]
        dec = at(15360, (T, 3, NN))
        selt = sb("selt", [P, T, 3, 32])
        lvl = at(16128, (T * 3, 8))
        selT = sb("selT", [96, T * P])
        seln = at(16512, (T * P,), 96, BF16)
        lselb = sb("lselb", [96, NB, P], BF16)

        s_phase = sem("phase_done")
        ld = {n: sem("ld_" + n) for n in ("x", "w0", "ctx", "msk", "w1", "scan", "moe", "l1x", "wqkv", "tree")}
        cx_in = [sem(f"cx_in{n}") for n in range(4)]
        s_out = sem("out_written")
        names = {}

        def S_(name):
            if name not in names:
                names[name] = sem(name)
            return names[name]

        phases = [0] * 5

        def end_phase(eng, k):
            phases[k] += 1
            eng.drain().then_inc(s_phase, 1)
            eng.wait_ge(s_phase, 5 * phases[k])

        block = ctx.enter_context(nc.Block())

        @block.sync
        def _(sp):
            sp.dma_start(x[:], A["x"]).then_inc(ld["x"], 16)
            for t, n in ((wqT, "l0_wqT"), (wkT, "l0_wkT"), (wvT, "l0_wvT"), (wo, "l0_wo"), (rows[:, 0:P], "l0_bo")):
                sp.dma_start(t if n == "l0_bo" else t[:], A[n]).then_inc(ld["w0"], 16)
            sp.dma_start(ctxT[0:CD, :], A["ctxT"]).then_inc(ld["ctx"], 16)
            for t, n in ((wx[:], "wx"), (wout[:], "wout"), (bx[:], "bx_d"), (bbc[:], "bx_bc"), (alog[:], "alog"),
                         (dp[:], "dp"), (rows[:, P:2 * P], "bout")):
                sp.dma_start(t, A[n]).then_inc(ld["scan"], 16)
            sp.dma_start(wrT[:], A["wrT"]).then_inc(ld["moe"], 16)
            for t, n in ((wqT1, "l1_wqT"), (wkT1, "l1_wkT"), (wvT1, "l1_wvT"), (wo1, "l1_wo")):
                sp.dma_start(t[:], A[n]).then_inc(ld["l1x"], 16)
            for n, name in enumerate("qkv"):
                sp.dma_start(w1[:, n, :], A[name + "_w1"]).then_inc(ld["tree"], 16)
                sp.dma_start(w2[:, n], A[name + "_w2"]).then_inc(ld["tree"], 16)
                sp.dma_start(b1[:, n], A[name + "_b1"]).then_inc(ld["tree"], 16)
                sp.dma_start(b2[32 * n:32 * n + LV, :], A[name + "_b2"]).then_inc(ld["tree"], 16)
                sp.dma_start(nw[:, NN * n:NN * n + NN], A[name + "_nw"]).then_inc(ld["tree"], 16)
                sp.dma_start(nb[:, NN * n:NN * n + NN], A[name + "_nb"]).then_inc(ld["tree"], 16)

            def contexts(layer):
                for n in range(4):
                    if layer:
                        sp.wait_ge(S_("xa_o"), 2 * B * layer + 4)
                    sp.dma_start(cx[:, n, :], A["ctx"][:, n, :]).then_inc(cx_in[n], 16)
                with sp.Fori(0, B // 4 - 1) as i:
                    for n in range(4):
                        sp.wait_ge(S_("xa_o"), 2 * (B * layer + 4 * i + n + 1) + 4)
                        sp.dma_start(cx[:, n, :], A["ctx"][:, bass.ds(4 * i + 4 + n, 1), :].rearrange("p a c -> p (a c)")).then_inc(cx_in[n], 16)

            end_phase(sp, 0)
            contexts(0)
            for k in range(2):
                end_phase(sp, 0)
            sp.dma_start(aT, A["aT"]).then_inc(ld["moe"], 16)
            sp.dma_start(bw, A["bw"]).then_inc(ld["moe"], 16)
            end_phase(sp, 0)
            sp.dma_start(msk8[CD:CD + 1, :], A["mask"]).then_inc(ld["msk"], 16)
            contexts(1)
            end_phase(sp, 0)
            sp.dma_start(wqkv, A["wqkv"]).then_inc(ld["wqkv"], 16)
            end_phase(sp, 0)
            end_phase(sp, 0)
            end_phase(sp, 0)
            sp.dma_start(out, x[:]).then_inc(s_out, 16)
            sp.wait_ge(s_out, 16)

        @block.gpsimd
        def _(g):
            g.memset(ident[:], 0.0).then_inc(S_("g0"), 1)
            g.memset(hmask[:], 1.0).then_inc(S_("g0"), 1)
            g.memset(bselb[:], 0.0).then_inc(S_("g0"), 1)
            g.memset(tri[:], 0.0).then_inc(S_("g0"), 1)
            g.memset(esel[:], 1.0).then_inc(S_("g0"), 1)
            g.memset(lselb[:], 0.0).then_inc(S_("g0"), 1)
            g.memset(ones[:], 1.0).then_inc(S_("g0"), 1)
            g.memset(epsc[:], EPS).then_inc(S_("g0"), 1)
            g.memset(onec[:], 1.0).then_inc(S_("g0"), 1)
            g.memset(selt[:], 0.0).then_inc(S_("g0"), 1)
            for n in range(2):
                g.wait_ge(S_("g0"), 10 + n)
                g.memset(qmT[n][CD:CD + 1], 1.0).then_inc(S_("g0"), 1)
            g.wait_ge(S_("g0"), 12)
            g.affine_select(out=ident[:], in_=ident[:], compare_op=ALU.not_equal, fill=1.0, base=0,
                            pattern=[[-1, P]], channel_multiplier=1).then_inc(S_("consts"), 1)
            g.affine_select(out=hmask[:], in_=hmask[:], compare_op=ALU.is_ge, fill=0.0, base=0,
                            pattern=[[-8, H]], channel_multiplier=1).then_inc(S_("g1"), 1)
            g.wait_ge(S_("g1"), 1)
            g.affine_select(out=hmask[:], in_=hmask[:], compare_op=ALU.is_ge, fill=0.0, base=7,
                            pattern=[[8, H]], channel_multiplier=-1).then_inc(S_("consts"), 1)
            for part in range(3):
                g.affine_select(out=bselb[:], in_=bselb[:], compare_op=ALU.not_equal, fill=1.0, base=-32 * part,
                                pattern=[[-1, 32], [0, P]], channel_multiplier=1).then_inc(S_("g1"), 1)
                g.wait_ge(S_("g1"), 2 + part)
            g.affine_select(out=tri[:], in_=tri[:], compare_op=ALU.is_ge, fill=1.0, base=0,
                            pattern=[[-1, E], [1, E]], channel_multiplier=0).then_inc(S_("g1"), 1)
            g.affine_select(out=esel[:], in_=esel[:], compare_op=ALU.is_ge, fill=0.0, base=0,
                            pattern=[[P, 4], [1, P]], channel_multiplier=-R).then_inc(S_("g1"), 1)
            g.wait_ge(S_("g1"), 6)
            g.affine_select(out=esel[:], in_=esel[:], compare_op=ALU.is_ge, fill=0.0, base=R - 1,
                            pattern=[[-P, 4], [-1, P]], channel_multiplier=R).then_inc(S_("g1"), 1)
            ls = lselb[:].rearrange("p k (u m) -> p k u m", u=2)
            for n in range(3):
                g.affine_select(out=ls, in_=ls, compare_op=ALU.not_equal, fill=1.0, base=-32 * n,
                                pattern=[[-2, NB], [-1, 2], [0, LW]], channel_multiplier=1).then_inc(S_("g1"), 1)
                g.wait_ge(S_("g1"), 8 + n)

            def normalise(layer):
                with g.Fori(0, T) as t:
                    for u in range(2):
                        b = B * layer + 2 * t + u
                        g.wait_ge(S_("xa_recip"), b + 1)
                        g.tensor_tensor(prob[u], prob[u], rs[:, u, :, None].broadcast_to([P, 8, KEYS]),
                                        ALU.mult).then_inc(S_("xa_prob"), 1)

            end_phase(g, 1)
            normalise(0)
            end_phase(g, 1)
            for n in range(NS):
                g.wait_ge(S_("sc_abar0"), n + 1)
                g.memset(abar[n % 2][:, 0:2048:S], 0.0).then_inc(S_("sc_abar"), 1)
            end_phase(g, 1)
            end_phase(g, 1)
            for n in range(2):
                g.memset(qmT[n][CD:CD + 1], 1.0).then_inc(S_("g2"), 1)
                g.wait_ge(S_("g2"), n + 1)
            normalise(1)
            end_phase(g, 1)
            g.memset(pd, 0.0).then_inc(S_("pd_zero"), 1)
            g.memset(keep, 1.0).then_inc(S_("g3"), 1)
            g.wait_ge(S_("g3"), 1)
            for u in range(2):
                ku = keep[64 * u:64 * u + 64, :]
                g.affine_select(out=ku, in_=ku, compare_op=ALU.is_ge, fill=0.0, base=0,
                                pattern=[[1, S]], channel_multiplier=-1).then_inc(S_("keep"), 1)
            end_phase(g, 1)
            end_phase(g, 1)
            end_phase(g, 1)

        @block.tensor
        def _(pe):
            def norm_transposes(k):
                if k == 0:
                    pe.wait_ge(S_("consts"), 1)
                with pe.Fori(0, T // 2) as i:
                    for u in range(2):
                        t = T * k + 2 * i + u
                        pe.wait_ge(S_("ln_xn"), t + 1)
                        pe.wait_ge(S_("ln_ev"), t + 1)
                        pe.transpose(ps(u)[:, 0:P], xn[:, u, :], ident[:]).then_inc(S_("ln_tr"), 1)

            def xattn(layer):
                m0 = 4 * layer
                if layer == 0:
                    pe.wait_ge(ld["w0"], 16 * 5)
                    for c in range(4):
                        for h in range(4 * c, 4 * c + 4):
                            mm = pe.matmul(ps(c)[:, CD * (h % 4):CD * (h % 4) + CD], wqT[:, h, :], wkT[:, h, :],
                                           start=True, stop=True)
                        mm.then_inc(S_("xa_m"), 1)
                        for h in range(4 * c, 4 * c + 4):
                            mm = pe.matmul(ps(4 + c)[0:CD, P * (h % 4):P * (h % 4) + P], wvT[:, h, :], wo[:, h, :],
                                           start=True, stop=True)
                        mm.then_inc(S_("xa_n"), 1)
                else:
                    pe.wait_ge(ld["l1x"], 16 * 4)
                    pe.wait_ge(S_("wkm"), 2)
                    for c in range(4):
                        pe.matmul(ps(c)[:, 0:4 * CD], wqT1[:], wkm[:, 4 * c:4 * c + 4, :],
                                  start=True, stop=True).then_inc(S_("xa_m"), 1)
                        pe.matmul(ps(4 + c)[0:CD, :], wvT1[:], wom[:, 4 * c:4 * c + 4, :],
                                  start=True, stop=True).then_inc(S_("xa_n"), 1)
                pe.wait_ge(ld["ctx"], 16)
                pe.wait_ge(S_("xa_wts"), layer + 1)
                pe.wait_ge(S_("xa_mask"), layer + 1)
                pe.wait_ge(S_("g2" if layer else "g0"), 2 if layer else 12)

                def tile(tf, f, tb, s):
                    def queries(c):
                        if tf is None:
                            return
                        wait(pe, S_("xa_qev"), 4 * (T * layer + tf) + c)
                        for h in range(4):
                            mm = pe.matmul(ps(2)[0:CD, P * h:P * h + P], M[:, 4 * c + h, :],
                                           xnT[:, bass.ds(tf * P, P)], start=True, stop=True)
                        mm.then_inc(S_("xa_q"), 1)

                    def turns(u, hh):
                        if tb is None:
                            return
                        b = B * layer + 2 * tb + u
                        if hh == 0:
                            pe.wait_ge(S_("xa_prob"), b + 1)
                        pe.wait_ge(S_("xa_ptev"), 2 * b + hh + 1)
                        for j in range(4):
                            mm = pe.transpose(ps(4 + hh)[:, P * j:P * j + P], prob[u][:, 4 * hh + j, :], ident[:])
                        mm.then_inc(S_("xa_pt"), 1)

                    def scores(u):
                        if tf is None:
                            return
                        b = B * layer + 2 * tf + u
                        if u == 0:
                            pe.wait_ge(S_("xa_qev"), 4 * (T * layer + tf) + 4)
                        wait(pe, S_("xa_sub"), b)
                        kv = ctxT[:, bass.ds((2 * tf + u) * KEYS, KEYS)]
                        for j in range(8):
                            mm = pe.matmul(ps(j // 4)[:, P * (j % 4):P * (j % 4) + P],
                                           qmT[f][:, u, 2 * j:2 * j + 2, :].rearrange("p a b -> p (a b)"), kv, start=True, stop=True)
                        mm.then_inc(S_("xa_sc"), 1)

                    def values(u):
                        if tb is None:
                            return
                        b = B * layer + 2 * tb + u
                        pe.wait_ge(cx_in[2 * s + u], 16 * ((B // 4) * layer + (tb // 2 if isinstance(tb, int) else tb_pair[0])) + 16)
                        for hh in range(2):
                            pe.wait_ge(S_("xa_ptev"), 2 * b + hh + 3)
                            pe.wait_ge(S_("xa_oev"), 2 * b + hh + 1)
                            mm = pe.matmul(ps(6 + hh)[0:CD, :], cx[:, 2 * s + u, :], PT[u][:, 4 * hh:4 * hh + 4, :],
                                           start=True, stop=True)
                            mm.then_inc(S_("xa_o"), 1)

                    def project():
                        if tb is None:
                            return
                        t = T * layer + tb
                        pe.wait_ge(S_("xa_oev"), 4 * t + 6)
                        wait(pe, S_("xa_qev"), 4 * t + 8 if tf is not None else 4 * t + 4)
                        pe.wait_ge(S_("xa_add"), t + 1)
                        if layer == 0:
                            pe.matmul(ps(3)[:, 0:P], ones[:], rows[:, 0:P], start=True, stop=False)
                        for h in range(H):
                            mm = pe.matmul(ps(3)[:, 0:P], OT[s][:, h, :], N[:, h, :],
                                           start=(h == 0 and layer == 1), stop=(h == H - 1))
                        mm.then_inc(S_("xa_y"), 1)

                    queries(0)
                    turns(0, 0)
                    queries(1)
                    turns(0, 1)
                    queries(2)
                    turns(1, 0)
                    queries(3)
                    turns(1, 1)
                    scores(0)
                    values(0)
                    scores(1)
                    values(1)
                    project()

                tb_pair = [None]
                tile(0, 0, None, None)
                with pe.Fori(0, T // 2 - 1) as i:
                    tb_pair[0] = i
                    tile(2 * i + 1, 1, 2 * i, 0)
                    tile(2 * i + 2, 0, 2 * i + 1, 1)
                tile(T - 1, 1, T - 2, 0)
                tile(None, None, T - 1, 1)

            pe.sem_inc(S_("xa_y"), 2)
            pe.sem_inc(S_("xa_o"), 4)
            norm_transposes(0)
            end_phase(pe, 2)
            xattn(0)
            end_phase(pe, 2)
            norm_transposes(1)
            pe.wait_ge(ld["scan"], 16 * 7)
            pe.wait_ge(S_("ln_ev"), 2 * T + 2)
            pe.wait_ge(S_("ddp"), 1)
            for c in range(CH):
                xc = xnT[:, CW * c:CW * c + CW]
                if c >= 2:
                    pe.wait_ge(S_("sc_d0"), c - 1)
                pe.matmul(ps(c % 2), wx[:, 0:D], xc, start=True, stop=True).then_inc(S_("sc_dp"), 1)
                if c >= 2:
                    pe.wait_ge(S_("sc_bcf"), c - 1)
                pe.matmul(ps(2 + c % 2)[0:32, :], wx[:, D:D + 32], xc, start=True, stop=True).then_inc(S_("sc_bc"), 1)
                pe.matmul(ps(4 + c), ddp[:], xc, start=True, stop=False)
            pe.wait_ge(S_("sc_split"), CH)
            pe.wait_ge(S_("g1"), 10)
            pe.wait_ge(S_("sc_delta"), CH)

            for k in range(4 * NS):
                n, c = divmod(k, 4)
                if k >= 2:
                    pe.wait_ge(S_("sc_bx"), k - 1)
                pe.matmul(ps(k % 2), bselb[:, n, :], bcs[:, CW * c:CW * c + CW], start=True, stop=True).then_inc(S_("sc_b"), 1)
                if k >= 2:
                    pe.wait_ge(S_("sc_hc"), k - 1)
                pe.matmul(ps(2 + k % 2), bselb[:, 16 + n, :], bcs[:, CW * c:CW * c + CW], start=True, stop=True).then_inc(S_("sc_c"), 1)
                if k >= 2:
                    pe.matmul(ps(4 + (k - 2) % 4), ident[:], hc[k % 2], start=False, stop=(k - 2) // 4 == NS - 1).then_inc(S_("sc_acc"), 1)
            for k in range(4 * NS, 4 * NS + 2):
                pe.wait_ge(S_("sc_hc"), k - 1)
                pe.matmul(ps(4 + (k - 2) % 4), ident[:], hc[k % 2], start=False, stop=True).then_inc(S_("sc_acc"), 1)
            for c in range(CH):
                pe.wait_ge(S_("sc_yT"), c + 1)
                for t in range(CT * c, CT * c + CT):
                    o = ps(c)[:, P * (t % CT):P * (t % CT) + P]
                    pe.matmul(o, ones[:], rows[:, P:2 * P], start=True, stop=False)
                    mm = pe.matmul(o, yT[:, P * t:P * t + P], wout[:], start=False, stop=True)
                mm.then_inc(S_("sc_out"), 1)
            end_phase(pe, 2)
            norm_transposes(2)
            pe.wait_ge(S_("ln_ev"), 3 * T + 2)
            pe.wait_ge(ld["moe"], 48)
            pe.matmul(ps(7)[0:B, 0:E], xnT[:, 0:2048:S], wrT[:], start=True, stop=True).then_inc(S_("me_lg"), 1)
            pe.wait_ge(S_("me_gate"), 1)
            pe.transpose(ps(7)[0:E, 64:64 + B], gate[:], ident[0:B, 0:B]).then_inc(S_("me_gT"), 1)
            pe.wait_ge(S_("me_gTs"), 1)
            for k in range(4):
                mm = pe.matmul(ps(7)[:, 128 + B * k:128 + B * k + B], esel[:, k, :], gT[:], start=True, stop=True)
            mm.then_inc(S_("me_gx"), 1)
            for c in range(CH):
                for k in range(4):
                    n = 4 * c + k
                    if n >= 2:
                        pe.wait_ge(S_("me_mev"), n - 1)
                    pe.matmul(ps(n % 2), aT[:, k, :], xnT[:, CW * c:CW * c + CW], start=True, stop=True).then_inc(S_("me_m"), 1)
                pe.wait_ge(S_("me_mev"), 4 * c + 4)
                for t in range(CT):
                    o = ps(2 + c)[:, P * t:P * t + P]
                    pe.matmul(o, xnT[:, CW * c + P * t:CW * c + P * t + P], ident[:], start=True, stop=False)
                    for k in range(4):
                        mm = pe.matmul(o, midT[c % 2][:, k, P * t:P * t + P], bw[:, k, :], start=False, stop=(k == 3))
                mm.then_inc(S_("me_y"), 1)
            end_phase(pe, 2)
            norm_transposes(3)
            pe.wait_ge(S_("ln_ev"), 4 * T + 2)
            xattn(1)
            end_phase(pe, 2)

            def attend(k):
                for b in range(B):
                    t, u = divmod(b, 2)
                    mm = pe.matmul(ps(t // 8)[64 * u:64 * u + 64, S * (t % 8):S * (t % 8) + S], qT[:, S * b:S * b + S],
                                   kT[:, S * b:S * b + S], start=True, stop=True)
                mm.then_inc(S_("at_sc"), 1)
                pe.wait_ge(S_("at_p"), 2 * k + 2)
                for c in range(CH):
                    for t in range(CT):
                        mm = pe.transpose(ps(2 + c)[:, P * t:P * t + P], pd[:, CT * c + t, :], ident[:])
                    mm.then_inc(S_("at_pt"), 1)
                for c in range(CH):
                    pe.wait_ge(S_("at_ptev"), CH * k + c + 1)
                    if c >= 2:
                        pe.wait_ge(S_("at_add"), CH * k + c - 1)
                    for t in range(CT):
                        mm = pe.matmul(ps(6 + c % 2)[:, P * t:P * t + P], pdT[:, CT * c + t, :], v[:, CT * c + t, :],
                                       start=True, stop=True)
                    mm.then_inc(S_("at_y"), 1)

            norm_transposes(4)
            pe.wait_ge(S_("ln_ev"), 5 * T + 2)
            pe.wait_ge(ld["wqkv"], 16)
            for c in range(CH):
                for w in range(2):
                    n = 2 * c + w
                    if n >= 2:
                        pe.wait_ge(S_("sa_qk"), n - 1)
                    pe.matmul(ps(n % 2), wqkv[:, D * w:D * w + D], xnT[:, CW * c:CW * c + CW], start=True,
                              stop=True).then_inc(S_("sa_q"), 1)
            for c in range(CH):
                for t in range(CT):
                    mm = pe.matmul(ps(2 + c)[:, P * t:P * t + P], xnT[:, CW * c + P * t:CW * c + P * t + P],
                                   wqkv[:, 2 * D:3 * D], start=True, stop=True)
                mm.then_inc(S_("sa_v"), 1)
            pe.wait_ge(S_("sa_qk"), 8)
            pe.wait_ge(S_("sa_vev"), 4)
            attend(0)
            end_phase(pe, 2)
            norm_transposes(5)
            pe.wait_ge(S_("ln_ev"), 6 * T + 2)
            pe.wait_ge(ld["tree"], 16 * 18)
            for t in range(T):
                o = ps(2 + t // 8)[:, 48 * (t % 8):48 * (t % 8) + 3 * NN]
                pe.matmul(o, ones[:], nb[:], start=True, stop=False)
                mm = pe.matmul(o, xnT[:, P * t:P * t + P], nw[:], start=False, stop=True)
            mm.then_inc(S_("tr_sc"), 1)
            pe.wait_ge(S_("tr_sel"), 1)
            for c in range(CH):
                for t in range(CT):
                    mm = pe.transpose(ps(4 + c)[0:96, P * t:P * t + P],
                                      selt[:, CT * c + t].rearrange("p a b -> p (a b)"), ident[:])
                mm.then_inc(S_("tr_st"), 1)
            pe.wait_ge(S_("tr_selT"), 2 * CH)
            for c in range(CH):
                for w in range(3):
                    g2 = 3 * c + w
                    r = slice(32 * w, 32 * w + LV)
                    for k in range(NB):
                        n = NB * g2 + k
                        if n >= 4:
                            pe.wait_ge(S_("lf_h0" if n % 2 == 0 else "lf_h1"), (n - 4) // 2 + 1)
                        pe.matmul(ps(n % 4), lselb[r, k, :], seln[r, CW * c:CW * c + CW], start=True, stop=False)
                        pe.matmul(ps(n % 4), w1[:, w, P * k:P * k + P], xnT[:, CW * c:CW * c + CW], start=False,
                                  stop=True).then_inc(S_("lf_pre"), 1)
                    pe.wait_ge(S_("lf_h0"), 4 * (g2 + 1))
                    pe.wait_ge(S_("lf_h1"), 4 * (g2 + 1))
                    if g2 >= 2:
                        pe.wait_ge(S_("lf_oev"), g2 - 1)
                    if w < 2:
                        o = ps(4 + g2 % 2)
                        pe.matmul(o, b2[r, :], selT[r, CW * c:CW * c + CW], start=True, stop=False)
                        for k in range(NB):
                            mm = pe.matmul(o, w2[:, w, k, :], hT[g2 % 2][:, k, :], start=False, stop=(k == NB - 1))
                    else:
                        for t in range(CT):
                            o = ps(4 + g2 % 2)[:, P * t:P * t + P]
                            tt = CW * c + P * t
                            pe.matmul(o, selT[r, tt:tt + P], b2[r, :], start=True, stop=False)
                            for k in range(NB):
                                mm = pe.matmul(o, hT[g2 % 2][:, k, P * t:P * t + P], w2[:, w, k, :], start=False,
                                               stop=(k == NB - 1))
                    mm.then_inc(S_("lf_o"), 1)
            pe.wait_ge(S_("lf_oev"), 12)
            end_phase(pe, 2)
            attend(1)
            end_phase(pe, 2)

        @block.vector
        def _(dve):
            def layernorm(k):
                if k == 0:
                    dve.wait_ge(ld["x"], 16)
                with dve.Fori(0, T // 2) as i:
                    for u in range(2):
                        t = 2 * i + u
                        dve.bn_stats(st6[:, bass.ds(t, 1), :].rearrange("p a b -> p (a b)"),
                                     x[:, bass.ds(t, 1), :].rearrange("p a b -> p (a b)")).then_inc(S_("ln_st"), 1)
                me, ve, mo, vo = (st6[:, :, n] for n in (1, 2, 4, 5))
                dve.wait_ge(S_("ln_st"), T * (k + 1))
                dve.tensor_tensor(lnv[:, 0], me, mo, ALU.subtract).then_inc(S_("ln_a"), 1)
                dve.tensor_tensor(lnv[:, 1], ve, vo, ALU.add).then_inc(S_("ln_a"), 1)
                dve.tensor_tensor(lnv[:, 2], me, mo, ALU.add).then_inc(S_("ln_a"), 1)
                dve.wait_ge(S_("ln_a"), 5 * k + 3)
                dve.tensor_tensor(lnv[:, 0], lnv[:, 0], lnv[:, 0], ALU.mult).then_inc(S_("ln_a"), 1)
                dve.tensor_scalar(mean[:], lnv[:, 2], 0.5, None, ALU.mult).then_inc(S_("ln_a"), 1)
                dve.wait_ge(S_("ln_a"), 5 * k + 5)
                dve.scalar_tensor_tensor(out=lnv[:, 1], in0=lnv[:, 1], scalar=4.0 / D, in1=lnv[:, 0],
                                         op0=ALU.mult, op1=ALU.add).then_inc(S_("ln_mv"), 1)
                dve.wait_ge(S_("ln_std"), k + 1)
                dve.reciprocal(rstd[:], std[:]).then_inc(S_("ln_r"), 1)
                dve.wait_ge(S_("ln_r"), k + 1)
                with dve.Fori(0, T // 2) as i:
                    for u in range(2):
                        t = 2 * i + u
                        dve.wait_ge(S_("ln_ev"), T * k + t + 1)
                        dve.tensor_scalar(xn[:, u, :], x[:, bass.ds(t, 1), :].rearrange("p a b -> p (a b)"),
                                          mean[:, bass.ds(t, 1)], rstd[:, bass.ds(t, 1)],
                                          ALU.subtract, ALU.mult).then_inc(S_("ln_xn"), 1)

            def xattn(layer):
                if layer == 1:
                    dve.wait_ge(ld["l1x"], 64)
                    dve.wait_ge(S_("consts"), 2)
                    dve.tensor_tensor(wkm, wkT1[:, None, :].broadcast_to([P, H, CD]),
                                      hmask[:, :, None].broadcast_to([P, H, CD]), ALU.mult).then_inc(S_("wkm"), 1)
                    dve.tensor_tensor(wom, wo1[:, None, :].broadcast_to([P, H, P]),
                                      hmask[:, :, None].broadcast_to([P, H, P]), ALU.mult).then_inc(S_("wkm"), 1)
                if layer == 0:
                    dve.memset(ctxT[CD:CD + 1, :], 0.0).then_inc(S_("xa_mask"), 1)
                else:
                    dve.wait_ge(ld["msk"], 16)
                    dve.tensor_scalar(ctxT[CD:CD + 1, :], msk8[CD:CD + 1, :], -1.0, BIG, ALU.add, ALU.mult).then_inc(S_("xa_mask"), 1)
                for c in range(4):
                    dve.wait_ge(S_("xa_m"), 4 * layer + c + 1)
                    dve.tensor_copy(M[:, 4 * c:4 * c + 4, :], ps(c)[:, 0:4 * CD].rearrange("p (a b) -> p a b", b=CD)).then_inc(S_("xa_w"), 1)
                    dve.wait_ge(S_("xa_n"), 4 * layer + c + 1)
                    dve.tensor_copy(N[:, 4 * c:4 * c + 4, :], ps(4 + c)[0:CD, :].rearrange("p (a b) -> p a b", b=P)).then_inc(S_("xa_w"), 1)
                dve.wait_ge(S_("xa_w"), 8 * layer + 8)
                dve.sem_inc(S_("xa_wts"), 1)

                def softmax(b, u):
                    A_ = bank[0][:, :].rearrange("p (j k) -> p j k", k=KEYS)
                    dve.wait_ge(S_("xa_sc"), b + 1)
                    dve.tensor_reduce(mx[:, u, :], A_, AX.X, ALU.max).then_inc(S_("xa_mx"), 1)
                    dve.wait_ge(S_("xa_mx"), b + 1)
                    wait(dve, S_("xa_pt"), 2 * (b - 1) if isinstance(b, int) else 2 * b - 2)
                    dve.tensor_tensor(prob[u], A_, mx[:, u, :, None].broadcast_to([P, 8, KEYS]), ALU.subtract).then_inc(S_("xa_sub"), 1)

                def sums(b, u):
                    dve.wait_ge(S_("xa_exp"), b + 1)
                    dve.tensor_reduce(sm[:, u, :], prob[u], AX.X, ALU.add).then_inc(S_("xa_sm"), 1)
                    dve.wait_ge(S_("xa_sm"), b + 1)
                    dve.reciprocal(rs[:, u, :], sm[:, u, :]).then_inc(S_("xa_recip"), 1)

                def outputs(tb, s, u):
                    b = B * layer + 2 * tb + u
                    for hh in range(2):
                        dve.wait_ge(S_("xa_o"), 2 * b + hh + 5)
                        if u == 0 and hh == 0:
                            dve.wait_ge(S_("xa_y"), T * layer + tb + 1)
                        dve.tensor_copy(OT[s][:, 8 * hh:8 * hh + 8, 64 * u:64 * u + 64],
                                        ps(6 + hh)[0:CD, :].rearrange("p (h t) -> p h t", t=S)).then_inc(S_("xa_oev"), 1)

                def add(tb):
                    t = T * layer + tb
                    dve.wait_ge(S_("xa_y"), t + 3)
                    xt = x[:, bass.ds(tb, 1), :].rearrange("p a b -> p (a b)")
                    dve.tensor_tensor(xt, ps(3)[:, 0:P], xt, ALU.add).then_inc(S_("xa_add"), 1)

                def tile(tf, tb, s):
                    if tf is not None:
                        softmax(B * layer + 2 * tf, 0)
                    if tb is not None:
                        outputs(tb, s, 0)
                    if tf is not None:
                        sums(B * layer + 2 * tf, 0)
                        softmax(B * layer + 2 * tf + 1, 1)
                    if tb is not None:
                        outputs(tb, s, 1)
                    if tf is not None:
                        sums(B * layer + 2 * tf + 1, 1)
                    if tb is not None:
                        add(tb)

                tile(0, None, None)
                with dve.Fori(0, T // 2 - 1) as i:
                    tile(2 * i + 1, 2 * i, 0)
                    tile(2 * i + 2, 2 * i + 1, 1)
                tile(T - 1, T - 2, 0)
                tile(None, T - 1, 1)

            dve.sem_inc(S_("xa_oev"), 2)
            dve.sem_inc(S_("xa_add"), 1)
            layernorm(0)
            end_phase(dve, 3)
            xattn(0)
            end_phase(dve, 3)
            layernorm(1)
            dve.wait_ge(ld["scan"], 16 * 7)
            dve.tensor_scalar(ddp[:], ident[:], dp[:, 0:1], None, ALU.mult).then_inc(S_("ddp"), 1)
            dve.wait_ge(S_("ln_ev"), 2 * T + 2)
            for c in range(CH):
                cc = slice(CW * c, CW * c + CW)
                dve.wait_ge(S_("sc_t"), 2 * c + 1)
                dve.tensor_scalar(delta[:, cc], ps(c % 2), bx[:, 0:1], 0.0, ALU.add, ALU.max).then_inc(S_("sc_d0"), 1)
                dve.wait_ge(S_("sc_ln"), c + 1)
                dve.wait_ge(S_("sc_d0"), c + 1)
                dve.tensor_tensor(delta[:, cc], delta[:, cc], tmp[c], ALU.add).then_inc(S_("sc_delta"), 1)
                dve.wait_ge(S_("sc_delta"), c + 1)
                dve.tensor_tensor(du[:, cc], delta[:, cc], xnT[:, cc], ALU.mult).then_inc(S_("sc_du"), 1)
                dve.wait_ge(S_("sc_bc"), c + 1)
                if c:
                    dve.wait_ge(S_("sc_sp"), 5 * c)
                dve.tensor_scalar(bcf, ps(2 + c % 2)[0:32, :], bbc[:, 0:1], None, ALU.add).then_inc(S_("sc_bcf"), 1)
                dve.wait_ge(S_("sc_bcf"), c + 1)
                dve.tensor_copy(bcs[0:32, cc], bcf).then_inc(S_("sc_sp"), 1)
                dve.wait_ge(S_("sc_sp"), 5 * c + 1)
                dve.tensor_tensor(bcr, bcf, bcs[0:32, cc], ALU.subtract).then_inc(S_("sc_sp"), 1)
                dve.wait_ge(S_("sc_sp"), 5 * c + 2)
                dve.tensor_copy(bcs[32:64, cc], bcr).then_inc(S_("sc_sp"), 1)
                dve.wait_ge(S_("sc_sp"), 5 * c + 3)
                dve.tensor_copy(bcf, bcs[32:64, cc]).then_inc(S_("sc_sp"), 1)
                dve.wait_ge(S_("sc_sp"), 5 * c + 4)
                dve.tensor_tensor(bcf, bcr, bcf, ALU.subtract).then_inc(S_("sc_sp"), 1)
                dve.wait_ge(S_("sc_sp"), 5 * c + 5)
                dve.tensor_copy(bcs[64:96, cc], bcf).then_inc(S_("sc_split"), 1)
                dve.wait_ge(S_("sc_split"), c + 1)
            for k in range(4 * NS + 1):
                n, c = divmod(k, 4)
                if k < 4 * NS:
                    cc = slice(CW * c, CW * c + CW)
                    dve.wait_ge(S_("sc_b"), k + 1)
                    if k == 0:
                        dve.wait_ge(S_("sc_du"), CH)
                    dve.tensor_tensor(bxs[k % 2], ps(k % 2), du[:, cc], ALU.mult).then_inc(S_("sc_bx"), 1)
                if k:
                    m = k - 1
                    dve.wait_ge(S_("sc_c"), m + 1)
                    dve.wait_ge(S_("sc_h"), m + 1)
                    if m >= 2:
                        dve.wait_ge(S_("sc_acc"), m - 1)
                    dve.tensor_tensor(hc[m % 2], ps(2 + m % 2), hs[m % 2], ALU.mult).then_inc(S_("sc_hc"), 1)
                if k < 4 * NS:
                    dve.wait_ge(S_("sc_bx"), k + 1)
                    dve.wait_ge(S_("sc_abar"), n + 1)
                    if k >= 2:
                        dve.wait_ge(S_("sc_hc"), k - 1)
                    dve.tensor_tensor_scan(hs[k % 2], abar[n % 2][:, cc], bxs[k % 2], 0.0, ALU.mult, ALU.add).then_inc(S_("sc_h"), 1)
            for c in range(CH):
                dve.wait_ge(S_("sc_out"), c + 1)
                xt = x[:, CT * c:CT * c + CT, :].rearrange("p a b -> p (a b)")
                dve.tensor_tensor(xt, ps(c), xt, ALU.add)
            end_phase(dve, 3)
            layernorm(2)
            link = [0]

            def chain(ins):
                ins.then_inc(S_("chain"), 1)
                link[0] += 1
                dve.wait_ge(S_("chain"), link[0])

            dve.wait_ge(S_("me_lg"), 1)
            chain(dve.tensor_copy(lg[:], ps(7)[0:B, 0:E]))
            li = lg[:, :, None].broadcast_to([B, E, E])
            lj = lg[:, None, :].broadcast_to([B, E, E])
            chain(dve.tensor_tensor(eq[:], lj, li, ALU.is_equal))
            dve.wait_ge(S_("g1"), 7)
            chain(dve.tensor_tensor(eq[:], eq[:], tri[:], ALU.mult))
            chain(dve.tensor_tensor(gt[:], lj, li, ALU.is_gt))
            chain(dve.tensor_tensor(gt[:], gt[:], eq[:], ALU.add))
            chain(dve.tensor_reduce(rank[:], gt[:], AX.X, ALU.add))
            chain(dve.tensor_scalar(rank[:], rank[:], 1.5, None, ALU.is_lt))
            chain(dve.tensor_reduce(lmx[:, 0:1], lg[:], AX.X, ALU.max))
            chain(dve.tensor_scalar(lg[:], lg[:], lmx[:, 0:1], None, ALU.subtract))
            dve.sem_inc(S_("me_lsub"), 1)
            dve.wait_ge(S_("me_exp"), 1)
            chain(dve.tensor_tensor(gate[:], gate[:], rank[:], ALU.mult))
            chain(dve.tensor_reduce(lmx[:, 1:2], gate[:], AX.X, ALU.add))
            chain(dve.reciprocal(lmx[:, 1:2], lmx[:, 1:2]))
            dve.tensor_scalar(gate[:], gate[:], lmx[:, 1:2], None, ALU.mult).then_inc(S_("me_gate"), 1)
            dve.wait_ge(S_("me_gT"), 1)
            dve.tensor_copy(gT[:], ps(7)[0:E, 64:64 + B]).then_inc(S_("me_gTs"), 1)
            dve.wait_ge(S_("me_gx"), 1)
            chain(dve.tensor_copy(gx[:], ps(7)[:, 128:128 + 4 * B].rearrange("p (k b) -> p k b", b=B)))
            for c in range(CH):
                for k in range(4):
                    n = 4 * c + k
                    dve.wait_ge(S_("me_m"), n + 1)
                    if k == 0 and c >= 2:
                        dve.wait_ge(S_("me_y"), c - 1)
                    dve.tensor_tensor(midT[c % 2][:, k, :].rearrange("p (b s) -> p b s", s=S),
                                      ps(n % 2).rearrange("p (b s) -> p b s", s=S),
                                      gx[:, k, 8 * c:8 * c + 8, None].broadcast_to([P, 8, S]), ALU.mult).then_inc(S_("me_mev"), 1)
            for c in range(CH):
                dve.wait_ge(S_("me_y"), c + 1)
                xt = x[:, CT * c:CT * c + CT, :].rearrange("p a b -> p (a b)")
                dve.tensor_tensor(xt, ps(2 + c), xt, ALU.add)
            end_phase(dve, 3)
            layernorm(3)
            xattn(1)
            end_phase(dve, 3)

            def attend(k):
                def chunk(c):
                    return slice(8 * c, 8 * c + 8)
                dve.wait_ge(S_("at_sc"), k + 1)
                for c in range(2):
                    chain(dve.tensor_scalar(sc[:, chunk(c), :], ps(c).rearrange("p (t s) -> p t s", s=S), D_SCALE, None, ALU.mult))
                if k == 0:
                    dve.wait_ge(S_("keep"), 2)
                    chain(dve.tensor_tensor(sc, sc, keep[:, None, :].broadcast_to([P, T, S]), ALU.mult))
                    chain(dve.tensor_scalar(eqz, sc, 0.0, MASK_NEG, ALU.is_equal, ALU.mult))
                    chain(dve.tensor_tensor(sc, sc, eqz, ALU.add))
                chain(dve.tensor_reduce(amx[:], sc, AX.X, ALU.max))
                chain(dve.tensor_tensor(sc, sc, amx[:, :, None].broadcast_to([P, T, S]), ALU.subtract))
                dve.sem_inc(S_("at_sub"), 1)
                dve.wait_ge(S_("at_exp"), k + 1)
                chain(dve.tensor_reduce(asm[:], sc, AX.X, ALU.add))
                chain(dve.reciprocal(ars[:], asm[:]))
                dve.wait_ge(S_("pd_zero"), k + 1)
                for u in range(2):
                    r = slice(64 * u, 64 * u + 64)
                    dve.tensor_tensor(pd[r, :, 64 * u:64 * u + 64], sc[r], ars[r, :, None].broadcast_to([64, T, S]),
                                      ALU.mult).then_inc(S_("at_p"), 1)
                for c in range(CH):
                    dve.wait_ge(S_("at_y"), CH * k + c + 1)
                    xt = x[:, CT * c:CT * c + CT, :].rearrange("p a b -> p (a b)")
                    dve.tensor_tensor(xt, ps(6 + c % 2), xt, ALU.add).then_inc(S_("at_add"), 1)

            layernorm(4)
            for c in range(CH):
                dve.wait_ge(S_("sa_v"), c + 1)
                dve.tensor_copy(v[:, CT * c:CT * c + CT, :], ps(2 + c).rearrange("p (a b) -> p a b", b=D)).then_inc(S_("sa_vev"), 1)
            attend(0)
            end_phase(dve, 3)
            layernorm(5)
            dve.wait_ge(S_("tr_sc"), 1)
            for c in range(2):
                chain(dve.tensor_scalar(dec[:, 8 * c:8 * c + 8].rearrange("p t a b -> p t (a b)"),
                                        ps(2 + c)[:, 0:384].rearrange("p (t n) -> p t n", n=48)[:, :, 0:3 * NN],
                                        0.0, None, ALU.is_ge))
            decf = dec.rearrange("p t a b -> p (t a) b")
            self_ = selt[:].rearrange("p t a b -> p (t a) b")
            bufs = [lvl, self_]
            dve.wait_ge(S_("g0"), 12)
            cur = self_
            chain(dve.tensor_copy(cur[:, :, 1:2], decf[:, :, 0:1]))
            chain(dve.tensor_scalar(cur[:, :, 0:1], decf[:, :, 0:1], -1.0, 1.0, ALU.mult, ALU.add))
            for depth in range(1, 4):
                w = 2 ** depth
                chain(dve.tensor_copy(lvl[:, :, 0:w], self_[:, :, 0:w]))
                chain(dve.tensor_tensor(self_[:, :, 1:2 * w:2], lvl[:, :, 0:w], decf[:, :, w - 1:2 * w - 1], ALU.mult))
                chain(dve.tensor_tensor(self_[:, :, 0:2 * w:2], lvl[:, :, 0:w], self_[:, :, 1:2 * w:2], ALU.subtract))
            dve.sem_inc(S_("tr_sel"), 1)
            for c in range(CH):
                dve.wait_ge(S_("tr_st"), c + 1)
                dve.tensor_copy(selT[:, CW * c:CW * c + CW], ps(4 + c)[0:96, :]).then_inc(S_("tr_selT"), 1)
                dve.tensor_scalar(seln[:, CW * c:CW * c + CW], ps(4 + c)[0:96, :], -1.0, BIG, ALU.add,
                                  ALU.mult).then_inc(S_("tr_selT"), 1)
            for c in range(CH):
                for w in range(3):
                    g2 = 3 * c + w
                    for k in range(1, NB, 2):
                        n = NB * g2 + k
                        dve.wait_ge(S_("lf_pre"), n + 1)
                        if g2 >= 2:
                            dve.wait_ge(S_("lf_o"), g2 - 1)
                        dve.tensor_scalar(hT[g2 % 2][:, k, :], ps(n % 4), b1[:, w, k:k + 1], 0.0, ALU.add,
                                          ALU.max).then_inc(S_("lf_h1"), 1)
                    dve.wait_ge(S_("lf_o"), g2 + 1)
                    o = ps(4 + g2 % 2)
                    cc = slice(CW * c, CW * c + CW)
                    if w < 2:
                        dve.tensor_copy((qT, kT)[w][:, cc], o).then_inc(S_("lf_oev"), 1)
                    else:
                        dve.tensor_copy(v[:, CT * c:CT * c + CT, :], o.rearrange("p (a b) -> p a b", b=D)).then_inc(S_("lf_oev"), 1)
            end_phase(dve, 3)
            dve.memset(pd, 0.0).then_inc(S_("pd_zero"), 1)
            attend(1)
            end_phase(dve, 3)

        @block.scalar
        def _(act):
            def layernorm(k):
                if k == 0:
                    act.wait_ge(S_("g0"), 12)
                    act.sem_inc(S_("ln_ev"), 2)
                act.wait_ge(S_("ln_mv"), k + 1)
                act.activation(std[:], lnv[:, 1], ACT.Sqrt, bias=epsc[:, 0:1], scale=0.25).then_inc(S_("ln_std"), 1)
                with act.Fori(0, T // 2) as i:
                    for u in range(2):
                        t = 2 * i + u
                        act.wait_ge(S_("ln_tr"), T * k + t + 1)
                        act.copy(xnT[:, bass.ds(t * P, P)], ps(u)[:, 0:P]).then_inc(S_("ln_ev"), 1)

            def xattn(layer):
                def exps(b, u):
                    act.wait_ge(S_("xa_sub"), b + 1)
                    act.activation(prob[u], prob[u], ACT.Exp, scale=XA_SCALE[layer]).then_inc(S_("xa_exp"), 1)

                def tile(tf, f, tb):
                    def queries(c):
                        if tf is None:
                            return
                        t = T * layer + tf
                        act.wait_ge(S_("xa_q"), 4 * t + c + 1)
                        wait(act, S_("xa_sc"), 2 * t - 2)
                        act.copy(qmT[f][0:CD, :, 4 * c:4 * c + 4, :].rearrange("p u h t -> p h u t"),
                                 ps(2)[0:CD, :].rearrange("p (h u t) -> p h u t", u=2, t=S)).then_inc(S_("xa_qev"), 1)

                    def turned(u, hh):
                        if tb is None:
                            return
                        b = B * layer + 2 * tb + u
                        act.wait_ge(S_("xa_pt"), 2 * b + hh + 1)
                        act.wait_ge(S_("xa_o"), 2 * b + hh + 1)
                        act.copy(PT[u][:, 4 * hh:4 * hh + 4, :],
                                 ps(4 + hh).rearrange("p (j r) -> p j r", r=P)).then_inc(S_("xa_ptev"), 1)

                    queries(0)
                    turned(0, 0)
                    queries(1)
                    turned(0, 1)
                    queries(2)
                    turned(1, 0)
                    queries(3)
                    turned(1, 1)
                    if tf is not None:
                        exps(B * layer + 2 * tf, 0)
                        exps(B * layer + 2 * tf + 1, 1)

                tile(0, 0, None)
                with act.Fori(0, T // 2 - 1) as i:
                    tile(2 * i + 1, 1, 2 * i)
                    tile(2 * i + 2, 0, 2 * i + 1)
                tile(T - 1, 1, T - 2)
                tile(None, None, T - 1)

            act.sem_inc(S_("xa_ptev"), 2)
            layernorm(0)
            end_phase(act, 4)
            xattn(0)
            end_phase(act, 4)
            layernorm(1)
            act.wait_ge(ld["scan"], 16 * 7)
            act.activation(amin[:], alog[:], ACT.Exp).then_inc(S_("sc_a"), 1)
            act.wait_ge(S_("sc_a"), 1)
            act.mul(amin[:], amin[:], -1.0).then_inc(S_("sc_a"), 1)
            for c in range(CH):
                act.wait_ge(S_("sc_dp"), c + 1)
                act.activation(tmp[c], ps(c % 2), ACT.Abs, bias=bx[:, 0:1]).then_inc(S_("sc_t"), 1)
                act.wait_ge(S_("sc_t"), 2 * c + 1)
                act.activation(tmp[c], tmp[c], ACT.Exp, scale=-1.0).then_inc(S_("sc_t"), 1)
                act.wait_ge(S_("sc_t"), 2 * c + 2)
                act.activation(tmp[c], tmp[c], ACT.Ln, bias=onec[:, 0:1]).then_inc(S_("sc_ln"), 1)
            act.wait_ge(S_("sc_delta"), CH)
            act.wait_ge(S_("sc_a"), 2)
            for n in range(NS):
                if n >= 2:
                    act.wait_ge(S_("sc_h"), 4 * (n - 1))
                act.activation(abar[n % 2], delta, ACT.Exp, scale=amin[:, n:n + 1]).then_inc(S_("sc_abar0"), 1)
            for c in range(CH):
                act.wait_ge(S_("sc_acc"), 4 * (NS - 1) + c + 1)
                act.copy(yT[:, CW * c:CW * c + CW], ps(4 + c)).then_inc(S_("sc_yT"), 1)
            end_phase(act, 4)
            layernorm(2)
            act.wait_ge(S_("me_lsub"), 1)
            act.activation(gate[:], lg[:], ACT.Exp).then_inc(S_("me_exp"), 1)
            end_phase(act, 4)
            layernorm(3)
            xattn(1)
            end_phase(act, 4)

            def attend(k):
                act.wait_ge(S_("at_sub"), k + 1)
                act.activation(sc, sc, ACT.Exp).then_inc(S_("at_exp"), 1)
                for c in range(CH):
                    act.wait_ge(S_("at_pt"), CH * k + c + 1)
                    act.copy(pdT[:, CT * c:CT * c + CT, :], ps(2 + c).rearrange("p (a b) -> p a b", b=P)).then_inc(S_("at_ptev"), 1)

            layernorm(4)
            for n in range(2 * CH):
                c, w = divmod(n, 2)
                act.wait_ge(S_("sa_q"), n + 1)
                act.copy((qT, kT)[w][:, CW * c:CW * c + CW], ps(n % 2)).then_inc(S_("sa_qk"), 1)
            attend(0)
            end_phase(act, 4)
            layernorm(5)
            for c in range(CH):
                for w in range(3):
                    g2 = 3 * c + w
                    for k in range(0, NB, 2):
                        n = NB * g2 + k
                        act.wait_ge(S_("lf_pre"), n + 1)
                        if g2 >= 2:
                            act.wait_ge(S_("lf_o"), g2 - 1)
                        act.activation(hT[g2 % 2][:, k, :], ps(n % 4), ACT.Relu, bias=b1[:, w, k:k + 1]).then_inc(S_("lf_h0"), 1)
            end_phase(act, 4)
            attend(1)
            end_phase(act, 4)


def kernel(**inputs):
    import concourse.bacc as bacc
    from concourse.bass_utils import run_bass_kernel_spmd as run

    def a(name):
        return np.asarray(inputs[name])

    T, B, D = 16, 32, 128
    w = {}
    w["x"] = a("x").reshape(T, 128, D).transpose(1, 0, 2)
    w["ctxT"] = a("ctx_768").transpose(2, 0, 1).reshape(96, -1)
    w["ctx"] = a("ctx_768").transpose(1, 0, 2)
    w["mask"] = a("mask_BxS2_bf1").reshape(1, -1).view(np.uint8)

    def blocks(m, rows=128):
        return m.reshape(-1, rows, m.shape[-1]).transpose(1, 0, 2)

    w["l0_wqT"] = blocks(a("L0_xattn_Wq").T, 64)
    w["l0_wkT"] = blocks(a("L0_xattn_Wk").T, 64)
    w["l0_wvT"] = blocks(a("L0_xattn_Wv").T, 64)
    w["l0_wo"] = blocks(a("L0_xattn_Wo"), 64)
    w["l0_bo"] = a("L0_xattn_bo").reshape(1, D)
    w["wx"] = a("L0_attn_W_xproj")
    w["bx_d"] = a("L0_attn_b_xproj")[:D].reshape(D, 1)
    w["bx_bc"] = a("L0_attn_b_xproj")[D:].reshape(32, 1)
    w["wout"] = a("L0_attn_W_out")
    w["bout"] = a("L0_attn_b_out").reshape(1, D)
    w["alog"] = a("L0_attn_A_log")
    w["dp"] = a("L0_attn_Dp").reshape(D, 1)
    w["wrT"] = a("L0_ffn_Wr").T
    w["aT"] = a("L0_ffn_A").reshape(512, D).T.reshape(D, 4, 128)
    w["bw"] = blocks(a("L0_ffn_Bw").transpose(0, 2, 1).reshape(512, D))
    w["l1_wqT"] = a("L1_xattn_Wq").T
    w["l1_wkT"] = a("L1_xattn_Wk").T
    w["l1_wvT"] = a("L1_xattn_Wv").T
    w["l1_wo"] = a("L1_xattn_Wo")
    w["wqkv"] = a("L1_attn_W")
    for n in "qkv":
        p = f"L1_ffn_{n}_"
        w[n + "_nw"] = a(p + "node_w").T
        w[n + "_nb"] = a(p + "node_b").reshape(1, -1)
        w[n + "_w1"] = a(p + "w1").transpose(1, 0, 2).reshape(D, -1)
        w[n + "_b1"] = a(p + "b1").reshape(8, 128).T
        w[n + "_w2"] = blocks(a(p + "w2").reshape(1024, D))
        w[n + "_b2"] = a(p + "b2")
    nc = bacc.Bacc("TRN2", target_bir_lowering=False, num_devices=1)
    arrays, aps = {}, {}
    for name, m in w.items():
        arrays["in_" + name] = m = np.ascontiguousarray(m)
        aps[name] = nc.dram_tensor("in_" + name, m.shape, mybir.dt.from_np(m.dtype), kind="ExternalInput").ap()
    out = nc.dram_tensor("out_0", (128, T, D), F32, kind="ExternalOutput").ap()
    build(nc, aps, out)
    r = run(nc, [arrays], core_ids=[0])
    return r.results[0]["out_0"].transpose(1, 0, 2).reshape(B, 64, D)
```

```python
from contextlib import ExitStack

import numpy as np

import concourse.bass as bass
from concourse import mybir

F32 = mybir.dt.float32
BF16 = mybir.dt.bfloat16
U8 = mybir.dt.uint8
ALU = mybir.AluOpType
ACT = mybir.ActivationFunctionType
AX = mybir.AxisListType

P = 128
EPS = 1e-5
BIG = 1e30
MASK_NEG = -9000000000000000.0


def wait(eng, sem, value):
    if isinstance(value, int) and value <= 0:
        return
    eng.wait_ge(sem, value)


def build(nc, A, out):
    B, S, D = 32, 64, 128
    KEYS, CD = 128, 96
    H = 16
    T = B * S // P
    CH = 4
    CT = T // CH
    CW = CT * P
    NS = 16
    E, R = 8, 64
    LV, LW = 16, 64
    NB = LV * LW // P
    NN = 15
    XA_SCALE = (64 ** -0.5, 8 ** -0.5)
    D_SCALE = float(D) ** -0.5

    with ExitStack() as ctx:
        def sb(name, shape, dt=F32):
            return ctx.enter_context(nc.sbuf_tensor(name, shape, dt))

        def sem(name):
            return ctx.enter_context(nc.semaphore(name))

        bank = [ctx.enter_context(nc.psum_tensor(f"bank{n}", [P, 1024], F32)) for n in range(4)]

        def ps(n):
            return bank[n // 2][:, 512 * (n % 2):512 * (n % 2) + 512]

        x = sb("x_sb", [P, T, D])
        xnT = sb("xnT", [P, T * P])
        ident = sb("ident", [P, P])
        ones = sb("ones", [1, P])
        st6 = sb("st6", [P, T, 6])
        mean = sb("mean", [P, T])
        lnv = sb("lnv", [P, 3, T])
        rstd = sb("rstd", [P, T])
        std = sb("std", [P, T])
        xn = sb("xn", [P, 2, CT, D])
        epsc = sb("epsc", [P, 1])
        onec = sb("onec", [P, 1])
        rows = sb("rows", [1, 3 * P])
        ctxT = sb("ctxT", [CD, B * KEYS])
        cx = sb("cx", [P, 4, CD])
        M = sb("M", [P, H, CD])
        N = sb("N", [CD, H, P])
        hmask = sb("hmask", [P, H])
        pool = sb("pool", [P, 17920])

        def at(o, shape, parts=P, dt=F32):
            n = int(np.prod(shape))
            words = n * (2 if dt is BF16 else 4) // 4
            v = pool[0:parts, o:o + words]
            if dt is not F32:
                v = v.bitcast(dt)
            if len(shape) == 2:
                v = v.rearrange("p (a b) -> p a b", b=shape[1])
            elif len(shape) == 3:
                v = v.rearrange("p (a b c) -> p a b c", b=shape[1], c=shape[2])
            return v

        qmT = [at(2048 * n, (2, H, S)) for n in range(2)]
        OT = [at(4096 + 2048 * n, (H, P), CD) for n in range(2)]
        prob = [at(8192 + 1024 * n, (8, KEYS)) for n in range(2)]
        PT = [at(10240 + 1024 * n, (8, P)) for n in range(2)]
        nmx = sb("nmx", [P, 2, 8])
        sm = sb("sm", [P, 2, 8])
        rs = sb("rs", [P, 2, 8])
        wq1 = sb("wq1", [P, P])
        wk1 = sb("wk1", [CD, P])
        wv1 = sb("wv1", [CD, P])
        wo1 = sb("wo1", [P, P])
        gmask = sb("gmask", [P, 4])
        onesb = sb("onesb", [1, P], BF16)
        Om = [at(4096 + 512 * n, (4, P)) for n in range(2)]
        mrow = at(5120, (B * KEYS,), 1, BF16)
        msk8 = pool[0:1, 7168:7168 + B * KEYS // 4].bitcast(U8)
        kTx = at(12288, (B * KEYS,))
        vs = at(16384, (2, P))
        cxT = at(16640, (4, KEYS), CD)
        wqT = at(8192, (H, P), 64)
        wkT = at(10240, (H, CD), 64)
        wvT = at(11776, (H, CD), 64)
        wo = at(13312, (H, P), 64)

        wx = sb("wx", [P, 160])
        wout = sb("wout", [P, P])
        bx = sb("bx", [P, 1])
        bbc = sb("bbc", [32, 1])
        alog = sb("alog", [P, NS])
        amin = sb("amin", [P, NS])
        dp = sb("dp", [P, 1])
        ddp = sb("ddp", [P, P])
        delta = at(0, (2048,))
        du = at(2048, (2048,))
        abar = [at(4096 + 2048 * n, (2048,)) for n in range(2)]
        bxs = [at(8192 + 512 * n, (512,)) for n in range(2)]
        hs = [at(9216 + 512 * n, (512,)) for n in range(2)]
        hc = [at(10240 + 512 * n, (512,)) for n in range(2)]
        tmp = [at(11264 + 512 * n, (512,)) for n in range(4)]
        yT = at(13312, (2048,))
        bcs = at(15360, (2048,), 96, BF16)
        bcf = at(16384, (512,), 32)
        bcr = at(16896, (512,), 32)
        bselb = sb("bselb", [96, 32, P], BF16)

        wrT = sb("wrT", [P, E])
        aT = at(0, (E * R // P, P))
        bw = at(512, (E * R // P, D))
        midT = [at(1024 + 2048 * n, (4, CW)) for n in range(2)]
        lg = sb("lg", [B, E])
        gt = sb("gt", [B, E, E])
        eq = sb("eq", [B, E, E])
        tri = sb("tri", [B, E, E])
        rank = sb("rank", [B, E])
        lmx = sb("lmx", [B, 2])
        gate = sb("gate", [B, E])
        gT = sb("gT", [E, B])
        esel = sb("esel", [E, 4, P])
        gx = sb("gx", [P, 4, B])

        wqkv = at(0, (384,))
        qT = at(1024, (2048,))
        kT = at(3072, (2048,))
        v = at(5120, (T, D))
        sc = at(7168, (T, S))
        pd = at(8192, (T, P))
        pdT = at(10240, (T, P))
        keep = at(12288, (S,))
        eqz = at(12352, (T, S))
        amx = sb("amx", [P, T])
        asm = sb("asm", [P, T])
        ars = sb("ars", [P, T])

        w1 = sb("w1", [P, 3, LV * LW])
        w2 = sb("w2", [P, 3, NB, D])
        b1 = sb("b1", [P, 3, NB])
        b2 = sb("b2", [96, D])
        nw = sb("nw", [P, 3 * NN])
        nb = sb("nb", [1, 3 * NN])
        hT = [at(7168 + 4096 * n, (NB, CW)) for n in range(2)]
        dec = at(15360, (T, 3, NN))
        selt = sb("selt", [P, T, 3, 32])
        lvl = at(16128, (T * 3, 8))
        selT = sb("selT", [96, T * P])
        seln = at(16512, (T * P,), 96, BF16)
        lselb = sb("lselb", [96, NB, P], BF16)

        s_phase = sem("phase_done")
        ld = {n: sem("ld_" + n) for n in ("x", "w0", "ctx", "msk", "w1", "scan", "moe", "l1x", "wqkv", "tree")}
        cx_in = [sem(f"cx_in{n}") for n in range(4)]
        s_out = sem("out_written")
        names = {}

        def S_(name):
            if name not in names:
                names[name] = sem(name)
            return names[name]

        phases = [0] * 5

        def end_phase(eng, k):
            phases[k] += 1
            eng.drain().then_inc(s_phase, 1)
            eng.wait_ge(s_phase, 5 * phases[k])

        block = ctx.enter_context(nc.Block())

        @block.sync
        def _(sp):
            sp.dma_start(x[:], A["x"]).then_inc(ld["x"], 16)
            for t, n in ((wqT, "l0_wqT"), (wkT, "l0_wkT"), (wvT, "l0_wvT"), (wo, "l0_wo"), (rows[:, 0:P], "l0_bo")):
                sp.dma_start(t, A[n]).then_inc(ld["w0"], 16)
            sp.dma_start(ctxT[0:CD, :], A["ctxT"]).then_inc(ld["ctx"], 16)
            for t, n in ((wx[:], "wx"), (wout[:], "wout"), (bx[:], "bx_d"), (bbc[:], "bx_bc"), (alog[:], "alog"),
                         (dp[:], "dp"), (rows[:, P:2 * P], "bout")):
                sp.dma_start(t, A[n]).then_inc(ld["scan"], 16)
            sp.dma_start(wrT[:], A["wrT"]).then_inc(ld["moe"], 16)
            for t, n in ((wq1, "l1_wq"), (wk1, "l1_wk"), (wv1, "l1_wv"), (wo1, "l1_wo")):
                sp.dma_start(t[:], A[n]).then_inc(ld["l1x"], 16)
            for n, name in enumerate("qkv"):
                sp.dma_start(w1[:, n, :], A[name + "_w1"]).then_inc(ld["tree"], 16)
                sp.dma_start(w2[:, n], A[name + "_w2"]).then_inc(ld["tree"], 16)
                sp.dma_start(b1[:, n], A[name + "_b1"]).then_inc(ld["tree"], 16)
                sp.dma_start(b2[32 * n:32 * n + LV, :], A[name + "_b2"]).then_inc(ld["tree"], 16)
                sp.dma_start(nw[:, NN * n:NN * n + NN], A[name + "_nw"]).then_inc(ld["tree"], 16)
                sp.dma_start(nb[:, NN * n:NN * n + NN], A[name + "_nb"]).then_inc(ld["tree"], 16)

            def contexts(layer):
                uses, first = ((2, 4), (1, 0))[layer]

                def load(b, n):
                    if layer == 0:
                        src = A["ctx"][:, bass.ds(b, 1), :].rearrange("p a c -> p (a c)")
                        sp.dma_start(cx[:, n, :], src).then_inc(cx_in[n], 16)
                    else:
                        sp.dma_start(cxT[:, n, :], A["ctxT"][:, bass.ds(b * KEYS, KEYS)]).then_inc(cx_in[n], 16)

                for n in range(4):
                    load(n, n)
                with sp.Fori(0, B // 4 - 1) as i:
                    for n in range(4):
                        sp.wait_ge(S_("xa_o0" if layer == 0 else "xa_v1"), uses * (4 * i + n + 1) + first)
                        load(4 * i + 4 + n, n)

            end_phase(sp, 0)
            contexts(0)
            for k in range(2):
                end_phase(sp, 0)
            sp.dma_start(aT, A["aT"]).then_inc(ld["moe"], 16)
            sp.dma_start(bw, A["bw"]).then_inc(ld["moe"], 16)
            end_phase(sp, 0)
            sp.dma_start(msk8, A["mask"]).then_inc(ld["msk"], 16)
            contexts(1)
            end_phase(sp, 0)
            sp.dma_start(wqkv, A["wqkv"]).then_inc(ld["wqkv"], 16)
            end_phase(sp, 0)
            end_phase(sp, 0)
            end_phase(sp, 0)
            sp.dma_start(out, x[:]).then_inc(s_out, 16)
            sp.wait_ge(s_out, 16)

        @block.gpsimd
        def _(g):
            g.memset(ident[:], 0.0).then_inc(S_("g0"), 1)
            g.memset(hmask[:], 1.0).then_inc(S_("g0"), 1)
            g.memset(bselb[:], 0.0).then_inc(S_("g0"), 1)
            g.memset(tri[:], 0.0).then_inc(S_("g0"), 1)
            g.memset(esel[:], 1.0).then_inc(S_("g0"), 1)
            g.memset(lselb[:], 0.0).then_inc(S_("g0"), 1)
            g.memset(ones[:], 1.0).then_inc(S_("g0"), 1)
            g.memset(epsc[:], EPS).then_inc(S_("g0"), 1)
            g.memset(onec[:], 1.0).then_inc(S_("g0"), 1)
            g.memset(selt[:], 0.0).then_inc(S_("g0"), 1)
            g.memset(onesb[:], 1.0).then_inc(S_("g0"), 1)
            g.wait_ge(S_("g0"), 11)
            g.affine_select(out=ident[:], in_=ident[:], compare_op=ALU.not_equal, fill=1.0, base=0,
                            pattern=[[-1, P]], channel_multiplier=1).then_inc(S_("consts"), 1)
            g.affine_select(out=hmask[:], in_=hmask[:], compare_op=ALU.is_ge, fill=0.0, base=0,
                            pattern=[[-8, H]], channel_multiplier=1).then_inc(S_("g1"), 1)
            g.wait_ge(S_("g1"), 1)
            g.affine_select(out=hmask[:], in_=hmask[:], compare_op=ALU.is_ge, fill=0.0, base=7,
                            pattern=[[8, H]], channel_multiplier=-1).then_inc(S_("consts"), 1)
            for part in range(3):
                g.affine_select(out=bselb[:], in_=bselb[:], compare_op=ALU.not_equal, fill=1.0, base=-32 * part,
                                pattern=[[-1, 32], [0, P]], channel_multiplier=1).then_inc(S_("g1"), 1)
                g.wait_ge(S_("g1"), 2 + part)
            g.affine_select(out=tri[:], in_=tri[:], compare_op=ALU.is_ge, fill=1.0, base=0,
                            pattern=[[-1, E], [1, E]], channel_multiplier=0).then_inc(S_("g1"), 1)
            g.affine_select(out=esel[:], in_=esel[:], compare_op=ALU.is_ge, fill=0.0, base=0,
                            pattern=[[P, 4], [1, P]], channel_multiplier=-R).then_inc(S_("g1"), 1)
            g.wait_ge(S_("g1"), 6)
            g.affine_select(out=esel[:], in_=esel[:], compare_op=ALU.is_ge, fill=0.0, base=R - 1,
                            pattern=[[-P, 4], [-1, P]], channel_multiplier=R).then_inc(S_("g1"), 1)
            ls = lselb[:].rearrange("p k (u m) -> p k u m", u=2)
            for n in range(3):
                g.affine_select(out=ls, in_=ls, compare_op=ALU.not_equal, fill=1.0, base=-32 * n,
                                pattern=[[-2, NB], [-1, 2], [0, LW]], channel_multiplier=1).then_inc(S_("g1"), 1)
                g.wait_ge(S_("g1"), 8 + n)

            def normalise(layer):
                recip, done = S_(f"xa_recip{layer}"), S_(f"xa_prob{layer}")
                g.sem_inc(done, 2)
                with g.Fori(0, T) as t:
                    for u in range(2):
                        g.wait_ge(recip, 2 * t + u + 1)
                        g.tensor_tensor(prob[u], prob[u], rs[:, u, :, None].broadcast_to([P, 8, KEYS]),
                                        ALU.mult).then_inc(done, 1)

            end_phase(g, 1)
            normalise(0)
            end_phase(g, 1)
            for n in range(NS):
                g.wait_ge(S_("sc_abar0"), n + 1)
                g.memset(abar[n % 2][:, 0:2048:S], 0.0).then_inc(S_("sc_abar"), 1)
            end_phase(g, 1)
            end_phase(g, 1)
            normalise(1)
            end_phase(g, 1)
            g.memset(pd, 0.0).then_inc(S_("pd_zero"), 1)
            g.memset(keep, 1.0).then_inc(S_("g3"), 1)
            g.wait_ge(S_("g3"), 1)
            for u in range(2):
                ku = keep[64 * u:64 * u + 64, :]
                g.affine_select(out=ku, in_=ku, compare_op=ALU.is_ge, fill=0.0, base=0,
                                pattern=[[1, S]], channel_multiplier=-1).then_inc(S_("keep"), 1)
            end_phase(g, 1)
            end_phase(g, 1)
            end_phase(g, 1)

        @block.tensor
        def _(pe):
            def norm_transposes(k):
                if k == 0:
                    pe.wait_ge(S_("consts"), 1)
                with pe.Fori(0, CH // 2) as i:
                    for u in range(2):
                        pe.wait_ge(S_("ln_ev"), CH * k + 2 * i + u + 1)
                        for m in range(CT):
                            pe.wait_ge(S_("ln_xn"), T * k + CT * (2 * i + u) + m + 1)
                            tr = pe.transpose(ps(u)[:, P * m:P * m + P], xn[:, u, m, :], ident[:])
                        tr.then_inc(S_("ln_tr"), 1)

            def turns(layer, tb, u, hh):
                if tb is None:
                    return
                b = 2 * tb + u
                if hh == 0:
                    pe.wait_ge(S_(f"xa_prob{layer}"), b + 3)
                pe.wait_ge(S_(f"xa_ptev{layer}"), 2 * b + hh + 1)
                for j in range(4):
                    mm = pe.transpose(ps(4)[:, P * j:P * j + P], prob[u][:, 4 * hh + j, :], ident[:])
                mm.then_inc(S_(f"xa_pt{layer}"), 1)

            def xattn0():
                pe.wait_ge(ld["w0"], 16 * 5)
                for c in range(4):
                    for h in range(4 * c, 4 * c + 4):
                        mm = pe.matmul(ps(c)[:, CD * (h % 4):CD * (h % 4) + CD], wqT[:, h, :], wkT[:, h, :],
                                       start=True, stop=True)
                    mm.then_inc(S_("xa_m"), 1)
                    for h in range(4 * c, 4 * c + 4):
                        mm = pe.matmul(ps(4 + c)[0:CD, P * (h % 4):P * (h % 4) + P], wvT[:, h, :], wo[:, h, :],
                                       start=True, stop=True)
                    mm.then_inc(S_("xa_n"), 1)
                pe.wait_ge(ld["ctx"], 16)
                pe.wait_ge(S_("xa_w"), 8)
                pe.sem_inc(S_("xa_y0"), 2)
                pe.sem_inc(S_("xa_o0"), 4)
                q_out, sc_free = S_("xa_qev0"), S_("xa_exp0")

                def body(tq, ta, tb, f):
                    def queries(c):
                        if tq is None:
                            return
                        wait(pe, q_out, 4 * tq + c)
                        for h in range(4):
                            mm = pe.matmul(ps(6)[0:CD, P * h:P * h + P], M[:, 4 * c + h, :],
                                           xnT[:, bass.ds(tq * P, P)], start=True, stop=True)
                        mm.then_inc(S_("xa_q0"), 1)

                    def scores(u, hh):
                        if ta is None:
                            return
                        if hh == 0:
                            pe.wait_ge(q_out, 4 * ta + 4)
                            pe.wait_ge(sc_free, 2 * ta + u + 1)
                        kv = ctxT[:, bass.ds((2 * ta + u) * KEYS, KEYS)]
                        for j in range(4 * hh, 4 * hh + 4):
                            mm = pe.matmul(bank[u][:, P * j:P * j + P],
                                           qmT[f][0:CD, u, 2 * j:2 * j + 2, :].rearrange("p a b -> p (a b)"), kv,
                                           start=True, stop=True)
                        if hh == 1:
                            mm.then_inc(S_("xa_sc0"), 1)

                    def values(u, hh):
                        if tb is None:
                            return
                        b = 2 * tb + u
                        slot = 2 * (1 - f) + u
                        if hh == 0:
                            pe.wait_ge(cx_in[slot], 16 * group[0] + 16)
                        pe.wait_ge(S_("xa_ptev0"), 2 * b + hh + 2)
                        pe.wait_ge(S_("xa_oev0"), 2 * b + hh + 1)
                        pe.matmul(ps(5)[0:CD, :], cx[:, slot, :], PT[u][:, 4 * hh:4 * hh + 4, :],
                                  start=True, stop=True).then_inc(S_("xa_o0"), 1)

                    def project():
                        if tb is None:
                            return
                        pe.wait_ge(S_("xa_add0"), tb + 1)
                        pe.wait_ge(S_("xa_oev0"), 4 * tb + 4)
                        pe.matmul(ps(7)[:, 0:P], ones[:], rows[:, 0:P], start=True, stop=False)
                        for h in range(H):
                            if h == H // 2:
                                pe.wait_ge(S_("xa_oev0"), 4 * tb + 5)
                            mm = pe.matmul(ps(7)[:, 0:P], OT[1 - f][:, h, :], N[:, h, :], start=False, stop=(h == H - 1))
                        mm.then_inc(S_("xa_y0"), 1)

                    for u in range(2):
                        turns(0, tb, u, 0)
                        queries(2 * u)
                        scores(u, 0)
                        turns(0, tb, u, 1)
                        scores(u, 1)
                        values(u, 0)
                        queries(2 * u + 1)
                        values(u, 1)
                    project()

                group = [0]
                body(0, None, None, 1)
                body(1, 0, None, 0)
                with pe.Fori(0, T // 2 - 1) as i:
                    group[0] = i
                    body(2 * i + 2, 2 * i + 1, 2 * i, 1)
                    body(2 * i + 3, 2 * i + 2, 2 * i + 1, 0)
                group[0] = T // 2 - 1
                body(None, T - 1, T - 2, 1)
                body(None, None, T - 1, 0)

            def xattn1():
                pe.wait_ge(ld["l1x"], 16 * 4)
                for c in range(8):
                    if c >= 2:
                        pe.wait_ge(S_("xa_kev"), c - 1)
                    pe.matmul(ps(6 + c % 2), wk1[:], ctxT[:, CW * c:CW * c + CW], start=True, stop=True).then_inc(S_("xa_k"), 1)
                pe.wait_ge(S_("xa_kev"), 8)
                pe.wait_ge(S_("xa_mask"), 1)
                pe.sem_inc(S_("xa_y1"), 2)
                pe.sem_inc(S_("xa_o1"), 2)
                group = [0]

                def body(tq, ta, tb, f):
                    def queries():
                        if tq is None:
                            return
                        wait(pe, S_("xa_qev1"), tq)
                        pe.matmul(ps(6)[:, 0:P], wq1[:], xnT[:, bass.ds(tq * P, P)], start=True, stop=True).then_inc(S_("xa_q1"), 1)

                    def scores(u, hh):
                        if ta is None:
                            return
                        if hh == 0:
                            pe.wait_ge(S_("xa_qev1"), ta + 1)
                            pe.wait_ge(S_("xa_exp1"), 2 * ta + u + 1)
                        off = (2 * ta + u) * KEYS
                        for j in range(4 * hh, 4 * hh + 4):
                            rows_j = bank[u][:, P * j:P * j + P]
                            pe.matmul(rows_j, onesb[:], mrow[:, bass.ds(off, KEYS)], start=True, stop=False)
                            mm = pe.matmul(rows_j, qmT[f][:, u, 2 * j:2 * j + 2, :].rearrange("p a b -> p (a b)"),
                                           kTx[:, bass.ds(off, KEYS)], start=False, stop=True)
                        if hh == 1:
                            mm.then_inc(S_("xa_sc1"), 1)

                    def project_values(u):
                        if tb is None:
                            return
                        slot = 2 * (1 - f) + u
                        pe.wait_ge(cx_in[slot], 16 * (B // 4) + 16 * group[0] + 16)
                        pe.wait_ge(S_("xa_oev1"), 2 * tb + u + 1)
                        pe.matmul(ps(5)[:, 0:P], cxT[:, slot, :], wv1[:], start=True, stop=True).then_inc(S_("xa_v1"), 1)

                    def values(u):
                        if tb is None:
                            return
                        b = 2 * tb + u
                        pe.wait_ge(S_("xa_vev1"), b + 1)
                        pe.wait_ge(S_("xa_ptev1"), 2 * b + 3)
                        for g in range(4):
                            mm = pe.matmul(ps(5)[32 * g:32 * g + 32, 0:4 * S], vs[:, u, 32 * g:32 * g + 32],
                                           PT[u][:, 2 * g:2 * g + 2, :], start=True, stop=True)
                        mm.then_inc(S_("xa_o1"), 1)

                    def project():
                        if tb is None:
                            return
                        pe.wait_ge(S_("xa_add1"), tb + 1)
                        pe.wait_ge(S_("xa_oev1"), 2 * tb + 3)
                        for m in range(4):
                            mm = pe.matmul(ps(7)[:, 0:P], Om[1 - f][:, m, :], wo1[:], start=(m == 0), stop=(m == 3))
                        mm.then_inc(S_("xa_y1"), 1)

                    for u in range(2):
                        turns(1, tb, u, 0)
                        if u == 0:
                            queries()
                        project_values(u)
                        scores(u, 0)
                        turns(1, tb, u, 1)
                        scores(u, 1)
                        values(u)
                    project()

                body(0, None, None, 1)
                body(1, 0, None, 0)
                with pe.Fori(0, T // 2 - 1) as i:
                    group[0] = i
                    body(2 * i + 2, 2 * i + 1, 2 * i, 1)
                    body(2 * i + 3, 2 * i + 2, 2 * i + 1, 0)
                group[0] = T // 2 - 1
                body(None, T - 1, T - 2, 1)
                body(None, None, T - 1, 0)

            norm_transposes(0)
            end_phase(pe, 2)
            xattn0()
            end_phase(pe, 2)
            norm_transposes(1)
            pe.wait_ge(ld["scan"], 16 * 7)
            pe.wait_ge(S_("ln_ev"), 2 * CH + 2)
            pe.wait_ge(S_("ddp"), 1)
            for c in range(CH):
                xc = xnT[:, CW * c:CW * c + CW]
                if c >= 2:
                    pe.wait_ge(S_("sc_d0"), c - 1)
                pe.matmul(ps(c % 2), wx[:, 0:D], xc, start=True, stop=True).then_inc(S_("sc_dp"), 1)
                if c >= 2:
                    pe.wait_ge(S_("sc_bcf"), c - 1)
                pe.matmul(ps(2 + c % 2)[0:32, :], wx[:, D:D + 32], xc, start=True, stop=True).then_inc(S_("sc_bc"), 1)
                pe.matmul(ps(4 + c), ddp[:], xc, start=True, stop=False)
            pe.wait_ge(S_("sc_split"), CH)
            pe.wait_ge(S_("g1"), 10)
            pe.wait_ge(S_("sc_delta"), CH)

            for k in range(4 * NS):
                n, c = divmod(k, 4)
                if k >= 2:
                    pe.wait_ge(S_("sc_bx"), k - 1)
                pe.matmul(ps(k % 2), bselb[:, n, :], bcs[:, CW * c:CW * c + CW], start=True, stop=True).then_inc(S_("sc_b"), 1)
                if k >= 2:
                    pe.wait_ge(S_("sc_hc"), k - 1)
                pe.matmul(ps(2 + k % 2), bselb[:, 16 + n, :], bcs[:, CW * c:CW * c + CW], start=True, stop=True).then_inc(S_("sc_c"), 1)
                if k >= 2:
                    pe.matmul(ps(4 + (k - 2) % 4), ident[:], hc[k % 2], start=False, stop=(k - 2) // 4 == NS - 1).then_inc(S_("sc_acc"), 1)
            for k in range(4 * NS, 4 * NS + 2):
                pe.wait_ge(S_("sc_hc"), k - 1)
                pe.matmul(ps(4 + (k - 2) % 4), ident[:], hc[k % 2], start=False, stop=True).then_inc(S_("sc_acc"), 1)
            for c in range(CH):
                pe.wait_ge(S_("sc_yT"), c + 1)
                for t in range(CT * c, CT * c + CT):
                    o = ps(c)[:, P * (t % CT):P * (t % CT) + P]
                    pe.matmul(o, ones[:], rows[:, P:2 * P], start=True, stop=False)
                    mm = pe.matmul(o, yT[:, P * t:P * t + P], wout[:], start=False, stop=True)
                mm.then_inc(S_("sc_out"), 1)
            end_phase(pe, 2)
            norm_transposes(2)
            pe.wait_ge(S_("ln_ev"), 3 * CH + 2)
            pe.wait_ge(ld["moe"], 48)
            pe.matmul(ps(7)[0:B, 0:E], xnT[:, 0:2048:S], wrT[:], start=True, stop=True).then_inc(S_("me_lg"), 1)
            pe.wait_ge(S_("me_gate"), 1)
            pe.transpose(ps(7)[0:E, 64:64 + B], gate[:], ident[0:B, 0:B]).then_inc(S_("me_gT"), 1)
            pe.wait_ge(S_("me_gTs"), 1)
            for k in range(4):
                mm = pe.matmul(ps(7)[:, 128 + B * k:128 + B * k + B], esel[:, k, :], gT[:], start=True, stop=True)
            mm.then_inc(S_("me_gx"), 1)
            for c in range(CH):
                for k in range(4):
                    n = 4 * c + k
                    if n >= 2:
                        pe.wait_ge(S_("me_mev"), n - 1)
                    pe.matmul(ps(n % 2), aT[:, k, :], xnT[:, CW * c:CW * c + CW], start=True, stop=True).then_inc(S_("me_m"), 1)
                pe.wait_ge(S_("me_mev"), 4 * c + 4)
                for t in range(CT):
                    o = ps(2 + c)[:, P * t:P * t + P]
                    pe.matmul(o, xnT[:, CW * c + P * t:CW * c + P * t + P], ident[:], start=True, stop=False)
                    for k in range(4):
                        mm = pe.matmul(o, midT[c % 2][:, k, P * t:P * t + P], bw[:, k, :], start=False, stop=(k == 3))
                mm.then_inc(S_("me_y"), 1)
            end_phase(pe, 2)
            norm_transposes(3)
            pe.wait_ge(S_("ln_ev"), 4 * CH + 2)
            xattn1()
            end_phase(pe, 2)

            def attend(k):
                for b in range(B):
                    t, u = divmod(b, 2)
                    mm = pe.matmul(ps(t // 8)[64 * u:64 * u + 64, S * (t % 8):S * (t % 8) + S], qT[:, S * b:S * b + S],
                                   kT[:, S * b:S * b + S], start=True, stop=True)
                mm.then_inc(S_("at_sc"), 1)
                pe.wait_ge(S_("at_p"), 2 * k + 2)
                for c in range(CH):
                    for t in range(CT):
                        mm = pe.transpose(ps(2 + c)[:, P * t:P * t + P], pd[:, CT * c + t, :], ident[:])
                    mm.then_inc(S_("at_pt"), 1)
                for c in range(CH):
                    pe.wait_ge(S_("at_ptev"), CH * k + c + 1)
                    if c >= 2:
                        pe.wait_ge(S_("at_add"), CH * k + c - 1)
                    for t in range(CT):
                        mm = pe.matmul(ps(6 + c % 2)[:, P * t:P * t + P], pdT[:, CT * c + t, :], v[:, CT * c + t, :],
                                       start=True, stop=True)
                    mm.then_inc(S_("at_y"), 1)

            norm_transposes(4)
            pe.wait_ge(S_("ln_ev"), 5 * CH + 2)
            pe.wait_ge(ld["wqkv"], 16)
            for c in range(CH):
                for w in range(2):
                    n = 2 * c + w
                    if n >= 2:
                        pe.wait_ge(S_("sa_qk"), n - 1)
                    pe.matmul(ps(n % 2), wqkv[:, D * w:D * w + D], xnT[:, CW * c:CW * c + CW], start=True,
                              stop=True).then_inc(S_("sa_q"), 1)
            for c in range(CH):
                for t in range(CT):
                    mm = pe.matmul(ps(2 + c)[:, P * t:P * t + P], xnT[:, CW * c + P * t:CW * c + P * t + P],
                                   wqkv[:, 2 * D:3 * D], start=True, stop=True)
                mm.then_inc(S_("sa_v"), 1)
            pe.wait_ge(S_("sa_qk"), 8)
            pe.wait_ge(S_("sa_vev"), 4)
            attend(0)
            end_phase(pe, 2)
            norm_transposes(5)
            pe.wait_ge(S_("ln_ev"), 6 * CH + 2)
            pe.wait_ge(ld["tree"], 16 * 18)
            for t in range(T):
                o = ps(2 + t // 8)[:, 48 * (t % 8):48 * (t % 8) + 3 * NN]
                pe.matmul(o, ones[:], nb[:], start=True, stop=False)
                mm = pe.matmul(o, xnT[:, P * t:P * t + P], nw[:], start=False, stop=True)
            mm.then_inc(S_("tr_sc"), 1)
            pe.wait_ge(S_("tr_sel"), 1)
            for c in range(CH):
                for t in range(CT):
                    mm = pe.transpose(ps(4 + c)[0:96, P * t:P * t + P],
                                      selt[:, CT * c + t].rearrange("p a b -> p (a b)"), ident[:])
                mm.then_inc(S_("tr_st"), 1)
            pe.wait_ge(S_("tr_selT"), 2 * CH)
            def hidden(g2):
                c, w = divmod(g2, 3)
                r = slice(32 * w, 32 * w + LV)
                for k in range(NB):
                    n = NB * g2 + k
                    if n >= 4:
                        pe.wait_ge(S_("lf_h0" if n % 2 == 0 else "lf_h1"), (n - 4) // 2 + 1)
                    pe.matmul(ps(n % 4), lselb[r, k, :], seln[r, CW * c:CW * c + CW], start=True, stop=False)
                    pe.matmul(ps(n % 4), w1[:, w, P * k:P * k + P], xnT[:, CW * c:CW * c + CW], start=False,
                              stop=True).then_inc(S_("lf_pre"), 1)

            def leaves_out(g2):
                c, w = divmod(g2, 3)
                r = slice(32 * w, 32 * w + LV)
                pe.wait_ge(S_("lf_h0"), 4 * (g2 + 1))
                pe.wait_ge(S_("lf_h1"), 4 * (g2 + 1))
                if g2 >= 2:
                    pe.wait_ge(S_("lf_oev"), g2 - 1)
                if w < 2:
                    o = ps(4 + g2 % 2)
                    pe.matmul(o, b2[r, :], selT[r, CW * c:CW * c + CW], start=True, stop=False)
                    for k in range(NB):
                        mm = pe.matmul(o, w2[:, w, k, :], hT[g2 % 2][:, k, :], start=False, stop=(k == NB - 1))
                else:
                    for t in range(CT):
                        o = ps(4 + g2 % 2)[:, P * t:P * t + P]
                        tt = CW * c + P * t
                        pe.matmul(o, selT[r, tt:tt + P], b2[r, :], start=True, stop=False)
                        for k in range(NB):
                            mm = pe.matmul(o, hT[g2 % 2][:, k, P * t:P * t + P], w2[:, w, k, :], start=False,
                                           stop=(k == NB - 1))
                mm.then_inc(S_("lf_o"), 1)

            for g2 in range(3 * CH + 1):
                if g2 < 3 * CH:
                    hidden(g2)
                if g2:
                    leaves_out(g2 - 1)
            pe.wait_ge(S_("lf_oev"), 12)
            end_phase(pe, 2)
            attend(1)
            end_phase(pe, 2)

        @block.vector
        def _(dve):
            def layernorm(k):
                if k == 0:
                    dve.wait_ge(ld["x"], 16)
                with dve.Fori(0, CH) as i:
                    for m in range(CT):
                        t = CT * i + m
                        dve.bn_stats(st6[:, bass.ds(t, 1), :].rearrange("p a b -> p (a b)"),
                                     x[:, bass.ds(t, 1), :].rearrange("p a b -> p (a b)")).then_inc(S_("ln_st"), 1)
                me, ve, mo, vo = (st6[:, :, n] for n in (1, 2, 4, 5))
                dve.wait_ge(S_("ln_st"), T * (k + 1))
                dve.tensor_tensor(lnv[:, 0], me, mo, ALU.subtract).then_inc(S_("ln_a"), 1)
                dve.tensor_tensor(lnv[:, 1], ve, vo, ALU.add).then_inc(S_("ln_a"), 1)
                dve.tensor_tensor(lnv[:, 2], me, mo, ALU.add).then_inc(S_("ln_a"), 1)
                dve.wait_ge(S_("ln_a"), 5 * k + 3)
                dve.tensor_tensor(lnv[:, 0], lnv[:, 0], lnv[:, 0], ALU.mult).then_inc(S_("ln_a"), 1)
                dve.tensor_scalar(mean[:], lnv[:, 2], 0.5, None, ALU.mult).then_inc(S_("ln_a"), 1)
                dve.wait_ge(S_("ln_a"), 5 * k + 5)
                dve.scalar_tensor_tensor(out=lnv[:, 1], in0=lnv[:, 1], scalar=4.0 / D, in1=lnv[:, 0],
                                         op0=ALU.mult, op1=ALU.add).then_inc(S_("ln_mv"), 1)
                dve.wait_ge(S_("ln_std"), k + 1)
                dve.reciprocal(rstd[:], std[:]).then_inc(S_("ln_r"), 1)
                dve.wait_ge(S_("ln_r"), k + 1)
                with dve.Fori(0, CH // 2) as i:
                    for u in range(2):
                        dve.wait_ge(S_("ln_ev"), CH * k + 2 * i + u + 1)
                        for m in range(CT):
                            t = CT * (2 * i + u) + m
                            dve.tensor_scalar(xn[:, u, m, :], x[:, bass.ds(t, 1), :].rearrange("p a b -> p (a b)"),
                                              mean[:, bass.ds(t, 1)], rstd[:, bass.ds(t, 1)],
                                              ALU.subtract, ALU.mult).then_inc(S_("ln_xn"), 1)

            def xattn(layer):
                n_q, n_o = ((4, 2), (1, 1))[layer]

                def sl(name):
                    return S_(f"xa_{name}{layer}")

                if layer == 0:
                    for c in range(4):
                        dve.wait_ge(S_("xa_m"), c + 1)
                        dve.tensor_scalar(M[:, 4 * c:4 * c + 4, :], ps(c)[:, 0:4 * CD].rearrange("p (a b) -> p a b", b=CD),
                                          XA_SCALE[0], None, ALU.mult).then_inc(S_("xa_w"), 1)
                        dve.wait_ge(S_("xa_n"), c + 1)
                        dve.tensor_copy(N[:, 4 * c:4 * c + 4, :],
                                        ps(4 + c)[0:CD, :].rearrange("p (a b) -> p a b", b=P)).then_inc(S_("xa_w"), 1)
                else:
                    dve.wait_ge(S_("consts"), 2)
                    dve.tensor_reduce(gmask[:], hmask[:].rearrange("p (g m) -> p m g", m=4), AX.X, ALU.add).then_inc(S_("gmask"), 1)
                    dve.wait_ge(S_("gmask"), 1)
                    dve.tensor_scalar(hmask[:], hmask[:], XA_SCALE[1], None, ALU.mult).then_inc(S_("gmask"), 1)
                    dve.wait_ge(ld["msk"], 16)
                    dve.tensor_scalar(mrow, msk8, -1.0, BIG, ALU.add, ALU.mult).then_inc(S_("xa_mask"), 1)
                    for c in range(0, 8):
                        dve.wait_ge(S_("xa_k"), c + 1)
                        dve.tensor_copy(kTx[:, CW * c:CW * c + CW], ps(6 + c % 2)).then_inc(S_("xa_kev"), 1)
                    dve.wait_ge(S_("gmask"), 2)
                dve.sem_inc(sl("oev"), 1)
                dve.sem_inc(sl("add"), 1)

                def body(tq, ta, tb, f):
                    def queries(c):
                        if tq is None or c >= n_q:
                            return
                        dve.wait_ge(sl("q"), n_q * tq + c + 1)
                        wait(dve, sl("sc"), 2 * tq - 2)
                        if layer == 0:
                            dve.tensor_copy(qmT[1 - f][0:CD, :, 4 * c:4 * c + 4, :].rearrange("p u h t -> p h u t"),
                                            ps(6)[0:CD, :].rearrange("p (h u t) -> p h u t", u=2, t=S)).then_inc(sl("qev"), 1)
                        else:
                            q = ps(6)[:, 0:P].rearrange("p (u t) -> p u t", t=S)
                            dve.tensor_tensor(qmT[1 - f], q[:, :, None, :].broadcast_to([P, 2, H, S]),
                                              hmask[:, None, :, None].broadcast_to([P, 2, H, S]), ALU.mult).then_inc(sl("qev"), 1)

                    def maxima(u):
                        if ta is None:
                            return
                        dve.wait_ge(sl("sc"), 2 * ta + u + 1)
                        dve.tensor_reduce(nmx[:, u, :], bank[u][:, :].rearrange("p (j k) -> p j k", k=KEYS), AX.X, ALU.max,
                                          negate=True).then_inc(sl("mx"), 1)

                    def reciprocals(t, u):
                        if t is None:
                            return
                        dve.wait_ge(sl("exp"), 2 * t + u + 3)
                        dve.wait_ge(sl("prob"), 2 * t + u + 1)
                        dve.reciprocal(rs[:, u, :], sm[:, u, :]).then_inc(sl("recip"), 1)

                    def outputs(u, hh):
                        if tb is None or hh >= n_o:
                            return
                        b = 2 * tb + u
                        dve.wait_ge(sl("o"), (2 * b + hh + 5) if layer == 0 else b + 3)
                        if u == 0 and hh == 0:
                            dve.wait_ge(sl("y"), tb + 1)
                        if layer == 0:
                            dve.tensor_copy(OT[1 - f][:, 8 * hh:8 * hh + 8, 64 * u:64 * u + 64],
                                            ps(5)[0:CD, :].rearrange("p (h t) -> p h t", t=S)).then_inc(sl("oev"), 1)
                        else:
                            dve.tensor_tensor(Om[1 - f][:, :, 64 * u:64 * u + 64],
                                              ps(5)[:, 0:4 * S].rearrange("p (h t) -> p h t", t=S),
                                              gmask[:, :, None].broadcast_to([P, 4, S]), ALU.mult).then_inc(sl("oev"), 1)

                    def own_values(u):
                        if tb is None or layer == 0:
                            return
                        dve.wait_ge(sl("v"), 2 * tb + u + 1)
                        dve.wait_ge(sl("o"), 2 * tb + u + 1)
                        dve.tensor_copy(vs[:, u, :], ps(5)[:, 0:P]).then_inc(sl("vev"), 1)

                    def add():
                        if tb is None:
                            return
                        dve.wait_ge(sl("y"), tb + 3)
                        xt = x[:, bass.ds(tb, 1), :].rearrange("p a b -> p (a b)")
                        dve.tensor_tensor(xt, ps(7)[:, 0:P], xt, ALU.add).then_inc(sl("add"), 1)

                    reciprocals(tb, 1)
                    for u in range(2):
                        own_values(u)
                        queries(2 * u)
                        maxima(u)
                        outputs(u, 0)
                        queries(2 * u + 1)
                        outputs(u, 1)
                    reciprocals(ta, 0)
                    add()

                body(0, None, None, 1)
                body(1, 0, None, 0)
                with dve.Fori(0, T // 2 - 1) as i:
                    body(2 * i + 2, 2 * i + 1, 2 * i, 1)
                    body(2 * i + 3, 2 * i + 2, 2 * i + 1, 0)
                body(None, T - 1, T - 2, 1)
                body(None, None, T - 1, 0)

            layernorm(0)
            end_phase(dve, 3)
            xattn(0)
            end_phase(dve, 3)
            layernorm(1)
            dve.wait_ge(ld["scan"], 16 * 7)
            dve.tensor_scalar(ddp[:], ident[:], dp[:, 0:1], None, ALU.mult).then_inc(S_("ddp"), 1)
            dve.wait_ge(S_("ln_ev"), 2 * CH + 2)
            for c in range(CH):
                cc = slice(CW * c, CW * c + CW)
                dve.wait_ge(S_("sc_t"), c + 1)
                dve.tensor_scalar(delta[:, cc], ps(c % 2), bx[:, 0:1], 0.0, ALU.add, ALU.max).then_inc(S_("sc_d0"), 1)
                dve.wait_ge(S_("sc_bc"), c + 1)
                if c:
                    dve.wait_ge(S_("sc_sp"), 5 * c)
                dve.tensor_scalar(bcf, ps(2 + c % 2)[0:32, :], bbc[:, 0:1], None, ALU.add).then_inc(S_("sc_bcf"), 1)
                dve.wait_ge(S_("sc_bcf"), c + 1)
                dve.tensor_copy(bcs[0:32, cc], bcf).then_inc(S_("sc_sp"), 1)
                dve.wait_ge(S_("sc_sp"), 5 * c + 1)
                dve.tensor_tensor(bcr, bcf, bcs[0:32, cc], ALU.subtract).then_inc(S_("sc_sp"), 1)
                dve.wait_ge(S_("sc_sp"), 5 * c + 2)
                dve.tensor_copy(bcs[32:64, cc], bcr).then_inc(S_("sc_sp"), 1)
                dve.wait_ge(S_("sc_sp"), 5 * c + 3)
                dve.tensor_copy(bcf, bcs[32:64, cc]).then_inc(S_("sc_sp"), 1)
                dve.wait_ge(S_("sc_sp"), 5 * c + 4)
                dve.tensor_tensor(bcf, bcr, bcf, ALU.subtract).then_inc(S_("sc_sp"), 1)
                dve.wait_ge(S_("sc_sp"), 5 * c + 5)
                dve.tensor_copy(bcs[64:96, cc], bcf).then_inc(S_("sc_split"), 1)
                dve.wait_ge(S_("sc_split"), c + 1)
            for c in range(CH):
                cc = slice(CW * c, CW * c + CW)
                dve.wait_ge(S_("sc_ln"), c + 1)
                dve.wait_ge(S_("sc_d0"), c + 1)
                dve.tensor_tensor(delta[:, cc], delta[:, cc], tmp[c], ALU.add).then_inc(S_("sc_delta"), 1)
                dve.wait_ge(S_("sc_delta"), c + 1)
                dve.tensor_tensor(du[:, cc], delta[:, cc], xnT[:, cc], ALU.mult).then_inc(S_("sc_du"), 1)
            for k in range(4 * NS + 1):
                n, c = divmod(k, 4)
                if k < 4 * NS:
                    cc = slice(CW * c, CW * c + CW)
                    dve.wait_ge(S_("sc_b"), k + 1)
                    if k == 0:
                        dve.wait_ge(S_("sc_du"), CH)
                    dve.tensor_tensor(bxs[k % 2], ps(k % 2), du[:, cc], ALU.mult).then_inc(S_("sc_bx"), 1)
                if k:
                    m = k - 1
                    dve.wait_ge(S_("sc_c"), m + 1)
                    dve.wait_ge(S_("sc_h"), m + 1)
                    if m >= 2:
                        dve.wait_ge(S_("sc_acc"), m - 1)
                    dve.tensor_tensor(hc[m % 2], ps(2 + m % 2), hs[m % 2], ALU.mult).then_inc(S_("sc_hc"), 1)
                if k < 4 * NS:
                    dve.wait_ge(S_("sc_bx"), k + 1)
                    dve.wait_ge(S_("sc_abar"), n + 1)
                    if k >= 2:
                        dve.wait_ge(S_("sc_hc"), k - 1)
                    dve.tensor_tensor_scan(hs[k % 2], abar[n % 2][:, cc], bxs[k % 2], 0.0, ALU.mult, ALU.add).then_inc(S_("sc_h"), 1)
            for c in range(CH):
                dve.wait_ge(S_("sc_out"), c + 1)
                xt = x[:, CT * c:CT * c + CT, :].rearrange("p a b -> p (a b)")
                dve.tensor_tensor(xt, ps(c), xt, ALU.add)
            end_phase(dve, 3)
            layernorm(2)
            link = [0]

            def chain(ins):
                ins.then_inc(S_("chain"), 1)
                link[0] += 1
                dve.wait_ge(S_("chain"), link[0])

            dve.wait_ge(S_("me_lg"), 1)
            chain(dve.tensor_copy(lg[:], ps(7)[0:B, 0:E]))
            li = lg[:, :, None].broadcast_to([B, E, E])
            lj = lg[:, None, :].broadcast_to([B, E, E])
            chain(dve.tensor_tensor(eq[:], lj, li, ALU.is_equal))
            dve.wait_ge(S_("g1"), 7)
            chain(dve.tensor_tensor(eq[:], eq[:], tri[:], ALU.mult))
            chain(dve.tensor_tensor(gt[:], lj, li, ALU.is_gt))
            chain(dve.tensor_tensor(gt[:], gt[:], eq[:], ALU.add))
            chain(dve.tensor_reduce(rank[:], gt[:], AX.X, ALU.add))
            chain(dve.tensor_scalar(rank[:], rank[:], 1.5, None, ALU.is_lt))
            chain(dve.tensor_reduce(lmx[:, 0:1], lg[:], AX.X, ALU.max))
            chain(dve.tensor_scalar(lg[:], lg[:], lmx[:, 0:1], None, ALU.subtract))
            dve.sem_inc(S_("me_lsub"), 1)
            dve.wait_ge(S_("me_exp"), 1)
            chain(dve.tensor_tensor(gate[:], gate[:], rank[:], ALU.mult))
            chain(dve.tensor_reduce(lmx[:, 1:2], gate[:], AX.X, ALU.add))
            chain(dve.reciprocal(lmx[:, 1:2], lmx[:, 1:2]))
            dve.tensor_scalar(gate[:], gate[:], lmx[:, 1:2], None, ALU.mult).then_inc(S_("me_gate"), 1)
            dve.wait_ge(S_("me_gT"), 1)
            dve.tensor_copy(gT[:], ps(7)[0:E, 64:64 + B]).then_inc(S_("me_gTs"), 1)
            dve.wait_ge(S_("me_gx"), 1)
            chain(dve.tensor_copy(gx[:], ps(7)[:, 128:128 + 4 * B].rearrange("p (k b) -> p k b", b=B)))
            for c in range(CH):
                for k in range(4):
                    n = 4 * c + k
                    dve.wait_ge(S_("me_m"), n + 1)
                    if k == 0 and c >= 2:
                        dve.wait_ge(S_("me_y"), c - 1)
                    dve.tensor_tensor(midT[c % 2][:, k, :].rearrange("p (b s) -> p b s", s=S),
                                      ps(n % 2).rearrange("p (b s) -> p b s", s=S),
                                      gx[:, k, 8 * c:8 * c + 8, None].broadcast_to([P, 8, S]), ALU.mult).then_inc(S_("me_mev"), 1)
            for c in range(CH):
                dve.wait_ge(S_("me_y"), c + 1)
                xt = x[:, CT * c:CT * c + CT, :].rearrange("p a b -> p (a b)")
                dve.tensor_tensor(xt, ps(2 + c), xt, ALU.add)
            end_phase(dve, 3)
            layernorm(3)
            xattn(1)
            end_phase(dve, 3)

            def attend(k):
                def chunk(c):
                    return slice(8 * c, 8 * c + 8)
                dve.wait_ge(S_("at_sc"), k + 1)
                for c in range(2):
                    chain(dve.tensor_scalar(sc[:, chunk(c), :], ps(c).rearrange("p (t s) -> p t s", s=S), D_SCALE, None, ALU.mult))
                if k == 0:
                    dve.wait_ge(S_("keep"), 2)
                    chain(dve.tensor_tensor(sc, sc, keep[:, None, :].broadcast_to([P, T, S]), ALU.mult))
                    chain(dve.tensor_scalar(eqz, sc, 0.0, MASK_NEG, ALU.is_equal, ALU.mult))
                    chain(dve.tensor_tensor(sc, sc, eqz, ALU.add))
                chain(dve.tensor_reduce(amx[:], sc, AX.X, ALU.max))
                chain(dve.tensor_tensor(sc, sc, amx[:, :, None].broadcast_to([P, T, S]), ALU.subtract))
                dve.sem_inc(S_("at_sub"), 1)
                dve.wait_ge(S_("at_exp"), k + 1)
                chain(dve.tensor_reduce(asm[:], sc, AX.X, ALU.add))
                chain(dve.reciprocal(ars[:], asm[:]))
                dve.wait_ge(S_("pd_zero"), k + 1)
                for u in range(2):
                    r = slice(64 * u, 64 * u + 64)
                    dve.tensor_tensor(pd[r, :, 64 * u:64 * u + 64], sc[r], ars[r, :, None].broadcast_to([64, T, S]),
                                      ALU.mult).then_inc(S_("at_p"), 1)
                for c in range(CH):
                    dve.wait_ge(S_("at_y"), CH * k + c + 1)
                    xt = x[:, CT * c:CT * c + CT, :].rearrange("p a b -> p (a b)")
                    dve.tensor_tensor(xt, ps(6 + c % 2), xt, ALU.add).then_inc(S_("at_add"), 1)

            layernorm(4)
            for c in range(CH):
                dve.wait_ge(S_("sa_v"), c + 1)
                dve.tensor_copy(v[:, CT * c:CT * c + CT, :], ps(2 + c).rearrange("p (a b) -> p a b", b=D)).then_inc(S_("sa_vev"), 1)
            attend(0)
            end_phase(dve, 3)
            layernorm(5)
            dve.wait_ge(S_("tr_sc"), 1)
            for c in range(2):
                chain(dve.tensor_scalar(dec[:, 8 * c:8 * c + 8].rearrange("p t a b -> p t (a b)"),
                                        ps(2 + c)[:, 0:384].rearrange("p (t n) -> p t n", n=48)[:, :, 0:3 * NN],
                                        0.0, None, ALU.is_ge))
            decf = dec.rearrange("p t a b -> p (t a) b")
            self_ = selt[:].rearrange("p t a b -> p (t a) b")
            bufs = [lvl, self_]
            dve.wait_ge(S_("g0"), 11)
            cur = self_
            chain(dve.tensor_copy(cur[:, :, 1:2], decf[:, :, 0:1]))
            chain(dve.tensor_scalar(cur[:, :, 0:1], decf[:, :, 0:1], -1.0, 1.0, ALU.mult, ALU.add))
            for depth in range(1, 4):
                w = 2 ** depth
                chain(dve.tensor_copy(lvl[:, :, 0:w], self_[:, :, 0:w]))
                chain(dve.tensor_tensor(self_[:, :, 1:2 * w:2], lvl[:, :, 0:w], decf[:, :, w - 1:2 * w - 1], ALU.mult))
                chain(dve.tensor_tensor(self_[:, :, 0:2 * w:2], lvl[:, :, 0:w], self_[:, :, 1:2 * w:2], ALU.subtract))
            dve.sem_inc(S_("tr_sel"), 1)
            for c in range(CH):
                dve.wait_ge(S_("tr_st"), c + 1)
                dve.tensor_copy(selT[:, CW * c:CW * c + CW], ps(4 + c)[0:96, :]).then_inc(S_("tr_selT"), 1)
                dve.tensor_scalar(seln[:, CW * c:CW * c + CW], ps(4 + c)[0:96, :], -1.0, BIG, ALU.add,
                                  ALU.mult).then_inc(S_("tr_selT"), 1)
            for g2 in range(3 * CH + 1):
                if g2 < 3 * CH:
                    for k in range(1, NB, 2):
                        n = NB * g2 + k
                        dve.wait_ge(S_("lf_pre"), n + 1)
                        if g2 >= 2:
                            dve.wait_ge(S_("lf_o"), g2 - 1)
                        dve.tensor_scalar(hT[g2 % 2][:, k, :], ps(n % 4), b1[:, g2 % 3, k:k + 1], 0.0, ALU.add,
                                          ALU.max).then_inc(S_("lf_h1"), 1)
                if g2:
                    c, w = divmod(g2 - 1, 3)
                    dve.wait_ge(S_("lf_o"), g2)
                    o = ps(4 + (g2 - 1) % 2)
                    cc = slice(CW * c, CW * c + CW)
                    if w < 2:
                        dve.tensor_copy((qT, kT)[w][:, cc], o).then_inc(S_("lf_oev"), 1)
                    else:
                        dve.tensor_copy(v[:, CT * c:CT * c + CT, :], o.rearrange("p (a b) -> p a b", b=D)).then_inc(S_("lf_oev"), 1)
            end_phase(dve, 3)
            dve.memset(pd, 0.0).then_inc(S_("pd_zero"), 1)
            attend(1)
            end_phase(dve, 3)

        @block.scalar
        def _(act):
            def layernorm(k):
                if k == 0:
                    act.wait_ge(S_("g0"), 11)
                    act.sem_inc(S_("ln_ev"), 2)
                act.wait_ge(S_("ln_mv"), k + 1)
                act.activation(std[:], lnv[:, 1], ACT.Sqrt, bias=epsc[:, 0:1], scale=0.25).then_inc(S_("ln_std"), 1)
                with act.Fori(0, CH // 2) as i:
                    for u in range(2):
                        c = 2 * i + u
                        act.wait_ge(S_("ln_tr"), CH * k + c + 1)
                        act.copy(xnT[:, bass.ds(c * CW, CW)], ps(u)).then_inc(S_("ln_ev"), 1)

            def xattn(layer):
                def sl(name):
                    return S_(f"xa_{name}{layer}")

                act.sem_inc(sl("ptev"), 1)
                act.sem_inc(sl("exp"), 2)

                def body(ta, tb):
                    def exponentials(u):
                        if ta is None:
                            return
                        b = 2 * ta + u
                        act.wait_ge(sl("mx"), b + 1)
                        wait(act, sl("pt"), 2 * b - 2)
                        for j in range(8):
                            ex = act.activation(prob[u][:, j, :], bank[u][:, P * j:P * j + P], ACT.Exp,
                                                bias=nmx[:, u, j:j + 1], accum_out=sm[:, u, j:j + 1])
                        ex.then_inc(sl("exp"), 1)

                    def turned(u, hh):
                        if tb is None:
                            return
                        b = 2 * tb + u
                        act.wait_ge(sl("pt"), 2 * b + hh + 1)
                        act.wait_ge(sl("o"), (2 * b + hh + 1) if layer == 0 else b + 1)
                        act.copy(PT[u][:, 4 * hh:4 * hh + 4, :],
                                 ps(4).rearrange("p (j r) -> p j r", r=P)).then_inc(sl("ptev"), 1)

                    turned(0, 0)
                    turned(0, 1)
                    exponentials(0)
                    turned(1, 0)
                    turned(1, 1)
                    exponentials(1)

                body(0, None)
                with act.Fori(0, T // 2 - 1) as i:
                    body(2 * i + 1, 2 * i)
                    body(2 * i + 2, 2 * i + 1)
                body(T - 1, T - 2)
                body(None, T - 1)

            layernorm(0)
            end_phase(act, 4)
            xattn(0)
            end_phase(act, 4)
            layernorm(1)
            act.wait_ge(ld["scan"], 16 * 7)
            act.activation(amin[:], alog[:], ACT.Exp).then_inc(S_("sc_a"), 1)
            act.wait_ge(S_("sc_a"), 1)
            act.mul(amin[:], amin[:], -1.0).then_inc(S_("sc_a"), 1)
            for c in range(CH):
                act.wait_ge(S_("sc_dp"), c + 1)
                act.activation(tmp[c], ps(c % 2), ACT.Abs, bias=bx[:, 0:1]).then_inc(S_("sc_t"), 1)
            for c in range(CH):
                act.wait_ge(S_("sc_t"), CH)
                act.activation(tmp[c], tmp[c], ACT.Exp, scale=-1.0).then_inc(S_("sc_e"), 1)
            for c in range(CH):
                act.wait_ge(S_("sc_e"), c + 1)
                act.activation(tmp[c], tmp[c], ACT.Ln, bias=onec[:, 0:1]).then_inc(S_("sc_ln"), 1)
            act.wait_ge(S_("sc_delta"), CH)
            act.wait_ge(S_("sc_a"), 2)
            for n in range(NS):
                if n >= 2:
                    act.wait_ge(S_("sc_h"), 4 * (n - 1))
                act.activation(abar[n % 2], delta, ACT.Exp, scale=amin[:, n:n + 1]).then_inc(S_("sc_abar0"), 1)
            for c in range(CH):
                act.wait_ge(S_("sc_acc"), 4 * (NS - 1) + c + 1)
                act.copy(yT[:, CW * c:CW * c + CW], ps(4 + c)).then_inc(S_("sc_yT"), 1)
            end_phase(act, 4)
            layernorm(2)
            act.wait_ge(S_("me_lsub"), 1)
            act.activation(gate[:], lg[:], ACT.Exp).then_inc(S_("me_exp"), 1)
            end_phase(act, 4)
            layernorm(3)
            xattn(1)
            end_phase(act, 4)

            def attend(k):
                act.wait_ge(S_("at_sub"), k + 1)
                act.activation(sc, sc, ACT.Exp).then_inc(S_("at_exp"), 1)
                for c in range(CH):
                    act.wait_ge(S_("at_pt"), CH * k + c + 1)
                    act.copy(pdT[:, CT * c:CT * c + CT, :], ps(2 + c).rearrange("p (a b) -> p a b", b=P)).then_inc(S_("at_ptev"), 1)

            layernorm(4)
            for n in range(2 * CH):
                c, w = divmod(n, 2)
                act.wait_ge(S_("sa_q"), n + 1)
                act.copy((qT, kT)[w][:, CW * c:CW * c + CW], ps(n % 2)).then_inc(S_("sa_qk"), 1)
            attend(0)
            end_phase(act, 4)
            layernorm(5)
            for c in range(CH):
                for w in range(3):
                    g2 = 3 * c + w
                    for k in range(0, NB, 2):
                        n = NB * g2 + k
                        act.wait_ge(S_("lf_pre"), n + 1)
                        if g2 >= 2:
                            act.wait_ge(S_("lf_o"), g2 - 1)
                        act.activation(hT[g2 % 2][:, k, :], ps(n % 4), ACT.Relu, bias=b1[:, w, k:k + 1]).then_inc(S_("lf_h0"), 1)
            end_phase(act, 4)
            attend(1)
            end_phase(act, 4)


def kernel(**inputs):
    import concourse.bacc as bacc
    from concourse.bass_utils import run_bass_kernel_spmd as run

    def a(name):
        return np.asarray(inputs[name])

    T, B, D = 16, 32, 128
    w = {}
    w["x"] = a("x").reshape(T, 128, D).transpose(1, 0, 2)
    w["ctxT"] = a("ctx_768").transpose(2, 0, 1).reshape(96, -1)
    w["ctx"] = a("ctx_768").transpose(1, 0, 2)
    w["mask"] = a("mask_BxS2_bf1").reshape(1, -1).view(np.uint8)

    def blocks(m, rows=128):
        return m.reshape(-1, rows, m.shape[-1]).transpose(1, 0, 2)

    w["l0_wqT"] = blocks(a("L0_xattn_Wq").T, 64)
    w["l0_wkT"] = blocks(a("L0_xattn_Wk").T, 64)
    w["l0_wvT"] = blocks(a("L0_xattn_Wv").T, 64)
    w["l0_wo"] = blocks(a("L0_xattn_Wo"), 64)
    w["l0_bo"] = a("L0_xattn_bo").reshape(1, D)
    w["wx"] = a("L0_attn_W_xproj")
    w["bx_d"] = a("L0_attn_b_xproj")[:D].reshape(D, 1)
    w["bx_bc"] = a("L0_attn_b_xproj")[D:].reshape(32, 1)
    w["wout"] = a("L0_attn_W_out")
    w["bout"] = a("L0_attn_b_out").reshape(1, D)
    w["alog"] = a("L0_attn_A_log")
    w["dp"] = a("L0_attn_Dp").reshape(D, 1)
    w["wrT"] = a("L0_ffn_Wr").T
    w["aT"] = a("L0_ffn_A").reshape(512, D).T.reshape(D, 4, 128)
    w["bw"] = blocks(a("L0_ffn_Bw").transpose(0, 2, 1).reshape(512, D))
    w["l1_wq"] = a("L1_xattn_Wq")
    w["l1_wk"] = a("L1_xattn_Wk")
    w["l1_wv"] = a("L1_xattn_Wv")
    w["l1_wo"] = a("L1_xattn_Wo")
    w["wqkv"] = a("L1_attn_W")
    for n in "qkv":
        p = f"L1_ffn_{n}_"
        w[n + "_nw"] = a(p + "node_w").T
        w[n + "_nb"] = a(p + "node_b").reshape(1, -1)
        w[n + "_w1"] = a(p + "w1").transpose(1, 0, 2).reshape(D, -1)
        w[n + "_b1"] = a(p + "b1").reshape(8, 128).T
        w[n + "_w2"] = blocks(a(p + "w2").reshape(1024, D))
        w[n + "_b2"] = a(p + "b2")
    nc = bacc.Bacc("TRN2", target_bir_lowering=False, num_devices=1)
    arrays, aps = {}, {}
    for name, m in w.items():
        arrays["in_" + name] = m = np.ascontiguousarray(m)
        aps[name] = nc.dram_tensor("in_" + name, m.shape, mybir.dt.from_np(m.dtype), kind="ExternalInput").ap()
    out = nc.dram_tensor("out_0", (128, T, D), F32, kind="ExternalOutput").ap()
    build(nc, aps, out)
    r = run(nc, [arrays], core_ids=[0])
    return r.results[0]["out_0"].transpose(1, 0, 2).reshape(B, 64, D)
```

```python
from contextlib import ExitStack

import numpy as np

import concourse.bass as bass
from concourse import mybir

F32 = mybir.dt.float32
BF16 = mybir.dt.bfloat16
U8 = mybir.dt.uint8
ALU = mybir.AluOpType
ACT = mybir.ActivationFunctionType
AX = mybir.AxisListType

P = 128
EPS = 1e-5
BIG = 1e30
MASK_NEG = -9000000000000000.0


def wait(eng, sem, value):
    if isinstance(value, int) and value <= 0:
        return
    eng.wait_ge(sem, value)


def build(nc, A, out, leaf_rows):
    B, S, D = 32, 64, 128
    KEYS, CD = 128, 96
    H = 16
    T = B * S // P
    CH = 4
    CT = T // CH
    CW = CT * P
    NS = 16
    LEAD = 2
    E, R = 8, 64
    LV, LW = 16, 64
    NB = LV * LW // P
    NN = 15
    XA_SCALE = (64 ** -0.5, 8 ** -0.5)
    D_SCALE = float(D) ** -0.5

    def own_tiles(k):
        return CT if k == 0 else CT - 1

    def tiles_before(k, c, rest=False):
        return sum((CT - own_tiles(m) if rest else own_tiles(m)) * (CH if m < k else c) for m in range(k + 1))

    with ExitStack() as ctx:
        def sb(name, shape, dt=F32):
            return ctx.enter_context(nc.sbuf_tensor(name, shape, dt))

        def sem(name):
            return ctx.enter_context(nc.semaphore(name))

        bank = [ctx.enter_context(nc.psum_tensor(f"bank{n}", [P, 1024], F32)) for n in range(4)]

        def ps(n):
            return bank[n // 2][:, 512 * (n % 2):512 * (n % 2) + 512]

        x = sb("x_sb", [P, T, D])
        xnT = sb("xnT", [P, T * P])
        ident = sb("ident", [P, P])
        st6 = sb("st6", [P, T, 6])
        mean = sb("mean", [P, T])
        lnv = sb("lnv", [P, 3, T])
        rstd = sb("rstd", [P, T])
        std = sb("std", [P, T])
        xn = sb("xn", [P, 2, CT, D])
        epsc = sb("epsc", [P, 1])
        warm = sb("warm", [P, 16])
        onec = sb("onec", [P, 1])
        bout = sb("bout", [P, D])
        ctxT = sb("ctxT", [CD, B * KEYS])
        cx = sb("cx", [P, 4, CD])
        M = sb("M", [P, H, CD])
        N = sb("N", [CD + 1, H, P])
        hmask = sb("hmask", [P, H])
        pool = sb("pool", [P, 17920])

        def at(o, shape, parts=P, dt=F32):
            n = int(np.prod(shape))
            words = n * (2 if dt is BF16 else 4) // 4
            v = pool[0:parts, o:o + words]
            if dt is not F32:
                v = v.bitcast(dt)
            if len(shape) == 2:
                v = v.rearrange("p (a b) -> p a b", b=shape[1])
            elif len(shape) == 3:
                v = v.rearrange("p (a b c) -> p a b c", b=shape[1], c=shape[2])
            return v

        qmT = [at(2048 * n, (2, H, S)) for n in range(2)]
        OT = [at(4096 + 2048 * n, (H, P), CD + 1) for n in range(2)]
        prob = [at(8192 + 1024 * n, (8, KEYS)) for n in range(2)]
        PT = [at(10240 + 1024 * n, (8, P)) for n in range(2)]
        nmx = sb("nmx", [P, 2, 8])
        sm = sb("sm", [P, 4, 8])
        rs = sb("rs", [P, 4, 8])
        wq1 = sb("wq1", [P, P])
        wk1 = sb("wk1", [CD, P])
        wv1 = sb("wv1", [CD, P])
        wo1 = sb("wo1", [P, P])
        gmask = sb("gmask", [P, 4])
        onesb = sb("onesb", [1, P], BF16)
        Om = [at(4096 + 512 * n, (4, P)) for n in range(2)]
        mrow = at(5120, (B * KEYS,), 1, BF16)
        msk8 = pool[0:1, 7168:7168 + B * KEYS // 4].bitcast(U8)
        kTx = at(12288, (B * KEYS,))
        vs = at(16384, (2, P))
        cxT = at(16640, (4, KEYS), CD)
        wqT = at(8192, (H, P), 64)
        wkT = at(10240, (H, CD), 64)
        wvT = at(11776, (H, CD), 64)
        wo = at(13312, (H, P), 64)

        wx = sb("wx", [P, 160])
        wout = sb("wout", [P, P])
        bx = sb("bx", [P, 1])
        bbc = sb("bbc", [32, 1])
        alog = sb("alog", [P, NS])
        amin = sb("amin", [P, NS])
        dp = sb("dp", [P, 1])
        ddp = sb("ddp", [P, P])
        delta = at(0, (2048,))
        du = at(2048, (2048,))
        abar = [at(4096 + 2048 * n, (2048,)) for n in range(2)]
        hs = [at(9216 + 512 * n, (512,)) for n in range(2)]
        hc = [at(10240 + 512 * n, (512,)) for n in range(2)]
        tmp = [at(11264 + 512 * n, (512,)) for n in range(4)]
        bn = [at(o, (512,)) for o in (11264, 11776)]
        bxs = [at(o, (512,)) for o in (8192, 8704, 12288, 12800)]
        yT = at(13312, (2048,))
        bcs = at(15360, (2048,), 96, BF16)
        bcr = [at(16384 + 512 * n, (512,), 32) for n in range(2)]
        bcm = [at(17408 + 256 * n, (512,), 32, BF16) for n in range(2)]
        bselb = sb("bselb", [P, 32, P], BF16)

        prob_odd = [bselb[:, 16 * n:16 * n + 16, :].bitcast(F32).rearrange("p a b -> p (a b)").rearrange(
            "p (j k) -> p j k", k=KEYS) for n in range(2)]

        wrT = sb("wrT", [P, E])
        aT = at(0, (E * R // P, P))
        bw = at(512, (E * R // P, D))
        midT = [at(1024 + 2048 * n, (4, CW)) for n in range(2)]
        lg = sb("lg", [B, E])
        gt = sb("gt", [B, E, E])
        eq = sb("eq", [B, E, E])
        tri = sb("tri", [B, E, E])
        rank = sb("rank", [B, E])
        lmx = sb("lmx", [B, 2])
        gate = sb("gate", [B, E])
        gT = sb("gT", [E, B])
        esel = sb("esel", [E, 4, P])
        gx = sb("gx", [P, 4, B])

        wqkv = at(0, (384,))
        qT = at(1024, (2048,))
        kT = at(3072, (2048,))
        v = at(5120, (T, D))
        sc = at(7168, (T, S))
        pd = at(8192, (T, P))
        pdT = at(10240, (T, P))
        keep = at(12288, (S,))
        eqz = at(12352, (T, S))
        amx = sb("amx", [P, T])
        asm = sb("asm", [P, T])
        ars = sb("ars", [P, T])

        w1 = sb("w1", [P, 3, LV * LW])
        w2 = sb("w2", [P, 3, NB, D])
        b1 = sb("b1", [P, 3, NB])
        b2 = sb("b2", [96, D])
        nw = sb("nw", [P, 96])
        nb = sb("nb", [96, 1])
        path = sb("path", [96, 96])
        pathb = sb("pathb", [96, 96], BF16)
        rights = sb("rights", [96, 1])
        decb = [sb(f"decb{n}", [96, CW], BF16) for n in range(2)]
        hT = [at(7168 + 4096 * n, (NB, CW)) for n in range(2)]
        selT = sb("selT", [96, T * P])
        selb = [at(17408 + 256 * n, (CW,), 96, BF16) for n in range(2)]
        selx = [at(15360, (NB, CW), P, BF16), bselb[:].rearrange("p (k a) m -> p k (a m)", a=4)]

        s_phase = sem("phase_done")
        ld = {n: sem("ld_" + n) for n in ("x0", "x1", "x2", "x3", "w0", "ctx", "msk", "w1", "scan", "moe", "l1x", "wqkv", "tree")}
        cx_in = [sem(f"cx_in{n}") for n in range(4)]
        s_out = sem("out_written")
        leaf_out = [sem(f"leaf_out{n}") for n in range(2)]
        selx_in = [sem(f"selx_in{n}") for n in range(2)]
        names = {}

        def S_(name):
            if name not in names:
                names[name] = sem(name)
            return names[name]

        phases = [0] * 5

        def end_phase(eng, k):
            phases[k] += 1
            eng.drain().then_inc(s_phase, 1)
            eng.wait_ge(s_phase, 5 * phases[k])

        def prob_slot(layer, odd, u):
            return prob_odd[u] if layer and odd else prob[u]

        def q_bank(tq, c):
            return 4 + (c + 2) % 4 if isinstance(tq, int) and tq == 0 else 6

        def pt_bank(layer, hh):
            return ps(6 if layer and hh else 4)

        block = ctx.enter_context(nc.Block())

        @block.sync
        def _(sp):
            for c in range(CH):
                sp.dma_start(x[:, CT * c:CT * c + CT, :], A["x"][:, CT * c:CT * c + CT, :]).then_inc(ld[f"x{c}"], 16)
            for t, n in ((wqT, "l0_wqT"), (wkT, "l0_wkT"), (wvT, "l0_wvT"), (wo, "l0_wo"), (N[CD:CD + 1, 0, :], "l0_bo")):
                sp.dma_start(t, A[n]).then_inc(ld["w0"], 16)
            sp.dma_start(ctxT[0:CD, :], A["ctxT"]).then_inc(ld["ctx"], 16)

            def later_loads():
                for t, n in ((wx[:], "wx"), (wout[:], "wout"), (bx[:], "bx_d"), (bbc[:], "bx_bc"), (alog[:], "alog"),
                             (dp[:], "dp"), (bout[:], "bout")):
                    src = A[n].broadcast_to([P, D]) if n == "bout" else A[n]
                    sp.dma_start(t, src).then_inc(ld["scan"], 16)
                sp.dma_start(wrT[:], A["wrT"]).then_inc(ld["moe"], 16)
                for t, n in ((wq1, "l1_wq"), (wk1, "l1_wk"), (wv1, "l1_wv"), (wo1, "l1_wo")):
                    sp.dma_start(t[:], A[n]).then_inc(ld["l1x"], 16)
                for n, name in enumerate("qkv"):
                    sp.dma_start(w1[:, n, :], A[name + "_w1"]).then_inc(ld["tree"], 16)
                    sp.dma_start(w2[:, n], A[name + "_w2"]).then_inc(ld["tree"], 16)
                    sp.dma_start(b1[:, n], A[name + "_b1"]).then_inc(ld["tree"], 16)
                    sp.dma_start(b2[32 * n:32 * n + LV, :], A[name + "_b2"]).then_inc(ld["tree"], 16)
                    if n == 0:
                        sp.wait_ge(S_("tree_zero"), 2)
                    sp.dma_start(nw[:, 32 * n:32 * n + NN], A[name + "_nw"]).then_inc(ld["tree"], 16)
                    sp.dma_start(nb[32 * n:32 * n + NN, :], A[name + "_nb"]).then_inc(ld["tree"], 16)
                sp.dma_start(path[:], A["path"]).then_inc(ld["tree"], 16)
                sp.dma_start(rights[:], A["rights"]).then_inc(ld["tree"], 16)

            def contexts(layer):
                uses, first = ((2, 4), (1, 0))[layer]

                def load(b, n):
                    if layer == 0:
                        src = A["ctx"][:, bass.ds(b, 1), :].rearrange("p a c -> p (a c)")
                        sp.dma_start(cx[:, n, :], src).then_inc(cx_in[n], 16)
                    else:
                        sp.dma_start(cxT[:, n, :], A["ctxT"][:, bass.ds(b * KEYS, KEYS)]).then_inc(cx_in[n], 16)

                for n in range(4):
                    load(n, n)
                if layer == 0:
                    later_loads()
                with sp.Fori(0, B // 4 - 1) as i:
                    for n in range(4):
                        sp.wait_ge(S_("xa_o0" if layer == 0 else "xa_v1"), uses * (4 * i + n + 1) + first)
                        load(4 * i + 4 + n, n)

            end_phase(sp, 0)
            contexts(0)
            for k in range(2):
                end_phase(sp, 0)
            sp.dma_start(aT, A["aT"]).then_inc(ld["moe"], 16)
            sp.dma_start(bw, A["bw"]).then_inc(ld["moe"], 16)
            end_phase(sp, 0)
            sp.dma_start(msk8, A["mask"]).then_inc(ld["msk"], 16)
            contexts(1)
            end_phase(sp, 0)
            sp.dma_start(wqkv, A["wqkv"]).then_inc(ld["wqkv"], 16)
            end_phase(sp, 0)

            def rows_out(c):
                sp.wait_ge(S_("tr_sel"), 2 * (c + 1))
                sp.dma_start(leaf_rows[:, CW * c:CW * c + CW], selb[c % 2]).then_inc(leaf_out[c % 2], 16)

            def spread(g2):
                c, w = divmod(g2, 3)
                for u in range(2):
                    rows_u = leaf_rows[32 * w + u:32 * w + u + LV - 1:2, CW * c:CW * c + CW]
                    sp.dma_start(selx[g2 % 2][64 * u:64 * u + 64],
                                 rows_u[None].broadcast_to([64, NB, CW])).then_inc(selx_in[g2 % 2], 16)

            rows_out(0)
            rows_out(1)
            sp.wait_ge(leaf_out[0], 16)
            spread(0)
            spread(1)
            rows_out(2)
            rows_out(3)
            for n in range(2):
                sp.wait_ge(leaf_out[n], 16 * CH // 2)
            for g2 in range(2, 3 * CH):
                sp.wait_ge(S_("lf_m"), 2 * (g2 - 1))
                spread(g2)
            for c in range(CH):
                sp.wait_ge(S_("x_add"), CH * 3 + c + 1)
                sp.dma_start(out[:, CT * c:CT * c + CT, :], x[:, CT * c:CT * c + CT, :]).then_inc(s_out, 16)
            sp.wait_ge(s_out, 16 * CH)

        @block.gpsimd
        def _(g):
            g.memset(ident[:], 0.0).then_inc(S_("g0"), 1)
            g.memset(epsc[:], EPS).then_inc(S_("g0"), 1)
            g.wait_ge(S_("g0"), 2)
            g.affine_select(out=ident[:], in_=ident[:], compare_op=ALU.not_equal, fill=1.0, base=0,
                            pattern=[[-1, P]], channel_multiplier=1).then_inc(S_("consts"), 1)
            g.memset(onec[:], 1.0).then_inc(S_("consts"), 1)
            g.memset(onesb[:], 1.0).then_inc(S_("consts"), 1)
            g.memset(nw[:], 0.0).then_inc(S_("tree_zero"), 1)
            g.memset(nb[:], 0.0).then_inc(S_("tree_zero"), 1)
            g.drain().then_inc(s_phase, 1)
            g.memset(hmask[:], 1.0).then_inc(S_("gs"), 1)
            g.memset(bselb[:], 0.0).then_inc(S_("gs"), 1)
            g.memset(tri[:], 0.0).then_inc(S_("gs"), 1)
            g.memset(esel[:], 1.0).then_inc(S_("gs"), 1)
            g.wait_ge(S_("gs"), 4)
            g.affine_select(out=hmask[:], in_=hmask[:], compare_op=ALU.is_ge, fill=0.0, base=0,
                            pattern=[[-8, H]], channel_multiplier=1).then_inc(S_("g1"), 1)
            g.wait_ge(S_("g1"), 1)
            g.affine_select(out=hmask[:], in_=hmask[:], compare_op=ALU.is_ge, fill=0.0, base=7,
                            pattern=[[8, H]], channel_multiplier=-1).then_inc(S_("hmask"), 1)
            for part in range(3):
                g.affine_select(out=bselb[0:96], in_=bselb[0:96], compare_op=ALU.not_equal, fill=1.0, base=-32 * part,
                                pattern=[[-1, 32], [0, P]], channel_multiplier=1).then_inc(S_("g1"), 1)
                g.wait_ge(S_("g1"), 2 + part)
            g.affine_select(out=tri[:], in_=tri[:], compare_op=ALU.is_ge, fill=1.0, base=0,
                            pattern=[[-1, E], [1, E]], channel_multiplier=0).then_inc(S_("g1"), 1)
            g.affine_select(out=esel[:], in_=esel[:], compare_op=ALU.is_ge, fill=0.0, base=0,
                            pattern=[[P, 4], [1, P]], channel_multiplier=-R).then_inc(S_("g1"), 1)
            g.wait_ge(S_("g1"), 6)
            g.affine_select(out=esel[:], in_=esel[:], compare_op=ALU.is_ge, fill=0.0, base=R - 1,
                            pattern=[[-P, 4], [-1, P]], channel_multiplier=R).then_inc(S_("g1"), 1)
            def layernorm(k):
                g.wait_ge(S_("ln_r"), k + 1)
                for c in range(CH):
                    g.wait_ge(S_("ln_ev"), CH * k + c + 1)
                    for m in range(own_tiles(k), CT):
                        t = CT * c + m
                        g.tensor_scalar(xn[:, c % 2, m, :], x[:, t, :], mean[:, t:t + 1], rstd[:, t:t + 1],
                                        ALU.subtract, ALU.mult).then_inc(S_("ln_xng"), 1)

            def normalise(layer):
                recip, done = S_(f"xa_recip{layer}"), S_(f"xa_prob{layer}")
                g.sem_inc(done, 2)
                with g.Fori(0, T // 2) as i:
                    for odd in range(2):
                        for u in range(2):
                            own = prob_slot(layer, odd, u)
                            g.wait_ge(recip, 4 * i + 2 * odd + u + 1)
                            g.tensor_tensor(own, own, rs[:, 2 * odd + u, :, None].broadcast_to([P, 8, KEYS]),
                                            ALU.mult).then_inc(done, 1)

            phases[1] += 1
            g.wait_ge(s_phase, 5)
            normalise(0)
            end_phase(g, 1)
            layernorm(1)
            g.wait_ge(S_("ln_ev"), 2 * CH + 2)
            g.wait_ge(ld["scan"], 16 * 7)
            g.tensor_tensor(x[:], x[:], bout[:, None, :].broadcast_to([P, T, D]), ALU.add).then_inc(S_("x_bias"), 1)

            def restart(k):
                n, c = divmod(k, CH)
                g.wait_ge(S_("sc_abar0"), k + 1)
                g.memset(abar[n % 2][:, CW * c:CW * c + CW:S], 0.0).then_inc(S_("sc_abar"), 1)

            g.wait_ge(S_("sc_du"), CH)
            for c in range(LEAD):
                restart(c)
            for k in range(CH * NS):
                c = k % CH
                g.wait_ge(S_("sc_bn"), k + 1)
                if k >= 4:
                    g.wait_ge(S_("sc_h"), k - 3)
                g.tensor_tensor(bxs[k % 4], bn[k % 2], du[:, CW * c:CW * c + CW], ALU.mult).then_inc(S_("sc_bx"), 1)
                if k + LEAD < CH * NS:
                    restart(k + LEAD)
            end_phase(g, 1)
            layernorm(2)
            g.wait_ge(S_("ln_ev"), 3 * CH + 2)
            for n, c in enumerate((2, 3, 0, 1)):
                if c < 2:
                    g.wait_ge(S_("x_own"), n - 1)
                    for m in range(CT):
                        t = CT * c + m
                        g.tensor_scalar(xn[:, c, m, :], x[:, t, :], mean[:, t:t + 1], rstd[:, t:t + 1],
                                        ALU.subtract, ALU.mult).then_inc(S_("xn_again"), 1)
                    g.wait_ge(S_("xn_again"), CT * (c + 1))
                xc = x[:, CT * c:CT * c + CT, :]
                g.tensor_tensor(xc, xc, xn[:, c % 2], ALU.add).then_inc(S_("x_own"), 1)
            end_phase(g, 1)
            layernorm(3)
            normalise(1)
            end_phase(g, 1)
            layernorm(4)
            g.memset(pd, 0.0).then_inc(S_("pd_zero"), 1)
            g.memset(keep, 1.0).then_inc(S_("g3"), 1)
            g.wait_ge(S_("g3"), 1)
            for u in range(2):
                ku = keep[64 * u:64 * u + 64, :]
                g.affine_select(out=ku, in_=ku, compare_op=ALU.is_ge, fill=0.0, base=0,
                                pattern=[[1, S]], channel_multiplier=-1).then_inc(S_("keep"), 1)
            end_phase(g, 1)
            layernorm(5)
            g.wait_ge(S_("lf_o"), 3 * CH - 1)
            g.memset(pd, 0.0).then_inc(S_("pd_zero"), 1)

        @block.tensor
        def _(pe):
            def norm_transposes(k):
                if k == 0:
                    pe.wait_ge(S_("consts"), 3)
                for c in range(CH):
                    pe.wait_ge(S_("ln_ev"), CH * k + c + 1)
                    for m in range(CT):
                        if m < own_tiles(k):
                            pe.wait_ge(S_("ln_xn"), tiles_before(k, c) + m + 1)
                        else:
                            pe.wait_ge(S_("ln_xng"), tiles_before(k, c, rest=True) + m - own_tiles(k) + 1)
                        tr = pe.transpose(ps(c % 2)[:, P * m:P * m + P], xn[:, c % 2, m, :], ident[:])
                    tr.then_inc(S_("ln_tr"), 1)

            def turns(layer, tb, odd, u, hh):
                if tb is None:
                    return
                b = 2 * tb + u
                if hh == 0:
                    pe.wait_ge(S_(f"xa_prob{layer}"), b + 3)
                pe.wait_ge(S_(f"xa_ptev{layer}"), 2 * b + hh + 1)
                for j in range(4):
                    mm = pe.transpose(pt_bank(layer, hh)[:, P * j:P * j + P],
                                      prob_slot(layer, odd, u)[:, 4 * hh + j, :], ident[:])
                mm.then_inc(S_(f"xa_pt{layer}"), 1)

            def xattn0():
                pe.wait_ge(ld["w0"], 16 * 5)
                for c in range(4):
                    for h in range(4 * c, 4 * c + 4):
                        mm = pe.matmul(ps(c)[:, CD * (h % 4):CD * (h % 4) + CD], wqT[:, h, :], wkT[:, h, :],
                                       start=True, stop=True)
                    mm.then_inc(S_("xa_m"), 1)
                    for h in range(4 * c, 4 * c + 4):
                        mm = pe.matmul(ps(4 + c)[0:CD, P * (h % 4):P * (h % 4) + P], wvT[:, h, :], wo[:, h, :],
                                       start=True, stop=True)
                    mm.then_inc(S_("xa_n"), 1)
                pe.wait_ge(ld["ctx"], 16)
                pe.wait_ge(S_("xa_w"), 8)
                pe.sem_inc(S_("xa_y0"), 2)
                pe.sem_inc(S_("xa_o0"), 4)
                q_out, sc_free = S_("xa_qev0"), S_("xa_exp0")

                def body(tq, ta, tb, f):
                    def queries(c):
                        if tq is None:
                            return
                        if q_bank(tq, c) == 6:
                            wait(pe, q_out, 4 * tq + c)
                        for h in range(4):
                            mm = pe.matmul(ps(q_bank(tq, c))[0:CD, P * h:P * h + P], M[:, 4 * c + h, :],
                                           xnT[:, bass.ds(tq * P, P)], start=True, stop=True)
                        mm.then_inc(S_("xa_q0"), 1)

                    def scores(u, hh):
                        if ta is None:
                            return
                        if hh == 0:
                            pe.wait_ge(q_out, 4 * ta + 4)
                        pe.wait_ge(sc_free, 4 * ta + 2 * u + hh + 1)
                        kv = ctxT[:, bass.ds((2 * ta + u) * KEYS, KEYS)]
                        for j in range(4 * hh, 4 * hh + 4):
                            mm = pe.matmul(bank[u][:, P * j:P * j + P],
                                           qmT[f][0:CD, u, 2 * j:2 * j + 2, :].rearrange("p a b -> p (a b)"), kv,
                                           start=True, stop=True)
                        mm.then_inc(S_("xa_sc0"), 1)

                    def values(u, hh):
                        if tb is None:
                            return
                        b = 2 * tb + u
                        slot = 2 * (1 - f) + u
                        if hh == 0:
                            pe.wait_ge(cx_in[slot], 16 * group[0] + 16)
                        pe.wait_ge(S_("xa_ptev0"), 2 * b + hh + 2)
                        pe.wait_ge(S_("xa_oev0"), 2 * b + hh + 1)
                        pe.matmul(ps(5)[0:CD, :], cx[:, slot, :], PT[u][:, 4 * hh:4 * hh + 4, :],
                                  start=True, stop=True).then_inc(S_("xa_o0"), 1)

                    def project():
                        if tb is None:
                            return
                        pe.wait_ge(S_("xa_add0"), tb + 1)
                        pe.wait_ge(S_("xa_oev0"), 4 * tb + 4)
                        for h in range(H):
                            r = slice(0, CD + 1 if h == 0 else CD)
                            if h == H // 2:
                                pe.wait_ge(S_("xa_oev0"), 4 * tb + 5)
                            mm = pe.matmul(ps(7)[:, 0:P], OT[1 - f][r, h, :], N[r, h, :], start=(h == 0),
                                           stop=(h == H - 1))
                        mm.then_inc(S_("xa_y0"), 1)

                    turns(0, tb, 1 - f, 0, 0)
                    queries(0)
                    scores(0, 0)
                    turns(0, tb, 1 - f, 0, 1)
                    scores(0, 1)
                    values(0, 0)
                    turns(0, tb, 1 - f, 1, 0)
                    queries(1)
                    values(0, 1)
                    scores(1, 0)
                    queries(2)
                    turns(0, tb, 1 - f, 1, 1)
                    scores(1, 1)
                    values(1, 0)
                    queries(3)
                    values(1, 1)
                    project()

                group = [0]
                body(0, None, None, 1)
                body(1, 0, None, 0)
                with pe.Fori(0, T // 2 - 1) as i:
                    group[0] = i
                    body(2 * i + 2, 2 * i + 1, 2 * i, 1)
                    body(2 * i + 3, 2 * i + 2, 2 * i + 1, 0)
                group[0] = T // 2 - 1
                body(None, T - 1, T - 2, 1)
                body(None, None, T - 1, 0)

            def xattn1():
                pe.wait_ge(S_("xa_mask"), 1)
                pe.sem_inc(S_("xa_y1"), 2)
                pe.sem_inc(S_("xa_o1"), 2)
                pe.sem_inc(S_("xa_pt1"), 4)
                group = [0]

                def body(tq, ta, tb, f):
                    def queries():
                        if tq is None:
                            return
                        wait(pe, S_("xa_add1"), tq - 1)
                        wait(pe, S_("xa_qev1"), tq)
                        pe.matmul(ps(7)[:, P:2 * P], wq1[:], xnT[:, bass.ds(tq * P, P)], start=True, stop=True).then_inc(S_("xa_q1"), 1)

                    def scores(u, hh):
                        if ta is None:
                            return
                        if hh == 0:
                            pe.wait_ge(S_("xa_qev1"), ta + 1)
                        pe.wait_ge(S_("xa_exp1"), 4 * ta + 2 * u + hh + 1)
                        pe.sem_inc(S_("xa_begun1"), 1)
                        off = (2 * ta + u) * KEYS
                        pe.matmul(bank[u][:, 512 * hh:512 * hh + 512], onesb[:],
                                  mrow[:, bass.ds(off, KEYS)][:, None, :].broadcast_to([1, 4, KEYS]),
                                  start=True, stop=False)
                        for j in range(4 * hh, 4 * hh + 4):
                            mm = pe.matmul(bank[u][:, P * j:P * j + P],
                                           qmT[f][:, u, 2 * j:2 * j + 2, :].rearrange("p a b -> p (a b)"),
                                           kTx[:, bass.ds(off, KEYS)], start=False, stop=(j % 4 == 3))
                        mm.then_inc(S_("xa_sc1"), 1)

                    def project_values(u):
                        if tb is None:
                            return
                        slot = 2 * (1 - f) + u
                        pe.wait_ge(cx_in[slot], 16 * (B // 4) + 16 * group[0] + 16)
                        pe.wait_ge(S_("xa_oev1"), 2 * tb + u + 1)
                        pe.matmul(ps(5)[:, 0:P], cxT[:, slot, :], wv1[:], start=True, stop=True).then_inc(S_("xa_v1"), 1)

                    def values(u):
                        if tb is None:
                            return
                        b = 2 * tb + u
                        pe.wait_ge(S_("xa_vev1"), b + 1)
                        pe.wait_ge(S_("xa_ptev1"), 2 * b + 4)
                        for g in range(4):
                            mm = pe.matmul(ps(5)[32 * g:32 * g + 32, 0:4 * S], vs[:, u, 32 * g:32 * g + 32],
                                           PT[u][:, 2 * g:2 * g + 2, :], start=True, stop=True)
                        mm.then_inc(S_("xa_o1"), 1)

                    def project():
                        if tb is None:
                            return
                        pe.wait_ge(S_("xa_add1"), tb + 1)
                        pe.wait_ge(S_("xa_oev1"), 2 * tb + 3)
                        if tq is not None:
                            pe.wait_ge(S_("xa_qev1"), tq + 1)
                        for m in range(4):
                            mm = pe.matmul(ps(7)[:, 0:P], Om[1 - f][:, m, :], wo1[:], start=(m == 0), stop=(m == 3))
                        mm.then_inc(S_("xa_y1"), 1)

                    project_values(0)
                    scores(0, 0)
                    turns(1, tb, 1 - f, 0, 0)
                    turns(1, tb, 1 - f, 0, 1)
                    scores(0, 1)
                    queries()
                    scores(1, 0)
                    values(0)
                    turns(1, tb, 1 - f, 1, 0)
                    turns(1, tb, 1 - f, 1, 1)
                    project_values(1)
                    scores(1, 1)
                    values(1)
                    project()

                body(0, None, None, 1)
                body(1, 0, None, 0)
                with pe.Fori(0, T // 2 - 1) as i:
                    group[0] = i
                    body(2 * i + 2, 2 * i + 1, 2 * i, 1)
                    body(2 * i + 3, 2 * i + 2, 2 * i + 1, 0)
                group[0] = T // 2 - 1
                body(None, T - 1, T - 2, 1)
                body(None, None, T - 1, 0)

            norm_transposes(0)
            end_phase(pe, 2)
            xattn0()
            end_phase(pe, 2)
            norm_transposes(1)
            pe.wait_ge(ld["scan"], 16 * 7)
            pe.wait_ge(S_("ln_ev"), 2 * CH + 2)
            pe.wait_ge(S_("ddp"), 1)
            for c in range(CH):
                xc = xnT[:, CW * c:CW * c + CW]
                if c >= 2:
                    pe.wait_ge(S_("sc_d0"), c - 1)
                pe.matmul(ps(c % 2), wx[:, 0:D], xc, start=True, stop=True).then_inc(S_("sc_dp"), 1)
                if c >= 2:
                    pe.wait_ge(S_("sc_r1"), c - 1)
                pe.matmul(ps(2 + c % 2)[0:32, :], wx[:, D:D + 32], xc, start=True, stop=True).then_inc(S_("sc_bc"), 1)
            for c in range(CH):
                pe.matmul(ps(4 + c), ddp[:], xnT[:, CW * c:CW * c + CW], start=True, stop=False)
            pe.wait_ge(S_("sc_hi"), CH)
            pe.wait_ge(S_("sc_mid2"), CH)
            pe.wait_ge(S_("sc_lo"), CH)
            pe.wait_ge(S_("g1"), 7)
            pe.wait_ge(S_("sc_t"), CH)
            pe.wait_ge(S_("sc_d0"), CH)

            def spread_b(k):
                n, c = divmod(k, CH)
                if k >= 2:
                    pe.wait_ge(S_("sc_bn"), k - 1)
                pe.matmul(ps(k % 2), bselb[0:96, n, :], bcs[:, CW * c:CW * c + CW], start=True, stop=True).then_inc(S_("sc_b"), 1)

            spread_b(0)
            spread_b(1)
            for k in range(CH * NS):
                n, c = divmod(k, CH)
                if k >= 2:
                    pe.wait_ge(S_("sc_hc"), k - 1)
                pe.matmul(ps(2 + k % 2), bselb[0:96, 16 + n, :], bcs[:, CW * c:CW * c + CW], start=True, stop=True).then_inc(S_("sc_c"), 1)
                if k + 2 < CH * NS:
                    spread_b(k + 2)
                if k >= 2:
                    pe.matmul(ps(4 + (k - 2) % 4), ident[:], hc[k % 2], start=False, stop=(k - 2) // 4 == NS - 1).then_inc(S_("sc_acc"), 1)
            for k in range(4 * NS, 4 * NS + 2):
                pe.wait_ge(S_("sc_hc"), k - 1)
                pe.matmul(ps(4 + (k - 2) % 4), ident[:], hc[k % 2], start=False, stop=True).then_inc(S_("sc_acc"), 1)
            for c in range(CH):
                pe.wait_ge(S_("sc_yT"), c + 1)
                for t in range(CT * c, CT * c + CT):
                    mm = pe.matmul(ps(c)[:, P * (t % CT):P * (t % CT) + P], yT[:, P * t:P * t + P], wout[:],
                                   start=True, stop=True)
                mm.then_inc(S_("sc_out"), 1)
            end_phase(pe, 2)
            norm_transposes(2)
            pe.wait_ge(S_("ln_ev"), 3 * CH + 2)
            pe.wait_ge(ld["moe"], 48)
            pe.matmul(ps(7)[0:B, 0:E], xnT[:, 0:2048:S], wrT[:], start=True, stop=True).then_inc(S_("me_lg"), 1)
            pe.wait_ge(ld["l1x"], 16 * 4)

            def keys(first, last):
                for c in range(first, last):
                    if c >= 2:
                        pe.wait_ge(S_("xa_kev"), c - 1)
                    pe.matmul(ps((0, 6)[c % 2]), wk1[:], ctxT[:, CW * c:CW * c + CW], start=True,
                              stop=True).then_inc(S_("xa_k"), 1)

            keys(0, 4)
            pe.wait_ge(S_("me_gate"), 1)
            pe.transpose(ps(7)[0:E, 64:64 + B], gate[:], ident[0:B, 0:B]).then_inc(S_("me_gT"), 1)
            keys(4, 6)
            pe.wait_ge(S_("me_gTs"), 1)
            for k in range(4):
                mm = pe.matmul(ps(7)[:, 128 + B * k:128 + B * k + B], esel[:, k, :], gT[:], start=True, stop=True)
            mm.then_inc(S_("me_gx"), 1)
            keys(6, B * KEYS // CW)
            pe.wait_ge(S_("xa_kev"), 8)

            def mids(c):
                for k in range(4):
                    n = 4 * c + k
                    if n >= 2:
                        pe.wait_ge(S_("me_mev"), n - 1)
                    pe.matmul(ps(n % 2), aT[:, k, :], xnT[:, CW * c:CW * c + CW], start=True, stop=True).then_inc(S_("me_m"), 1)

            mids(0)
            for c in range(CH):
                if c + 1 < CH:
                    mids(c + 1)
                pe.wait_ge(S_("me_mev"), 4 * c + 4)
                for t in range(CT):
                    for k in range(4):
                        mm = pe.matmul(ps(2 + c)[:, P * t:P * t + P], midT[c % 2][:, k, P * t:P * t + P], bw[:, k, :],
                                       start=(k == 0), stop=(k == 3))
                mm.then_inc(S_("me_y"), 1)
            end_phase(pe, 2)
            norm_transposes(3)
            pe.wait_ge(S_("ln_ev"), 4 * CH + 2)
            xattn1()
            end_phase(pe, 2)

            def own_scores(half):
                for b in range(B // 2 * half, B // 2 * (half + 1)):
                    t, u = divmod(b, 2)
                    mm = pe.matmul(ps(half)[64 * u:64 * u + 64, S * (t % 8):S * (t % 8) + S], qT[:, S * b:S * b + S],
                                   kT[:, S * b:S * b + S], start=True, stop=True)
                mm.then_inc(S_("at_sc"), 1)

            def attend(k):
                for half in range(2):
                    pe.wait_ge(S_("at_p"), 4 * k + 2 * half + 2)
                    for c in (2 * half, 2 * half + 1):
                        for t in range(CT):
                            mm = pe.transpose(ps(2 + c)[:, P * t:P * t + P], pd[:, CT * c + t, :], ident[:])
                        mm.then_inc(S_("at_pt"), 1)
                    for c in (2 * half, 2 * half + 1):
                        pe.wait_ge(S_("at_ptev"), CH * k + c + 1)
                        if c >= 2:
                            pe.wait_ge(S_("x_add"), CH * (2 + k) + c - 1)
                        for t in range(CT):
                            mm = pe.matmul(ps(6 + c % 2)[:, P * t:P * t + P], pdT[:, CT * c + t, :], v[:, CT * c + t, :],
                                           start=True, stop=True)
                        mm.then_inc(S_("at_y"), 1)

            norm_transposes(4)
            pe.wait_ge(S_("ln_ev"), 5 * CH + 2)
            pe.wait_ge(ld["wqkv"], 16)
            for c in range(CH):
                for w in range(2):
                    n = 2 * c + w
                    if n >= 2:
                        pe.wait_ge(S_("sa_qk"), n - 1)
                    pe.matmul(ps(6 + n % 2), wqkv[:, D * w:D * w + D], xnT[:, CW * c:CW * c + CW], start=True,
                              stop=True).then_inc(S_("sa_q"), 1)
                if c == CH // 2:
                    pe.wait_ge(S_("sa_qk"), CH)
                    own_scores(0)
            pe.wait_ge(S_("sa_qk"), 2 * CH)
            own_scores(1)
            for c in range(CH):
                for t in range(CT):
                    mm = pe.matmul(ps(2 + c)[:, P * t:P * t + P], xnT[:, CW * c + P * t:CW * c + P * t + P],
                                   wqkv[:, 2 * D:3 * D], start=True, stop=True)
                mm.then_inc(S_("sa_v"), 1)
            pe.wait_ge(S_("sa_vev"), CH)
            attend(0)
            end_phase(pe, 2)
            norm_transposes(5)
            pe.wait_ge(S_("ln_ev"), 6 * CH + 2)
            pe.wait_ge(ld["tree"], 16 * 20)
            pe.wait_ge(S_("tr_path"), 1)
            for c in range(CH):
                pe.matmul(ps(4 + c)[0:96, :], nw[:], xnT[:, CW * c:CW * c + CW], start=True, stop=True).then_inc(S_("tr_sc"), 1)

            def paths(c):
                pe.wait_ge(S_("tr_dec"), c + 1)
                pe.matmul(ps(4 + c)[0:96, :], pathb[:], decb[c % 2][:], start=True, stop=True).then_inc(S_("tr_z"), 1)

            def hidden(g2, blocks=range(NB)):
                c, w = divmod(g2, 3)
                for k in blocks:
                    n = NB * g2 + k
                    if n >= 4:
                        pe.wait_ge(S_("lf_h"), n - 3)
                    pe.matmul(ps(n % 4), w1[:, w, P * k:P * k + P], xnT[:, CW * c:CW * c + CW], start=True,
                              stop=True).then_inc(S_("lf_pre"), 1)

            def leaves_out(g2):
                c, w = divmod(g2, 3)
                r = slice(32 * w, 32 * w + LV)
                pe.wait_ge(S_("lf_m"), 2 * (g2 + 1))
                if g2 == 0:
                    pe.wait_ge(S_("tr_sel"), 2 * CH)
                if g2 >= 2:
                    pe.wait_ge(S_("lf_oev"), g2 - 1)
                if w < 2:
                    o = ps(4 + g2 % 2)
                    pe.matmul(o, b2[r, :], selT[r, CW * c:CW * c + CW], start=True, stop=False)
                    for k in range(NB):
                        mm = pe.matmul(o, w2[:, w, k, :], hT[g2 % 2][:, k, :], start=False, stop=(k == NB - 1))
                else:
                    for t in range(CT):
                        o = ps(4 + g2 % 2)[:, P * t:P * t + P]
                        tt = CW * c + P * t
                        pe.matmul(o, selT[r, tt:tt + P], b2[r, :], start=True, stop=False)
                        for k in range(NB):
                            mm = pe.matmul(o, hT[g2 % 2][:, k, P * t:P * t + P], w2[:, w, k, :], start=False,
                                           stop=(k == NB - 1))
                mm.then_inc(S_("lf_o"), 1)

            for c in range(CH):
                hidden(0, (2 * c, 2 * c + 1))
                paths(c)
            for g2 in range(3 * CH + 1):
                if 0 < g2 < 3 * CH:
                    hidden(g2)
                if g2 == 3 * CH:
                    pe.wait_ge(S_("lf_oev"), 3 * CH - 1)
                    pe.wait_ge(S_("lf_h"), NB * 3 * CH)
                    own_scores(0)
                    own_scores(1)
                if g2:
                    leaves_out(g2 - 1)
            pe.wait_ge(S_("lf_oev"), 3 * CH)
            attend(1)

        @block.vector
        def _(dve):
            def statistics(t):
                tile = bass.ds(t, 1)
                dve.bn_stats(st6[:, tile, :].rearrange("p a b -> p (a b)"),
                             x[:, tile, :].rearrange("p a b -> p (a b)")).then_inc(S_("ln_st"), 1)

            def add_chunk(c, y):
                xt = x[:, CT * c:CT * c + CT, :].rearrange("p a b -> p (a b)")
                dve.tensor_tensor(xt, y, xt, ALU.add).then_inc(S_("x_add"), 1)
                adds[0] += 1
                dve.wait_ge(S_("x_add"), adds[0])
                for t in range(CT * c, CT * c + CT):
                    statistics(t)

            adds = [0]

            def layernorm(k):
                me, ve, mo, vo = (st6[:, :, n] for n in (1, 2, 4, 5))
                dve.wait_ge(S_("ln_st"), T * (k + 1))
                dve.tensor_tensor(lnv[:, 0], me, mo, ALU.subtract).then_inc(S_("ln_a"), 1)
                dve.tensor_tensor(lnv[:, 1], ve, vo, ALU.add).then_inc(S_("ln_a"), 1)
                dve.tensor_tensor(lnv[:, 2], me, mo, ALU.add).then_inc(S_("ln_a"), 1)
                dve.wait_ge(S_("ln_a"), 5 * k + 3)
                dve.tensor_tensor(lnv[:, 0], lnv[:, 0], lnv[:, 0], ALU.mult).then_inc(S_("ln_a"), 1)
                dve.tensor_scalar(mean[:], lnv[:, 2], 0.5, None, ALU.mult).then_inc(S_("ln_a"), 1)
                dve.wait_ge(S_("ln_a"), 5 * k + 5)
                dve.scalar_tensor_tensor(out=lnv[:, 1], in0=lnv[:, 1], scalar=4.0 / D, in1=lnv[:, 0],
                                         op0=ALU.mult, op1=ALU.add).then_inc(S_("ln_mv"), 1)
                dve.wait_ge(S_("ln_std"), k + 1)
                dve.reciprocal(rstd[:], std[:]).then_inc(S_("ln_r"), 1)
                dve.wait_ge(S_("ln_r"), k + 1)
                for c in range(CH):
                    dve.wait_ge(S_("ln_ev"), CH * k + c + 1)
                    for m in range(own_tiles(k)):
                        t = CT * c + m
                        dve.tensor_scalar(xn[:, c % 2, m, :], x[:, t, :], mean[:, t:t + 1], rstd[:, t:t + 1],
                                          ALU.subtract, ALU.mult).then_inc(S_("ln_xn"), 1)

            def xattn(layer):
                n_q, n_o = ((4, 2), (1, 1))[layer]

                def sl(name):
                    return S_(f"xa_{name}{layer}")

                if layer == 0:
                    for n in range(2):
                        dve.memset(OT[n][CD:CD + 1, 0, :], 1.0)
                    for c in range(4):
                        dve.wait_ge(S_("xa_m"), c + 1)
                        dve.tensor_scalar(M[:, 4 * c:4 * c + 4, :], ps(c)[:, 0:4 * CD].rearrange("p (a b) -> p a b", b=CD),
                                          XA_SCALE[0], None, ALU.mult).then_inc(S_("xa_w"), 1)
                        dve.wait_ge(S_("xa_n"), c + 1)
                        dve.tensor_copy(N[0:CD, 4 * c:4 * c + 4, :],
                                        ps(4 + c)[0:CD, :].rearrange("p (a b) -> p a b", b=P)).then_inc(S_("xa_w"), 1)
                else:
                    dve.wait_ge(S_("hmask"), 1)
                    dve.tensor_reduce(gmask[:], hmask[:].rearrange("p (g m) -> p m g", m=4), AX.X, ALU.add).then_inc(S_("gmask"), 1)
                    dve.wait_ge(S_("gmask"), 1)
                    dve.tensor_scalar(hmask[:], hmask[:], XA_SCALE[1], None, ALU.mult).then_inc(S_("gmask"), 1)
                    dve.wait_ge(ld["msk"], 16)
                    dve.tensor_scalar(mrow, msk8, -1.0, BIG, ALU.add, ALU.mult).then_inc(S_("xa_mask"), 1)
                    dve.wait_ge(S_("gmask"), 2)
                dve.sem_inc(sl("oev"), 1)
                dve.sem_inc(sl("add"), 1)

                def body(tq, ta, tb, f):
                    def queries(c):
                        if tq is None or c >= n_q:
                            return
                        dve.wait_ge(sl("q"), n_q * tq + c + 1)
                        wait(dve, sl("sc"), 4 * tq - 4)
                        if layer == 0:
                            dve.tensor_copy(qmT[1 - f][0:CD, :, 4 * c:4 * c + 4, :].rearrange("p u h t -> p h u t"),
                                            ps(q_bank(tq, c))[0:CD, :].rearrange("p (h u t) -> p h u t", u=2,
                                                                                 t=S)).then_inc(sl("qev"), 1)
                        else:
                            q = ps(7)[:, P:2 * P].rearrange("p (u t) -> p u t", t=S)
                            dve.tensor_tensor(qmT[1 - f], q[:, :, None, :].broadcast_to([P, 2, H, S]),
                                              hmask[:, None, :, None].broadcast_to([P, 2, H, S]), ALU.mult).then_inc(sl("qev"), 1)

                    def maxima(u, hh):
                        if ta is None:
                            return
                        dve.wait_ge(sl("sc"), 4 * ta + 2 * u + hh + 1)
                        dve.tensor_reduce(nmx[:, u, 4 * hh:4 * hh + 4], ps(2 * u + hh).rearrange("p (j k) -> p j k", k=KEYS),
                                          AX.X, ALU.max, negate=True).then_inc(sl("mx"), 1)

                    def reciprocals(t, odd, u):
                        if t is None:
                            return
                        dve.wait_ge(sl("exp"), 4 * t + 2 * u + 6)
                        dve.wait_ge(sl("prob"), 2 * t + u + 1)
                        dve.reciprocal(rs[:, 2 * odd + u, :], sm[:, 2 * odd + u, :]).then_inc(sl("recip"), 1)

                    def outputs(u, hh):
                        if tb is None or hh >= n_o:
                            return
                        b = 2 * tb + u
                        dve.wait_ge(sl("o"), (2 * b + hh + 5) if layer == 0 else b + 3)
                        if u == 0 and hh == 0:
                            dve.wait_ge(sl("y"), tb + 1)
                        if layer == 0:
                            dve.tensor_copy(OT[1 - f][0:CD, 8 * hh:8 * hh + 8, 64 * u:64 * u + 64],
                                            ps(5)[0:CD, :].rearrange("p (h t) -> p h t", t=S)).then_inc(sl("oev"), 1)
                        else:
                            dve.tensor_tensor(Om[1 - f][:, :, 64 * u:64 * u + 64],
                                              ps(5)[:, 0:4 * S].rearrange("p (h t) -> p h t", t=S),
                                              gmask[:, :, None].broadcast_to([P, 4, S]), ALU.mult).then_inc(sl("oev"), 1)

                    def own_values(u):
                        if tb is None or layer == 0:
                            return
                        dve.wait_ge(sl("v"), 2 * tb + u + 1)
                        dve.wait_ge(sl("o"), 2 * tb + u + 1)
                        dve.tensor_copy(vs[:, u, :], ps(5)[:, 0:P]).then_inc(sl("vev"), 1)

                    def add():
                        if tb is None:
                            return
                        dve.wait_ge(sl("y"), tb + 3)
                        xt = x[:, bass.ds(tb, 1), :].rearrange("p a b -> p (a b)")
                        dve.tensor_tensor(xt, ps(7)[:, 0:P], xt, ALU.add).then_inc(sl("add"), 1)
                        dve.wait_ge(sl("add"), tb + 2)
                        statistics(tb)

                    for u in range(2):
                        own_values(u)
                        reciprocals((tb, ta)[u], (1 - f, f)[u], 1 - u)
                        if layer == 0:
                            queries(2 * u)
                        maxima(u, 0)
                        maxima(u, 1)
                        if layer == 1:
                            queries(u)
                        outputs(u, 0)
                        if layer == 0:
                            queries(2 * u + 1)
                        outputs(u, 1)
                    add()

                body(0, None, None, 1)
                body(1, 0, None, 0)
                with dve.Fori(0, T // 2 - 1) as i:
                    body(2 * i + 2, 2 * i + 1, 2 * i, 1)
                    body(2 * i + 3, 2 * i + 2, 2 * i + 1, 0)
                body(None, T - 1, T - 2, 1)
                body(None, None, T - 1, 0)

            for c in range(CH):
                dve.wait_ge(ld[f"x{c}"], 16)
                for t in range(CT * c, CT * c + CT):
                    statistics(t)
            layernorm(0)
            end_phase(dve, 3)
            xattn(0)
            end_phase(dve, 3)
            layernorm(1)
            dve.wait_ge(ld["scan"], 16 * 7)
            dve.tensor_scalar(ddp[:], ident[:], dp[:, 0:1], None, ALU.mult).then_inc(S_("ddp"), 1)
            dve.wait_ge(S_("ln_ev"), 2 * CH + 2)

            def third(c):
                dve.wait_ge(S_("sc_mid"), c + 1)
                dve.wait_ge(S_("sc_r1"), c + 1)
                dve.tensor_tensor(bcs[64:96, CW * c:CW * c + CW], bcr[c % 2], bcm[c % 2], ALU.subtract).then_inc(S_("sc_lo"), 1)

            for c in range(CH):
                cc = slice(CW * c, CW * c + CW)
                dve.wait_ge(S_("sc_t"), c + 1)
                dve.tensor_scalar(delta[:, cc], ps(c % 2), bx[:, 0:1], 0.0, ALU.add, ALU.max).then_inc(S_("sc_d0"), 1)
                dve.wait_ge(S_("sc_hi"), c + 1)
                if c >= 2:
                    dve.wait_ge(S_("sc_mid"), c - 1)
                    dve.wait_ge(S_("sc_mid2"), c - 1)
                    dve.wait_ge(S_("sc_lo"), c - 1)
                dve.scalar_tensor_tensor(out=bcr[c % 2], in0=ps(2 + c % 2)[0:32, :], scalar=bbc[:, 0:1],
                                         in1=bcs[0:32, cc], op0=ALU.add, op1=ALU.subtract).then_inc(S_("sc_r1"), 1)
                dve.wait_ge(S_("sc_r1"), c + 1)
                dve.tensor_copy(bcs[32:64, cc], bcr[c % 2]).then_inc(S_("sc_mid2"), 1)
                if c:
                    third(c - 1)
            third(CH - 1)
            for c in range(CH):
                cc = slice(CW * c, CW * c + CW)
                dve.wait_ge(S_("sc_ln"), c + 1)
                dve.wait_ge(S_("sc_d0"), c + 1)
                dve.tensor_tensor(delta[:, cc], delta[:, cc], tmp[c], ALU.add).then_inc(S_("sc_delta"), 1)
                dve.wait_ge(S_("sc_delta"), c + 1)
                dve.tensor_tensor(du[:, cc], delta[:, cc], xnT[:, cc], ALU.mult).then_inc(S_("sc_du"), 1)
            for k in range(CH * NS + 1):
                n, c = divmod(k, CH)
                if k < CH * NS:
                    dve.wait_ge(S_("sc_bx"), k + 1)
                    dve.wait_ge(S_("sc_abar"), k + 1)
                    if k >= 2:
                        dve.wait_ge(S_("sc_hc"), k - 1)
                    dve.tensor_tensor_scan(hs[k % 2], abar[n % 2][:, CW * c:CW * c + CW], bxs[k % 4], 0.0, ALU.mult,
                                           ALU.add).then_inc(S_("sc_h"), 1)
                if k:
                    m = k - 1
                    dve.wait_ge(S_("sc_c"), m + 1)
                    dve.wait_ge(S_("sc_h"), m + 1)
                    if m >= 2:
                        dve.wait_ge(S_("sc_acc"), m - 1)
                    dve.tensor_tensor(hc[m % 2], ps(2 + m % 2), hs[m % 2], ALU.mult).then_inc(S_("sc_hc"), 1)
            dve.wait_ge(S_("x_bias"), 1)
            for c in range(CH):
                dve.wait_ge(S_("sc_out"), c + 1)
                add_chunk(c, ps(c))
            end_phase(dve, 3)
            layernorm(2)
            link = [0]

            def chain(ins):
                ins.then_inc(S_("chain"), 1)
                link[0] += 1
                dve.wait_ge(S_("chain"), link[0])

            dve.wait_ge(S_("me_lg"), 1)
            chain(dve.tensor_copy(lg[:], ps(7)[0:B, 0:E]))
            li = lg[:, :, None].broadcast_to([B, E, E])
            lj = lg[:, None, :].broadcast_to([B, E, E])
            chain(dve.tensor_tensor(eq[:], lj, li, ALU.is_equal))
            dve.wait_ge(S_("g1"), 7)
            chain(dve.tensor_tensor(eq[:], eq[:], tri[:], ALU.mult))
            chain(dve.tensor_tensor(gt[:], lj, li, ALU.is_gt))
            chain(dve.tensor_tensor(gt[:], gt[:], eq[:], ALU.add))
            chain(dve.tensor_reduce(rank[:], gt[:], AX.X, ALU.add))
            chain(dve.tensor_scalar(rank[:], rank[:], 1.5, None, ALU.is_lt))
            chain(dve.tensor_reduce(lmx[:, 0:1], lg[:], AX.X, ALU.max))
            chain(dve.tensor_scalar(lg[:], lg[:], lmx[:, 0:1], None, ALU.subtract))
            dve.sem_inc(S_("me_lsub"), 1)
            dve.wait_ge(S_("me_exp"), 1)
            chain(dve.tensor_tensor(gate[:], gate[:], rank[:], ALU.mult))
            chain(dve.tensor_reduce(lmx[:, 1:2], gate[:], AX.X, ALU.add))
            chain(dve.reciprocal(lmx[:, 1:2], lmx[:, 1:2]))
            dve.tensor_scalar(gate[:], gate[:], lmx[:, 1:2], None, ALU.mult).then_inc(S_("me_gate"), 1)
            dve.wait_ge(S_("me_gT"), 1)
            dve.tensor_copy(gT[:], ps(7)[0:E, 64:64 + B]).then_inc(S_("me_gTs"), 1)
            dve.wait_ge(S_("me_gx"), 1)
            chain(dve.tensor_copy(gx[:], ps(7)[:, 128:128 + 4 * B].rearrange("p (k b) -> p k b", b=B)))
            for c in range(CH):
                for k in range(4):
                    n = 4 * c + k
                    dve.wait_ge(S_("me_m"), n + 1)
                    if k == 0 and c >= 2:
                        dve.wait_ge(S_("me_y"), c - 1)
                    dve.tensor_tensor(midT[c % 2][:, k, :].rearrange("p (b s) -> p b s", s=S),
                                      ps(n % 2).rearrange("p (b s) -> p b s", s=S),
                                      gx[:, k, 8 * c:8 * c + 8, None].broadcast_to([P, 8, S]), ALU.mult).then_inc(S_("me_mev"), 1)
            for c in range(CH):
                dve.wait_ge(S_("me_y"), c + 1)
                dve.wait_ge(S_("x_own"), min(c + 3, 4))
                add_chunk(c, ps(2 + c))
            end_phase(dve, 3)
            layernorm(3)
            xattn(1)
            end_phase(dve, 3)

            def softmax(k):
                for c in range(2):
                    h = slice(8 * c, 8 * c + 8)
                    shape = [P, 8, S]
                    own = ps(c).rearrange("p (t s) -> p t s", s=S)
                    dve.wait_ge(S_("at_sc"), 2 * k + c + 1)
                    if k == 0:
                        if c == 0:
                            dve.wait_ge(S_("keep"), 2)
                        chain(dve.tensor_tensor(sc[:, h], own, keep[:, None, :].broadcast_to(shape), ALU.mult))
                        chain(dve.tensor_scalar(eqz[:, h], sc[:, h], 0.0, MASK_NEG / D_SCALE, ALU.is_equal, ALU.mult))
                        chain(dve.tensor_tensor(sc[:, h], sc[:, h], eqz[:, h], ALU.add))
                        own = sc[:, h]
                    chain(dve.tensor_reduce(amx[:, h], own, AX.X, ALU.max))
                    dve.tensor_tensor(sc[:, h], own, amx[:, h, None].broadcast_to(shape), ALU.subtract).then_inc(S_("at_sub"), 1)
                for c in range(2):
                    h = slice(8 * c, 8 * c + 8)
                    dve.wait_ge(S_("at_exp"), 2 * k + c + 1)
                    chain(dve.tensor_reduce(asm[:, h], sc[:, h], AX.X, ALU.add))
                    chain(dve.reciprocal(ars[:, h], asm[:, h]))
                    dve.wait_ge(S_("pd_zero"), k + 1)
                    for u in range(2):
                        r = slice(64 * u, 64 * u + 64)
                        dve.tensor_tensor(pd[r, h, 64 * u:64 * u + 64], sc[r, h], ars[r, h, None].broadcast_to([64, 8, S]),
                                          ALU.mult).then_inc(S_("at_p"), 1)

            def add_values(k):
                for c in range(CH):
                    dve.wait_ge(S_("at_y"), CH * k + c + 1)
                    if k == 0:
                        add_chunk(c, ps(6 + c % 2))
                    else:
                        xt = x[:, CT * c:CT * c + CT, :].rearrange("p a b -> p (a b)")
                        dve.tensor_tensor(xt, ps(6 + c % 2), xt, ALU.add).then_inc(S_("x_add"), 1)

            layernorm(4)
            softmax(0)
            add_values(0)
            end_phase(dve, 3)
            dve.wait_ge(ld["tree"], 16 * 20)
            dve.tensor_copy(pathb[:], path[:]).then_inc(S_("tr_path"), 1)
            layernorm(5)
            for c in range(CH + 1):
                if c < CH:
                    dve.wait_ge(S_("tr_sc"), c + 1)
                    if c >= 2:
                        dve.wait_ge(S_("tr_z"), c - 1)
                    dve.tensor_scalar(decb[c % 2][:], ps(4 + c)[0:96, :], nb[:, 0:1], 0.0, ALU.add,
                                      ALU.is_ge).then_inc(S_("tr_dec"), 1)
                if c:
                    cc = slice(CW * (c - 1), CW * c)
                    dve.wait_ge(S_("tr_z"), c)
                    if c >= 3:
                        dve.wait_ge(leaf_out[(c - 1) % 2], 16)
                    dve.tensor_scalar(selT[:, cc], ps(3 + c)[0:96, :], rights[:, 0:1], None, ALU.is_equal).then_inc(S_("tr_sel"), 1)
                    dve.tensor_scalar(selb[(c - 1) % 2], ps(3 + c)[0:96, :], rights[:, 0:1], None,
                                      ALU.is_equal).then_inc(S_("tr_sel"), 1)
            for g2 in range(3 * CH + 1):
                if g2 < 3 * CH:
                    dve.wait_ge(selx_in[g2 % 2], 32 * (g2 // 2 + 1))
                    for half in range(2):
                        kk = slice(NB // 2 * half, NB // 2 * (half + 1))
                        dve.wait_ge(S_("lf_h"), NB * g2 + kk.stop)
                        dve.tensor_tensor(hT[g2 % 2][:, kk, :], hT[g2 % 2][:, kk, :], selx[g2 % 2][:, kk, :],
                                          ALU.mult).then_inc(S_("lf_m"), 1)
                if g2 == 3 * CH:
                    dve.wait_ge(S_("lf_o"), 3 * CH - 1)
                    softmax(1)
                if g2:
                    c, w = divmod(g2 - 1, 3)
                    dve.wait_ge(S_("lf_o"), g2)
                    o = ps(4 + (g2 - 1) % 2)
                    cc = slice(CW * c, CW * c + CW)
                    if w < 2:
                        dve.tensor_copy((qT, kT)[w][:, cc], o).then_inc(S_("lf_oev"), 1)
                    else:
                        dve.tensor_copy(v[:, CT * c:CT * c + CT, :], o.rearrange("p (a b) -> p a b", b=D)).then_inc(S_("lf_oev"), 1)
            add_values(1)

        @block.scalar
        def _(act):
            def layernorm(k):
                if k == 0:
                    act.wait_ge(S_("consts"), 3)
                    act.sem_inc(S_("ln_ev"), 2)
                act.activation(warm[:, k:k + 1], epsc[:, 0:1], ACT.Sqrt)
                act.wait_ge(S_("ln_mv"), k + 1)
                act.activation(std[:], lnv[:, 1], ACT.Sqrt, bias=epsc[:, 0:1], scale=0.25).then_inc(S_("ln_std"), 1)
                if k < 5:
                    act.activation(warm[:, 8 + k:9 + k], epsc[:, 0:1], ACT.Exp)
                for c in range(CH):
                    act.wait_ge(S_("ln_tr"), CH * k + c + 1)
                    act.copy(xnT[:, c * CW:c * CW + CW], ps(c % 2)).then_inc(S_("ln_ev"), 1)

            def xattn(layer):
                def sl(name):
                    return S_(f"xa_{name}{layer}")

                act.sem_inc(sl("ptev"), 1 + layer)
                act.sem_inc(sl("exp"), 4)

                def body(ta, tb, odd):
                    def exponentials(u, hh):
                        if ta is None:
                            return
                        b = 2 * ta + u
                        act.wait_ge(sl("mx"), 2 * b + hh + 1)
                        wait(act, sl("pt"), 2 * b - 3 + hh)
                        for j in range(4 * hh, 4 * hh + 4):
                            ex = act.activation(prob_slot(layer, odd, u)[:, j, :], bank[u][:, P * j:P * j + P], ACT.Exp,
                                                bias=nmx[:, u, j:j + 1],
                                                accum_out=sm[:, 2 * odd + u, j:j + 1])
                        ex.then_inc(sl("exp"), 1)

                    def turned(u, hh):
                        if tb is None:
                            return
                        b = 2 * tb + u
                        act.wait_ge(sl("pt"), 2 * b + hh + 1 + 4 * layer)
                        act.wait_ge(sl("o"), (2 * b + hh + 1) if layer == 0 else b + 1)
                        act.copy(PT[u][:, 4 * hh:4 * hh + 4, :],
                                 pt_bank(layer, hh).rearrange("p (j r) -> p j r", r=P)).then_inc(sl("ptev"), 1)

                    for u in range(2):
                        turned(u, 0)
                        turned(u, 1)
                        exponentials(u, 0)
                        exponentials(u, 1)

                body(0, None, 0)
                with act.Fori(0, T // 2 - 1) as i:
                    body(2 * i + 1, 2 * i, 1)
                    body(2 * i + 2, 2 * i + 1, 0)
                body(T - 1, T - 2, 1)
                body(None, T - 1, 0)

            layernorm(0)
            end_phase(act, 4)
            xattn(0)
            end_phase(act, 4)
            layernorm(1)
            act.wait_ge(ld["scan"], 16 * 7)
            act.activation(amin[:], alog[:], ACT.Exp).then_inc(S_("sc_a"), 1)
            act.wait_ge(S_("sc_a"), 1)
            act.mul(amin[:], amin[:], -1.0).then_inc(S_("sc_a"), 1)
            def second(c):
                act.wait_ge(S_("sc_r1"), c + 1)
                if c >= 2:
                    act.wait_ge(S_("sc_lo"), c - 1)
                act.copy(bcm[c % 2], bcr[c % 2]).then_inc(S_("sc_mid"), 1)

            for c in range(CH):
                act.wait_ge(S_("sc_dp"), c + 1)
                act.activation(tmp[c], ps(c % 2), ACT.Abs, bias=bx[:, 0:1]).then_inc(S_("sc_t"), 1)
                act.wait_ge(S_("sc_bc"), c + 1)
                act.activation(bcs[0:32, CW * c:CW * c + CW], ps(2 + c % 2)[0:32, :], ACT.Identity,
                               bias=bbc[:, 0:1]).then_inc(S_("sc_hi"), 1)
                if c:
                    second(c - 1)
            second(CH - 1)
            for c in range(CH):
                act.wait_ge(S_("sc_t"), CH)
                act.activation(tmp[c], tmp[c], ACT.Exp, scale=-1.0).then_inc(S_("sc_e"), 1)
            for c in range(CH):
                act.wait_ge(S_("sc_e"), c + 1)
                act.activation(tmp[c], tmp[c], ACT.Ln, bias=onec[:, 0:1]).then_inc(S_("sc_ln"), 1)

            def decay(k):
                n, c = divmod(k, CH)
                cc = slice(CW * c, CW * c + CW)
                if k < CH:
                    act.wait_ge(S_("sc_delta"), k + 1)
                if k >= 2 * CH:
                    act.wait_ge(S_("sc_h"), k - 2 * CH + 1)
                act.activation(abar[n % 2][:, cc], delta[:, cc], ACT.Exp, scale=amin[:, n:n + 1]).then_inc(S_("sc_abar0"), 1)

            act.wait_ge(S_("sc_a"), 2)
            for c in range(LEAD):
                decay(c)
            act.wait_ge(S_("sc_delta"), CH)
            for k in range(CH * NS):
                act.wait_ge(S_("sc_b"), k + 1)
                if k >= 2:
                    act.wait_ge(S_("sc_bx"), k - 1)
                act.copy(bn[k % 2], ps(k % 2)).then_inc(S_("sc_bn"), 1)
                if k + LEAD < CH * NS:
                    decay(k + LEAD)
            for c in range(CH):
                act.wait_ge(S_("sc_acc"), 4 * (NS - 1) + c + 1)
                act.copy(yT[:, CW * c:CW * c + CW], ps(4 + c)).then_inc(S_("sc_yT"), 1)
            end_phase(act, 4)
            layernorm(2)
            def keys(first, last):
                for c in range(first, last):
                    act.wait_ge(S_("xa_k"), c + 1)
                    act.copy(kTx[:, CW * c:CW * c + CW], ps((0, 6)[c % 2])).then_inc(S_("xa_kev"), 1)

            keys(0, 1)
            act.wait_ge(S_("me_lsub"), 1)
            act.activation(gate[:], lg[:], ACT.Exp).then_inc(S_("me_exp"), 1)
            keys(1, B * KEYS // CW)
            end_phase(act, 4)
            layernorm(3)
            xattn(1)
            end_phase(act, 4)

            def attend(k):
                for c in range(2):
                    h = slice(8 * c, 8 * c + 8)
                    act.wait_ge(S_("at_sub"), 2 * k + c + 1)
                    act.activation(sc[:, h], sc[:, h], ACT.Exp, scale=D_SCALE).then_inc(S_("at_exp"), 1)
                    if k == 0 and c == 0:
                        for m in range(CH):
                            act.wait_ge(S_("sa_v"), m + 1)
                            act.copy(v[:, CT * m:CT * m + CT, :],
                                     ps(2 + m).rearrange("p (a b) -> p a b", b=D)).then_inc(S_("sa_vev"), 1)
                for c in range(CH):
                    act.wait_ge(S_("at_pt"), CH * k + c + 1)
                    act.copy(pdT[:, CT * c:CT * c + CT, :], ps(2 + c).rearrange("p (a b) -> p a b", b=P)).then_inc(S_("at_ptev"), 1)

            layernorm(4)
            for n in range(2 * CH):
                c, w = divmod(n, 2)
                act.wait_ge(S_("sa_q"), n + 1)
                act.copy((qT, kT)[w][:, CW * c:CW * c + CW], ps(6 + n % 2)).then_inc(S_("sa_qk"), 1)
            attend(0)
            end_phase(act, 4)
            layernorm(5)
            for c in range(CH):
                for w in range(3):
                    g2 = 3 * c + w
                    for k in range(NB):
                        n = NB * g2 + k
                        act.wait_ge(S_("lf_pre"), n + 1)
                        if g2 >= 2:
                            act.wait_ge(S_("lf_o"), g2 - 1)
                        act.activation(hT[g2 % 2][:, k, :], ps(n % 4), ACT.Relu, bias=b1[:, w, k:k + 1]).then_inc(S_("lf_h"), 1)
            attend(1)


def tree_paths(trees, depth):
    path = np.zeros((32 * trees, 32 * trees), np.float32)
    rights = np.full((32 * trees, 1), -1, np.float32)
    for tree in range(trees):
        for leaf in range(2 ** depth):
            node, count = 0, 0
            for level in range(depth):
                right = leaf >> (depth - 1 - level) & 1
                path[32 * tree + node, 32 * tree + leaf] = 2 * right - 1
                node = 2 * node + 1 + right
                count += right
            rights[32 * tree + leaf] = count
    return path, rights


def kernel(**inputs):
    import concourse.bacc as bacc
    from concourse.bass_utils import run_bass_kernel_spmd as run

    def a(name):
        return np.asarray(inputs[name])

    T, B, D = 16, 32, 128
    w = {}
    w["x"] = a("x").reshape(T, 128, D).transpose(1, 0, 2)
    w["ctxT"] = a("ctx_768").transpose(2, 0, 1).reshape(96, -1)
    w["ctx"] = a("ctx_768").transpose(1, 0, 2)
    w["mask"] = a("mask_BxS2_bf1").reshape(1, -1).view(np.uint8)

    def blocks(m, rows=128):
        return m.reshape(-1, rows, m.shape[-1]).transpose(1, 0, 2)

    w["l0_wqT"] = blocks(a("L0_xattn_Wq").T, 64)
    w["l0_wkT"] = blocks(a("L0_xattn_Wk").T, 64)
    w["l0_wvT"] = blocks(a("L0_xattn_Wv").T, 64)
    w["l0_wo"] = blocks(a("L0_xattn_Wo"), 64)
    w["l0_bo"] = a("L0_xattn_bo").reshape(1, D)
    w["wx"] = a("L0_attn_W_xproj")
    w["bx_d"] = a("L0_attn_b_xproj")[:D].reshape(D, 1)
    w["bx_bc"] = a("L0_attn_b_xproj")[D:].reshape(32, 1)
    w["wout"] = a("L0_attn_W_out")
    w["bout"] = a("L0_attn_b_out").reshape(1, D)
    w["alog"] = a("L0_attn_A_log")
    w["dp"] = a("L0_attn_Dp").reshape(D, 1)
    w["wrT"] = a("L0_ffn_Wr").T
    w["aT"] = a("L0_ffn_A").reshape(512, D).T.reshape(D, 4, 128)
    w["bw"] = blocks(a("L0_ffn_Bw").transpose(0, 2, 1).reshape(512, D))
    w["l1_wq"] = a("L1_xattn_Wq")
    w["l1_wk"] = a("L1_xattn_Wk")
    w["l1_wv"] = a("L1_xattn_Wv")
    w["l1_wo"] = a("L1_xattn_Wo")
    w["wqkv"] = a("L1_attn_W")
    for n in "qkv":
        p = f"L1_ffn_{n}_"
        w[n + "_nw"] = a(p + "node_w").T
        w[n + "_nb"] = a(p + "node_b").reshape(-1, 1)
        w[n + "_w1"] = a(p + "w1").transpose(1, 0, 2).reshape(D, -1)
        w[n + "_b1"] = a(p + "b1").reshape(8, 128).T
        w[n + "_w2"] = blocks(a(p + "w2").reshape(1024, D))
        w[n + "_b2"] = a(p + "b2")
    w["path"], w["rights"] = tree_paths(3, 4)
    nc = bacc.Bacc("TRN2", target_bir_lowering=False, num_devices=1)
    arrays, aps = {}, {}
    for name, m in w.items():
        arrays["in_" + name] = m = np.ascontiguousarray(m)
        aps[name] = nc.dram_tensor("in_" + name, m.shape, mybir.dt.from_np(m.dtype), kind="ExternalInput").ap()
    out = nc.dram_tensor("out_0", (128, T, D), F32, kind="ExternalOutput").ap()
    leaf_rows = nc.dram_tensor("leaf_rows", (96, T * 128), BF16, kind="Internal").ap()
    build(nc, aps, out, leaf_rows)
    r = run(nc, [arrays], core_ids=[0])
    return r.results[0]["out_0"].transpose(1, 0, 2).reshape(B, 64, D)
```
